# Optimizing a Trainium2 kernel written in Bass

```python
import numpy as np
import jax
import jax.numpy as jnp

def _softmax(x, axis=-1):
    return jax.nn.softmax(x, axis=axis)

def _gelu(x):
    return jax.nn.gelu(x, approximate=True)

def _silu(x):
    return jax.nn.silu(x)

def _sigmoid(x):
    return jax.nn.sigmoid(x)

def _layernorm(x, axis=-1, eps=1e-05):
    m = jnp.mean(x, axis=axis, keepdims=True)
    v = jnp.var(x, axis=axis, keepdims=True)
    return (x - m) / jnp.sqrt(v + eps)

def _scatter_add(tgt, idx, src, axis=0):
    return tgt.at[idx].add(src)

def _segment_sum(src, seg, n):
    return jax.ops.segment_sum(src, seg, n)
kernel_name = 'mk_seq_postln_d4_jaxref_r8_877a31'

def setup_inputs(seed: int=0):
    np.random.seed(seed)
    _w = jnp.asarray

    def _L0_attn_setup():
        import jax, jax.numpy as jnp
        import numpy as np
        B, T, D = (8, 256, 128)
        K_SIZE = 128
        key = jax.random.key(seed)
        ks = jax.random.split(key, 4)
        s = 0.02
        return {'minibatch': jax.random.normal(ks[0], (B, T, D), dtype=jnp.float32), 'Wq': jax.random.normal(ks[1], (D, K_SIZE), dtype=jnp.float32) * s, 'bq': jnp.zeros((K_SIZE,), dtype=jnp.float32), 'Wk': jax.random.normal(ks[2], (D, K_SIZE), dtype=jnp.float32) * s, 'bk': jnp.zeros((K_SIZE,), dtype=jnp.float32), 'Wv': jax.random.normal(ks[3], (D, D), dtype=jnp.float32) * s, 'bv': jnp.zeros((D,), dtype=jnp.float32)}
    _L0_attn_in = _L0_attn_setup()

    def _L0_ffn_setup():
        import jax, jax.numpy as jnp
        import numpy as np
        H = 8
        KD = 128
        TOPK = 8
        NUM_KEYS = 32
        N_EXPERTS = NUM_KEYS * NUM_KEYS
        N_DIM = 128
        BN_EPS = 1e-05

        def gelu_new(x):
            c = jnp.sqrt(jnp.asarray(2.0 / jnp.pi, x.dtype))
            return 0.5 * x * (1.0 + jnp.tanh(c * (x + 0.044715 * x * x * x)))
        key = jax.random.key(seed)
        ks = jax.random.split(key, 5)
        b, s = (2, 128)
        x = jax.random.normal(ks[0], (b, s, N_DIM), dtype=jnp.float32)
        w_q = jax.random.normal(ks[1], (N_DIM, 2 * H * KD), dtype=jnp.float32) * 0.02
        bn_gamma = jnp.ones((2 * H * KD,), dtype=jnp.float32)
        bn_beta = jnp.zeros((2 * H * KD,), dtype=jnp.float32)
        keys = jax.random.normal(ks[2], (H, NUM_KEYS, 2, KD), dtype=jnp.float32) * 0.02
        down_embed = jax.random.normal(ks[3], (N_EXPERTS, N_DIM), dtype=jnp.float32) * 0.02
        up_embed = jax.random.normal(ks[4], (N_EXPERTS, N_DIM), dtype=jnp.float32) * 0.02
        return {'x': x, 'w_q': w_q, 'bn_gamma': bn_gamma, 'bn_beta': bn_beta, 'keys': keys, 'down_embed': down_embed, 'up_embed': up_embed}
    _L0_ffn_in = _L0_ffn_setup()

    def _L1_attn_setup():
        import jax, jax.numpy as jnp
        import numpy as np
        B, S, DIM = (2, 1024, 128)
        NH, NKV, HD = (16, 4, 64)
        GROUPS = NH // NKV
        CHUNK = 128
        THETA = 10000.0

        def _slopes(h):
            return jnp.asarray([2.0 ** (-8.0 / h * (i + 1)) for i in range(h)], dtype=jnp.float32)

        def _rope_tables(s, d):
            inv = 1.0 / THETA ** (np.arange(0, d, 2, dtype=np.float64) / d)
            freqs = np.outer(np.arange(s, dtype=np.float64), inv)
            emb = np.concatenate([freqs, freqs], axis=-1)
            return (jnp.asarray(np.cos(emb), jnp.float32), jnp.asarray(np.sin(emb), jnp.float32))

        def _apply_rope(x, cos, sin):
            x1, x2 = jnp.split(x, 2, axis=-1)
            rot = jnp.concatenate([-x2, x1], axis=-1)
            return x * cos + rot * sin

        def _lightning_attn(q, k, v, slopes, chunk):
            b, h, s, d = q.shape
            nc = s // chunk
            t = jnp.arange(chunk, dtype=jnp.float32)
            sl = slopes[:, None, None]
            mask = jnp.where(t[:, None] >= t[None, :], jnp.exp(-sl * (t[:, None] - t[None, :])), 0.0)
            q_dec = jnp.exp(-slopes[:, None] * (t + 1.0))[..., None]
            k_dec = jnp.exp(-slopes[:, None] * (chunk - 1.0 - t))[..., None]
            blk_dec = jnp.exp(-slopes * chunk)[None, :, None, None]

            def to_chunks(x):
                return x.reshape(b, h, nc, chunk, d).transpose(2, 0, 1, 3, 4)
            qc, kc, vc = (to_chunks(q), to_chunks(k), to_chunks(v))

            def step(kv, inp):
                qi, ki, vi = inp
                scores = jnp.einsum('bhtd,bhsd->bhts', qi, ki) * mask
                o = jnp.einsum('bhts,bhsd->bhtd', scores, vi) + jnp.einsum('bhtd,bhde->bhte', qi * q_dec, kv)
                kv = blk_dec * kv + jnp.einsum('bhtd,bhte->bhde', ki * k_dec, vi)
                return (kv, o)
            kv0 = jnp.zeros((b, h, d, d), q.dtype)
            _, outs = jax.lax.scan(step, kv0, (qc, kc, vc))
            return outs.transpose(1, 2, 0, 3, 4).reshape(b, h, s, d)
        key = jax.random.key(seed)
        k0, k1, k2, k3, k4 = jax.random.split(key, 5)
        x = jax.random.normal(k0, (B, S, DIM), jnp.float32)
        Wq = jax.random.normal(k1, (NH * HD, DIM), jnp.float32) * 0.02
        Wk = jax.random.normal(k2, (NKV * HD, DIM), jnp.float32) * 0.02
        Wv = jax.random.normal(k3, (NKV * HD, DIM), jnp.float32) * 0.02
        Wo = jax.random.normal(k4, (DIM, NH * HD), jnp.float32) * 0.02
        return {'x': x, 'Wq': Wq, 'Wk': Wk, 'Wv': Wv, 'Wo': Wo}
    _L1_attn_in = _L1_attn_setup()

    def _L1_ffn_setup():
        import jax, jax.numpy as jnp
        import numpy as np
        D_MODEL = 128
        D_FF = 512
        NUM_M = 2
        E_ROUTER = 8 * NUM_M - 1
        D_FF_R = D_FF // NUM_M
        TOP_K = NUM_M * 2 - 1
        B, T = (2, 256)

        def _expert_stack(x, W1, b1, W2, b2):
            h = jax.nn.gelu(jnp.einsum('btd,edf->ebtf', x, W1) + b1[:, None, None, :], approximate=False)
            return jnp.einsum('ebtf,efd->ebtd', h, W2) + b2[:, None, None, :]
        key = jax.random.key(seed)
        ks = jax.random.split(key, 12)
        s = lambda fan_in: 1.0 / np.sqrt(fan_in)
        x = jax.random.normal(ks[0], (B, T, D_MODEL), dtype=jnp.float32)
        sW1 = jax.random.uniform(ks[1], (1, D_MODEL, D_FF), jnp.float32, -s(D_MODEL), s(D_MODEL))
        sb1 = jax.random.uniform(ks[2], (1, D_FF), jnp.float32, -s(D_MODEL), s(D_MODEL))
        sW2 = jax.random.uniform(ks[3], (1, D_FF, D_MODEL), jnp.float32, -s(D_FF), s(D_FF))
        sb2 = jax.random.uniform(ks[4], (1, D_MODEL), jnp.float32, -s(D_FF), s(D_FF))
        rW1 = jax.random.uniform(ks[5], (E_ROUTER, D_MODEL, D_FF_R), jnp.float32, -s(D_MODEL), s(D_MODEL))
        rb1 = jax.random.uniform(ks[6], (E_ROUTER, D_FF_R), jnp.float32, -s(D_MODEL), s(D_MODEL))
        rW2 = jax.random.uniform(ks[7], (E_ROUTER, D_FF_R, D_MODEL), jnp.float32, -s(D_FF_R), s(D_FF_R))
        rb2 = jax.random.uniform(ks[8], (E_ROUTER, D_MODEL), jnp.float32, -s(D_FF_R), s(D_FF_R))
        gW = jax.random.uniform(ks[9], (D_MODEL, E_ROUTER), jnp.float32, -s(D_MODEL), s(D_MODEL))
        gb = jax.random.uniform(ks[10], (E_ROUTER,), jnp.float32, -s(D_MODEL), s(D_MODEL))
        return {'x': x, 'sW1': sW1, 'sb1': sb1, 'sW2': sW2, 'sb2': sb2, 'rW1': rW1, 'rb1': rb1, 'rW2': rW2, 'rb2': rb2, 'gW': gW, 'gb': gb}
    _L1_ffn_in = _L1_ffn_setup()

    def _L2_attn_setup():
        import jax, jax.numpy as jnp
        import numpy as np
        B, N, D = (2, 256, 128)
        H = 16
        HD = D // H
        NEG = -1e+30
        key = jax.random.key(seed)
        ks = jax.random.split(key, 6)
        s = 0.02
        return {'x': jax.random.normal(ks[0], (B, N, D), dtype=jnp.float32), 'Wq': jax.random.normal(ks[1], (D, D), dtype=jnp.float32) * s, 'Wk': jax.random.normal(ks[2], (D, D), dtype=jnp.float32) * s, 'Wv': jax.random.normal(ks[3], (D, D), dtype=jnp.float32) * s, 'Wo': jax.random.normal(ks[4], (D, D), dtype=jnp.float32) * s, 'Wf': jax.random.normal(ks[5], (D, H), dtype=jnp.float32) * s}
    _L2_attn_in = _L2_attn_setup()

    def _L2_ffn_setup():
        import jax, jax.numpy as jnp
        import numpy as np
        TOP_K = 2
        EPS = 1e-20
        key = jax.random.key(seed)
        ks = jax.random.split(key, 8)
        B, S, H, E, D = (4, 256, 128, 8, 256)
        s = 0.02
        return {'x': jax.random.normal(ks[0], (B, S, H), dtype=jnp.float32), 'Wr': jax.random.normal(ks[1], (H, E), dtype=jnp.float32) * s, 'Wg': jax.random.normal(ks[2], (E, H, D), dtype=jnp.float32) * s, 'Wu': jax.random.normal(ks[3], (E, H, D), dtype=jnp.float32) * s, 'Wd': jax.random.normal(ks[4], (E, D, H), dtype=jnp.float32) * s, 'Sg': jax.random.normal(ks[5], (H, D), dtype=jnp.float32) * s, 'Su': jax.random.normal(ks[6], (H, D), dtype=jnp.float32) * s, 'Sd': jax.random.normal(ks[7], (D, H), dtype=jnp.float32) * s}
    _L2_ffn_in = _L2_ffn_setup()

    def _L3_attn_setup():
        import jax, jax.numpy as jnp
        import numpy as np
        B, N, C, H = (8, 512, 128, 16)
        D = C // H
        EPS = 1e-12

        def _l2norm(x):
            n = jnp.sqrt(jnp.sum(x * x, axis=-1, keepdims=True))
            return x / jnp.maximum(n, EPS)
        key = jax.random.key(seed)
        ks = jax.random.split(key, 5)
        return {'x': jax.random.normal(ks[0], (B, N, C), dtype=jnp.float32), 'qkv_w': jax.random.normal(ks[1], (C, 3 * C), dtype=jnp.float32) * 0.02, 'qkv_b': jax.random.normal(ks[2], (3 * C,), dtype=jnp.float32) * 0.02, 'proj_w': jax.random.normal(ks[3], (C, C), dtype=jnp.float32) * 0.02, 'proj_b': jax.random.normal(ks[4], (C,), dtype=jnp.float32) * 0.02}
    _L3_attn_in = _L3_attn_setup()

    def _L3_ffn_setup():
        import jax, jax.numpy as jnp
        import numpy as np
        B, S, H, F, E = (8, 256, 128, 512, 8)
        INIT_LAMBDA = 0.2
        key = jax.random.key(seed)
        ks = jax.random.split(key, 12)
        std = 0.02
        return {'hidden_states': jax.random.normal(ks[0], (B, S, H), jnp.float32), 'gate_w1': jax.random.normal(ks[1], (H, H), jnp.float32) * 0.01, 'gate_b1': jnp.zeros((H,), jnp.float32), 'gate_w2': jax.random.normal(ks[2], (E, H), jnp.float32) * 0.01, 'gate_b2': jnp.full((E,), INIT_LAMBDA, jnp.float32), 'W1': jax.random.normal(ks[3], (F, H), jnp.float32) * std, 'b1': jax.random.normal(ks[4], (F,), jnp.float32) * std, 'W2': jax.random.normal(ks[5], (H, F), jnp.float32) * std, 'b2': jax.random.normal(ks[6], (H,), jnp.float32) * std, 'TW1': jax.random.normal(ks[7], (E, F, H), jnp.float32) * std, 'Tb1': jax.random.normal(ks[8], (E, F), jnp.float32) * std, 'TW2': jax.random.normal(ks[9], (E, H, F), jnp.float32) * std, 'Tb2': jax.random.normal(ks[10], (E, H), jnp.float32) * std}
    _L3_ffn_in = _L3_ffn_setup()
    _d = {'L0_attn_minibatch': _L0_attn_in['minibatch'], 'L0_attn_Wq': _L0_attn_in['Wq'], 'L0_attn_bq': _L0_attn_in['bq'], 'L0_attn_Wk': _L0_attn_in['Wk'], 'L0_attn_bk': _L0_attn_in['bk'], 'L0_attn_Wv': _L0_attn_in['Wv'], 'L0_attn_bv': _L0_attn_in['bv'], 'L0_ffn_w_q': _L0_ffn_in['w_q'], 'L0_ffn_bn_gamma': _L0_ffn_in['bn_gamma'], 'L0_ffn_bn_beta': _L0_ffn_in['bn_beta'], 'L0_ffn_keys': _L0_ffn_in['keys'], 'L0_ffn_down_embed': _L0_ffn_in['down_embed'], 'L0_ffn_up_embed': _L0_ffn_in['up_embed'], 'L1_attn_Wq': _L1_attn_in['Wq'], 'L1_attn_Wk': _L1_attn_in['Wk'], 'L1_attn_Wv': _L1_attn_in['Wv'], 'L1_attn_Wo': _L1_attn_in['Wo'], 'L1_ffn_sW1': _L1_ffn_in['sW1'], 'L1_ffn_sb1': _L1_ffn_in['sb1'], 'L1_ffn_sW2': _L1_ffn_in['sW2'], 'L1_ffn_sb2': _L1_ffn_in['sb2'], 'L1_ffn_rW1': _L1_ffn_in['rW1'], 'L1_ffn_rb1': _L1_ffn_in['rb1'], 'L1_ffn_rW2': _L1_ffn_in['rW2'], 'L1_ffn_rb2': _L1_ffn_in['rb2'], 'L1_ffn_gW': _L1_ffn_in['gW'], 'L1_ffn_gb': _L1_ffn_in['gb'], 'L2_attn_Wq': _L2_attn_in['Wq'], 'L2_attn_Wk': _L2_attn_in['Wk'], 'L2_attn_Wv': _L2_attn_in['Wv'], 'L2_attn_Wo': _L2_attn_in['Wo'], 'L2_attn_Wf': _L2_attn_in['Wf'], 'L2_ffn_Wr': _L2_ffn_in['Wr'], 'L2_ffn_Wg': _L2_ffn_in['Wg'], 'L2_ffn_Wu': _L2_ffn_in['Wu'], 'L2_ffn_Wd': _L2_ffn_in['Wd'], 'L2_ffn_Sg': _L2_ffn_in['Sg'], 'L2_ffn_Su': _L2_ffn_in['Su'], 'L2_ffn_Sd': _L2_ffn_in['Sd'], 'L3_attn_qkv_w': _L3_attn_in['qkv_w'], 'L3_attn_qkv_b': _L3_attn_in['qkv_b'], 'L3_attn_proj_w': _L3_attn_in['proj_w'], 'L3_attn_proj_b': _L3_attn_in['proj_b'], 'L3_ffn_gate_w1': _L3_ffn_in['gate_w1'], 'L3_ffn_gate_b1': _L3_ffn_in['gate_b1'], 'L3_ffn_gate_w2': _L3_ffn_in['gate_w2'], 'L3_ffn_gate_b2': _L3_ffn_in['gate_b2'], 'L3_ffn_W1': _L3_ffn_in['W1'], 'L3_ffn_b1': _L3_ffn_in['b1'], 'L3_ffn_W2': _L3_ffn_in['W2'], 'L3_ffn_b2': _L3_ffn_in['b2'], 'L3_ffn_TW1': _L3_ffn_in['TW1'], 'L3_ffn_Tb1': _L3_ffn_in['Tb1'], 'L3_ffn_TW2': _L3_ffn_in['TW2'], 'L3_ffn_Tb2': _L3_ffn_in['Tb2']}
    _x0 = _d['L0_attn_minibatch']
    _d['L0_attn_minibatch'] = jax.random.normal(jax.random.fold_in(jax.random.key(seed), 1), (2, 1024, 128), dtype=_x0.dtype)
    del _x0
    return _d

def reference(L0_attn_minibatch, L0_attn_Wq, L0_attn_bq, L0_attn_Wk, L0_attn_bk, L0_attn_Wv, L0_attn_bv, L0_ffn_w_q, L0_ffn_bn_gamma, L0_ffn_bn_beta, L0_ffn_keys, L0_ffn_down_embed, L0_ffn_up_embed, L1_attn_Wq, L1_attn_Wk, L1_attn_Wv, L1_attn_Wo, L1_ffn_sW1, L1_ffn_sb1, L1_ffn_sW2, L1_ffn_sb2, L1_ffn_rW1, L1_ffn_rb1, L1_ffn_rW2, L1_ffn_rb2, L1_ffn_gW, L1_ffn_gb, L2_attn_Wq, L2_attn_Wk, L2_attn_Wv, L2_attn_Wo, L2_attn_Wf, L2_ffn_Wr, L2_ffn_Wg, L2_ffn_Wu, L2_ffn_Wd, L2_ffn_Sg, L2_ffn_Su, L2_ffn_Sd, L3_attn_qkv_w, L3_attn_qkv_b, L3_attn_proj_w, L3_attn_proj_b, L3_ffn_gate_w1, L3_ffn_gate_b1, L3_ffn_gate_w2, L3_ffn_gate_b2, L3_ffn_W1, L3_ffn_b1, L3_ffn_W2, L3_ffn_b2, L3_ffn_TW1, L3_ffn_Tb1, L3_ffn_TW2, L3_ffn_Tb2):

    def _L0_attn_ref(minibatch, Wq, bq, Wk, bk, Wv, bv):
        import jax, jax.numpy as jnp
        import numpy as np
        B, T, D = (8, 256, 128)
        K_SIZE = 128
        queries = minibatch @ Wq + bq
        keys = minibatch @ Wk + bk
        values = minibatch @ Wv + bv
        logits = jnp.einsum('bik,bjk->bij', queries, keys)
        t = logits.shape[1]
        causal = jnp.triu(jnp.ones((t, t), dtype=bool), k=1)
        logits = jnp.where(causal[None, :, :], -jnp.inf, logits)
        sqrt_k = jnp.sqrt(jnp.asarray(Wq.shape[1], dtype=logits.dtype))
        probs = jax.nn.softmax(logits, axis=1) / sqrt_k
        read = jnp.einsum('bij,bjv->biv', probs, values)
        return minibatch + read

    def _L0_ffn_ref(x, w_q, bn_gamma, bn_beta, keys, down_embed, up_embed):
        import jax, jax.numpy as jnp
        import numpy as np
        H = 8
        KD = 128
        TOPK = 8
        NUM_KEYS = 32
        N_EXPERTS = NUM_KEYS * NUM_KEYS
        N_DIM = 128
        BN_EPS = 1e-05

        def gelu_new(x):
            c = jnp.sqrt(jnp.asarray(2.0 / jnp.pi, x.dtype))
            return 0.5 * x * (1.0 + jnp.tanh(c * (x + 0.044715 * x * x * x)))
        b, n, d = x.shape
        q = jnp.einsum('bnd,de->bne', x, w_q)
        mean = jnp.mean(q, axis=(0, 1))
        var = jnp.var(q, axis=(0, 1))
        q = (q - mean) * jax.lax.rsqrt(var + BN_EPS) * bn_gamma + bn_beta
        q = q.reshape(b, n, 2, H, KD).transpose(2, 0, 1, 3, 4)
        sim = jnp.einsum('pbnhd,hkpd->pbnhk', q, keys)
        sx, ix = jax.lax.top_k(sim[0], TOPK)
        sy, iy = jax.lax.top_k(sim[1], TOPK)
        all_scores = (sx[..., :, None] + sy[..., None, :]).reshape(b, n, H, TOPK * TOPK)
        all_indices = (ix[..., :, None] * NUM_KEYS + iy[..., None, :]).reshape(b, n, H, TOPK * TOPK)
        scores, pk = jax.lax.top_k(all_scores, TOPK)
        indices = jnp.take_along_axis(all_indices, pk, axis=-1)
        wd = down_embed[indices]
        wu = up_embed[indices]
        h = jnp.einsum('bnd,bnhkd->bnhk', x, wd)
        h = gelu_new(h)
        h = jax.nn.softmax(scores, axis=-1) * h
        out = jnp.einsum('bnhk,bnhkd->bnd', h, wu)
        return out

    def _L1_attn_ref(x, Wq, Wk, Wv, Wo):
        import jax, jax.numpy as jnp
        import numpy as np
        B, S, DIM = (2, 1024, 128)
        NH, NKV, HD = (16, 4, 64)
        GROUPS = NH // NKV
        CHUNK = 128
        THETA = 10000.0

        def _slopes(h):
            return jnp.asarray([2.0 ** (-8.0 / h * (i + 1)) for i in range(h)], dtype=jnp.float32)

        def _rope_tables(s, d):
            inv = 1.0 / THETA ** (np.arange(0, d, 2, dtype=np.float64) / d)
            freqs = np.outer(np.arange(s, dtype=np.float64), inv)
            emb = np.concatenate([freqs, freqs], axis=-1)
            return (jnp.asarray(np.cos(emb), jnp.float32), jnp.asarray(np.sin(emb), jnp.float32))

        def _apply_rope(x, cos, sin):
            x1, x2 = jnp.split(x, 2, axis=-1)
            rot = jnp.concatenate([-x2, x1], axis=-1)
            return x * cos + rot * sin

        def _lightning_attn(q, k, v, slopes, chunk):
            b, h, s, d = q.shape
            nc = s // chunk
            t = jnp.arange(chunk, dtype=jnp.float32)
            sl = slopes[:, None, None]
            mask = jnp.where(t[:, None] >= t[None, :], jnp.exp(-sl * (t[:, None] - t[None, :])), 0.0)
            q_dec = jnp.exp(-slopes[:, None] * (t + 1.0))[..., None]
            k_dec = jnp.exp(-slopes[:, None] * (chunk - 1.0 - t))[..., None]
            blk_dec = jnp.exp(-slopes * chunk)[None, :, None, None]

            def to_chunks(x):
                return x.reshape(b, h, nc, chunk, d).transpose(2, 0, 1, 3, 4)
            qc, kc, vc = (to_chunks(q), to_chunks(k), to_chunks(v))

            def step(kv, inp):
                qi, ki, vi = inp
                scores = jnp.einsum('bhtd,bhsd->bhts', qi, ki) * mask
                o = jnp.einsum('bhts,bhsd->bhtd', scores, vi) + jnp.einsum('bhtd,bhde->bhte', qi * q_dec, kv)
                kv = blk_dec * kv + jnp.einsum('bhtd,bhte->bhde', ki * k_dec, vi)
                return (kv, o)
            kv0 = jnp.zeros((b, h, d, d), q.dtype)
            _, outs = jax.lax.scan(step, kv0, (qc, kc, vc))
            return outs.transpose(1, 2, 0, 3, 4).reshape(b, h, s, d)
        b, s, _ = x.shape
        q = (x @ Wq.T).reshape(b, s, NH, HD).transpose(0, 2, 1, 3)
        k = (x @ Wk.T).reshape(b, s, NKV, HD).transpose(0, 2, 1, 3)
        v = (x @ Wv.T).reshape(b, s, NKV, HD).transpose(0, 2, 1, 3)
        cos, sin = _rope_tables(s, HD)
        q = _apply_rope(q, cos, sin)
        k = _apply_rope(k, cos, sin)
        k = jnp.repeat(k, GROUPS, axis=1)
        v = jnp.repeat(v, GROUPS, axis=1)
        out = _lightning_attn(q, k, v, _slopes(NH), CHUNK)
        out = out.transpose(0, 2, 1, 3).reshape(b, s, NH * HD)
        return out @ Wo.T

    def _L1_ffn_ref(x, sW1, sb1, sW2, sb2, rW1, rb1, rW2, rb2, gW, gb):
        import jax, jax.numpy as jnp
        import numpy as np
        D_MODEL = 128
        D_FF = 512
        NUM_M = 2
        E_ROUTER = 8 * NUM_M - 1
        D_FF_R = D_FF // NUM_M
        TOP_K = NUM_M * 2 - 1
        B, T = (2, 256)

        def _expert_stack(x, W1, b1, W2, b2):
            h = jax.nn.gelu(jnp.einsum('btd,edf->ebtf', x, W1) + b1[:, None, None, :], approximate=False)
            return jnp.einsum('ebtf,efd->ebtd', h, W2) + b2[:, None, None, :]
        shared_enc = _expert_stack(x, sW1, sb1, sW2, sb2).sum(0)
        weights = jax.nn.softmax(x @ gW + gb, axis=-1)
        topv, topi = jax.lax.top_k(weights, TOP_K)
        gated = (jax.nn.one_hot(topi, E_ROUTER, dtype=weights.dtype) * topv[..., None]).sum(axis=-2)
        router_out = _expert_stack(x, rW1, rb1, rW2, rb2)
        router_enc = jnp.einsum('ebtd,bte->btd', router_out, gated)
        return shared_enc + router_enc + x

    def _L2_attn_ref(x, Wq, Wk, Wv, Wo, Wf):
        import jax, jax.numpy as jnp
        import numpy as np
        B, N, D = (2, 256, 128)
        H = 16
        HD = D // H
        NEG = -1e+30
        b, n, d = x.shape
        h, hd = (H, HD)
        scale = hd ** (-0.5)
        q = (x @ Wq).reshape(b, n, h, hd).transpose(0, 2, 1, 3)
        k = (x @ Wk).reshape(b, n, h, hd).transpose(0, 2, 1, 3)
        v = (x @ Wv).reshape(b, n, h, hd).transpose(0, 2, 1, 3)
        log_f = jax.nn.log_sigmoid(x @ Wf).transpose(0, 2, 1)
        c = jnp.cumsum(log_f, axis=-1)
        scores = jnp.einsum('bhid,bhjd->bhij', q, k) * scale
        scores = scores + c[..., :, None] - c[..., None, :]
        causal = jnp.tril(jnp.ones((n, n), dtype=bool))
        scores = jnp.where(causal, scores, NEG)
        attn = jax.nn.softmax(scores, axis=-1)
        out = jnp.einsum('bhij,bhjd->bhid', attn, v)
        out = out.transpose(0, 2, 1, 3).reshape(b, n, d)
        return out @ Wo

    def _L2_ffn_ref(x, Wr, Wg, Wu, Wd, Sg, Su, Sd):
        import jax, jax.numpy as jnp
        import numpy as np
        TOP_K = 2
        EPS = 1e-20
        B, S, H = x.shape
        T = B * S
        xt = x.reshape(T, H)
        scores = jax.nn.softmax(xt @ Wr, axis=-1)
        topk_w, topk_idx = jax.lax.top_k(scores, TOP_K)
        topk_w = topk_w / (topk_w.sum(axis=-1, keepdims=True) + EPS)
        g = jax.nn.silu(jnp.einsum('th,ehd->etd', xt, Wg))
        u = jnp.einsum('th,ehd->etd', xt, Wu)
        out_all = jnp.einsum('etd,edh->eth', g * u, Wd)
        tok = jnp.arange(T)[:, None]
        gathered = out_all[topk_idx, tok, :]
        out = jnp.sum(gathered * topk_w[..., None], axis=1).reshape(B, S, H)
        shared = jax.nn.silu(x @ Sg) * (x @ Su) @ Sd
        return out + shared

    def _L3_attn_ref(x, qkv_w, qkv_b, proj_w, proj_b):
        import jax, jax.numpy as jnp
        import numpy as np
        B, N, C, H = (8, 512, 128, 16)
        D = C // H
        EPS = 1e-12

        def _l2norm(x):
            n = jnp.sqrt(jnp.sum(x * x, axis=-1, keepdims=True))
            return x / jnp.maximum(n, EPS)
        b, n, c = x.shape
        qkv = (x @ qkv_w + qkv_b).reshape(b, n, 3, H, D)
        qkv = jnp.transpose(qkv, (2, 0, 3, 1, 4))
        q, k, v = (qkv[0], qkv[1], qkv[2])
        q = _l2norm(q)
        k = _l2norm(k)
        kv = jnp.einsum('bhnd,bhne->bhde', k, v)
        out = jnp.einsum('bhnd,bhde->bhne', q, kv)
        out = jnp.transpose(out, (0, 2, 1, 3)).reshape(b, n, c)
        return out @ proj_w + proj_b

    def _L3_ffn_ref(hidden_states, gate_w1, gate_b1, gate_w2, gate_b2, W1, b1, W2, b2, TW1, Tb1, TW2, Tb2):
        import jax, jax.numpy as jnp
        import numpy as np
        B, S, H, F, E = (8, 256, 128, 512, 8)
        INIT_LAMBDA = 0.2
        x = hidden_states
        h = jax.nn.relu(jnp.einsum('bsh,oh->bso', x, gate_w1) + gate_b1)
        g = jnp.einsum('bso,eo->bse', h, gate_w2) + gate_b2
        g = g.mean(axis=1)
        mW1 = W1 + jnp.einsum('be,efh->bfh', g, TW1)
        mb1 = b1 + g @ Tb1
        mW2 = W2 + jnp.einsum('be,ehf->bhf', g, TW2)
        mb2 = b2 + g @ Tb2
        u = jax.nn.gelu(jnp.einsum('bsh,bfh->bsf', x, mW1) + mb1[:, None, :])
        out = jnp.einsum('bsf,bhf->bsh', u, mW2) + mb2[:, None, :]
        return out
    x = L0_attn_minibatch
    x = _layernorm(x + _L0_attn_ref(x, L0_attn_Wq, L0_attn_bq, L0_attn_Wk, L0_attn_bk, L0_attn_Wv, L0_attn_bv), axis=-1)
    x = _layernorm(x + _L0_ffn_ref(x, L0_ffn_w_q, L0_ffn_bn_gamma, L0_ffn_bn_beta, L0_ffn_keys, L0_ffn_down_embed, L0_ffn_up_embed), axis=-1)
    x = _layernorm(x + _L1_attn_ref(x, L1_attn_Wq, L1_attn_Wk, L1_attn_Wv, L1_attn_Wo), axis=-1)
    x = _layernorm(x + _L1_ffn_ref(x, L1_ffn_sW1, L1_ffn_sb1, L1_ffn_sW2, L1_ffn_sb2, L1_ffn_rW1, L1_ffn_rb1, L1_ffn_rW2, L1_ffn_rb2, L1_ffn_gW, L1_ffn_gb), axis=-1)
    x = _layernorm(x + _L2_attn_ref(x, L2_attn_Wq, L2_attn_Wk, L2_attn_Wv, L2_attn_Wo, L2_attn_Wf), axis=-1)
    x = _layernorm(x + _L2_ffn_ref(x, L2_ffn_Wr, L2_ffn_Wg, L2_ffn_Wu, L2_ffn_Wd, L2_ffn_Sg, L2_ffn_Su, L2_ffn_Sd), axis=-1)
    x = _layernorm(x + _L3_attn_ref(x, L3_attn_qkv_w, L3_attn_qkv_b, L3_attn_proj_w, L3_attn_proj_b), axis=-1)
    x = _layernorm(x + _L3_ffn_ref(x, L3_ffn_gate_w1, L3_ffn_gate_b1, L3_ffn_gate_w2, L3_ffn_gate_b2, L3_ffn_W1, L3_ffn_b1, L3_ffn_W2, L3_ffn_b2, L3_ffn_TW1, L3_ffn_Tb1, L3_ffn_TW2, L3_ffn_Tb2), axis=-1)
    return x

_drawn_inputs = setup_inputs


def setup_inputs(seed=0):
    import zlib

    import numpy as np

    out = dict(_drawn_inputs(seed))
    spreads = {'L0_attn_bq': (0.0, 0.8),
     'L0_attn_bk': (0.0, 0.8),
     'L0_attn_bv': (0.0, 0.8),
     'L0_ffn_bn_gamma': (1.0, 0.6),
     'L0_ffn_bn_beta': (0.0, 0.8),
     'L3_ffn_gate_b1': (0.0, 0.8),
     'L3_ffn_gate_b2': (0.20000000298023224, 0.6)}
    factors = {'L0_attn_Wq': 8.0,
     'L0_attn_Wk': 8.0,
     'L0_attn_Wv': 8.0,
     'L0_ffn_w_q': 8.0,
     'L0_ffn_keys': 8.0,
     'L0_ffn_down_embed': 8.0,
     'L0_ffn_up_embed': 8.0,
     'L1_ffn_sb1': 3.892,
     'L1_ffn_rb1': 8.0,
     'L1_ffn_rb2': 8.0,
     'L1_ffn_gb': 8.0,
     'L2_attn_Wq': 8.0,
     'L2_attn_Wk': 8.0,
     'L2_attn_Wf': 8.0,
     'L2_ffn_Wr': 8.0,
     'L2_ffn_Wg': 8.0,
     'L2_ffn_Wu': 8.0,
     'L2_ffn_Wd': 8.0,
     'L2_ffn_Sg': 6.054,
     'L2_ffn_Su': 5.959,
     'L2_ffn_Sd': 5.944,
     'L3_attn_proj_b': 5.683,
     'L3_ffn_gate_w1': 8.0,
     'L3_ffn_gate_w2': 8.0,
     'L3_ffn_b1': 8.0,
     'L3_ffn_b2': 2.676,
     'L3_ffn_Tb1': 8.0,
     'L3_ffn_Tb2': 5.25}
    for name, (base, spread) in spreads.items():
        noise = np.random.default_rng([zlib.crc32(name.encode()), seed]).standard_normal(out[name].shape)
        drawn = base * np.exp(spread * noise) if base else spread * noise
        out[name] = jnp.asarray(drawn.astype(out[name].dtype))
    for name, factor in factors.items():
        out[name] = (out[name] * factor).astype(out[name].dtype)
    return out
```

```python
from contextlib import ExitStack

import numpy as np

import concourse.bass as bass
from concourse import mybir

F32 = mybir.dt.float32
BF16 = mybir.dt.bfloat16
U32 = mybir.dt.uint32
ALU = mybir.AluOpType
ACT = mybir.ActivationFunctionType
AX = mybir.AxisListType

P = 128
NT = 16
NG = 4
GT = 4
GW = 512
TOK = 2048
LN_EPS = 1e-5
NEG = -1.0e30

PH, PKEYS, PTOP = 8, 32, 8
PC = 2 * PH
NKV, HD = 4, 64
FH, FD = 16, 8
E1, C1S, C1 = 15, 4, 34
E2, C2 = 8, 18
E3, C3 = 8, 4


class Arena:

    def __init__(self, tensor):
        self.tensor, self.at = tensor, 0

    def take(self, *shape):
        n = int(np.prod(shape))
        ap = self.tensor[:, self.at:self.at + n]
        self.at += n
        assert self.at <= self.tensor.shape[1], (self.at, self.tensor.shape)
        if len(shape) == 2:
            ap = ap.rearrange("p (a b) -> p a b", a=shape[0])
        if len(shape) == 3:
            ap = ap.rearrange("p (a b c) -> p a b c", a=shape[0], b=shape[1])
        return ap


class Chain:

    def __init__(self, engine, semaphore):
        self.engine, self.semaphore, self.count = engine, semaphore, 0

    def link(self, ins):
        self.count += 1
        ins.then_inc(self.semaphore, 1)
        self.engine.wait_ge(self.semaphore, self.count)


def bc(ap, axis, n):
    a = ap.unsqueeze(axis)
    shape = list(a.shape)
    shape[axis] = n
    return a.broadcast_to(shape)


def flat(ap):
    return ap.rearrange("p a b -> p (a b)")


class Net:

    def __init__(self, nc, ctx, io):
        self.nc, self.ctx, self.io = nc, ctx, io
        self.signals = {}

        def sb(name, n):
            return ctx.enter_context(nc.sbuf_tensor(name, [P, n], F32))

        self.pairs = [ctx.enter_context(nc.psum_tensor(f"banks{2 * i}{2 * i + 1}", [P, 2 * GW], F32))
                      for i in range(4)]
        self.bank = [self.pairs[i // 2][:, (i % 2) * GW:(i % 2 + 1) * GW] for i in range(8)]
        self.xT = [sb("xT0", TOK), sb("xT1", TOK)]
        self.x = sb("x_tokens", TOK)[:, :].rearrange("p (t d) -> p t d", t=NT)
        self.yT = sb("yT", GW)
        self.stats = sb("stats", GT * 6)[:, :].rearrange("p (a b) -> p a b", a=GT)
        self.moments = sb("moments", GT * 2)[:, :].rearrange("p (a b) -> p a b", a=GT)
        self.rstd, self.var = sb("rstd", GT), sb("variance_eps", GT)
        self.const = Arena(sb("constants", CONST_COLS))
        self.late = Arena(sb("late_weights", LATE_COLS))
        self.mid = Arena(sb("expert_weights", MID_COLS))
        self.work = sb("work", WORK_COLS)
        self.ident = self.const.take(P)
        self.ones = self.const.take(P)
        self.zeros = ctx.enter_context(nc.sbuf_tensor("zeros", [1, GW], BF16))
        self.minus_half, self.half = self.const.take(16), self.const.take(32)
        self.minus_half4 = self.minus_half[:, 0:GT]

    def __getitem__(self, name):
        if name not in self.signals:
            self.signals[name] = self.ctx.enter_context(self.nc.semaphore(name))
        return self.signals[name]

    def bias(self, layer, g):
        return None

    def norm_pe_back(self, pe, n):
        pe.wait_ge(self["y_ready"], n + 1)
        if n:
            pe.wait_ge(self["normed"], n)
        for k in range(GT):
            mm = pe.transpose(self.bank[2][:, k * P:(k + 1) * P], self.yT[:, k * P:(k + 1) * P], self.ident)
        mm.then_inc(self["y_tokens"], 1)

    def norm_pe_forth(self, pe, n):
        g = n % NG
        pe.wait_ge(self["normed"], n + 1)
        if n:
            pe.wait_ge(self["xT_done"], n)
        for k in range(GT):
            mm = pe.transpose(self.bank[3][:, k * P:(k + 1) * P], self.x[:, g * GT + k, :], self.ident)
        mm.then_inc(self["xT_in_psum"], 1)

    def norm_act(self, act, n):
        g = n % NG
        act.wait_ge(self["xT_in_psum"], n + 1)
        act.activation(self.xT[(n // NG + 1) % 2][:, g * GW:(g + 1) * GW], self.bank[3], ACT.Copy) \
           .then_inc(self["xT_done"], 1)

    def norm_dve(self, dve, ch, n, scalar=0.0, op=ALU.add, twice=False):
        g = n % NG
        xT = self.xT[(n // NG) % 2][:, g * GW:(g + 1) * GW]
        out = self.bank[g % 2]
        dve.wait_ge(self["out_ready"], n + 1)
        if twice:
            ins = dve.scalar_tensor_tensor(out=self.yT[:], in0=xT, scalar=2.0, in1=out, op0=ALU.mult, op1=ALU.add)
        else:
            ins = dve.scalar_tensor_tensor(out=self.yT[:], in0=out, scalar=scalar, in1=xT, op0=op, op1=ALU.add)
        ins.then_inc(self["y_ready"], 1)
        dve.wait_ge(self["y_tokens"], n + 1)
        for k in range(GT):
            ins = dve.bn_stats(self.stats[:, k, :], self.bank[2][:, k * P:(k + 1) * P])
        ch.link(ins)
        for k in range(GT):
            ins = dve.bn_aggr(self.moments[:, k, :], self.stats[:, k, :])
        ch.link(ins)
        dve.tensor_scalar(self.var[:], self.moments[:, :, 1], LN_EPS, None, ALU.add).then_inc(self["variance"], 1)
        dve.wait_ge(self["rstd_done"], n + 1)
        for k in range(GT):
            ins = dve.tensor_scalar(self.x[:, g * GT + k, :], self.bank[2][:, k * P:(k + 1) * P],
                                    self.moments[:, k, 0:1], self.rstd[:, k:k + 1], ALU.subtract, ALU.mult)
        ins.then_inc(self["normed"], 1)

    def norm_pool(self, pool, n):
        pool.wait_ge(self["variance"], n + 1)
        pool.tensor_tensor(out=self.rstd[:], in0=self.var[:], in1=self.minus_half4, op=ALU.pow) \
            .then_inc(self["rstd_done"], 1)

    def layer_start(self, eng, layer):
        if layer:
            eng.wait_ge(self["xT_done"], NG * layer)


class QueryAttention:
    LAYER = 0

    def __init__(self, net):
        self.net = net
        a = Arena(net.work)
        self.qT, self.kT = a.take(TOK), a.take(TOK)
        self.v = a.take(NT, P)
        self.exp = a.take(2, 1024)
        self.v_scaled = a.take(2, P)
        self.negmax = a.take(2 * NT)
        self.total = a.take(2 * NT)
        w = net.const
        self.w = net.late.take(3, P) if False else a.take(3, P)
        self.b = a.take(2)
        self.bv = a.take(P)
        self.mask = w.take(P)

    def pv_wait(self, eng, n):
        if n % 8 == 7:
            eng.wait_ge(self.net["out_ready"], 2 * (n // 8) + 2)
        else:
            eng.wait_ge(self.net["a0_pv_done"], n + 1 - n // 8)

    def pe(self, pe):
        net, bank = self.net, self.net.bank
        xT = net.xT[0]
        pe.wait_ge(net["w0_loaded"], 16 * 9)
        for i in range(2 * NG):
            if i >= 2:
                pe.wait_ge(net["a0_qk_copied"], i - 1)
            pe.matmul(bank[4 + i % 2], self.w[:, i // NG, :], xT[:, (i % NG) * GW:(i % NG + 1) * GW],
                      start=True, stop=True).then_inc(net["a0_qk_psum"], 1)
        for g in range(NG):
            if g >= 2:
                pe.wait_ge(net["a0_v_copied"], g - 1)
            for k in range(GT):
                t = g * GT + k
                mm = pe.matmul(bank[6 + g % 2][:, k * P:(k + 1) * P], xT[:, t * P:(t + 1) * P],
                               self.w[:, 2, :], start=True, stop=True)
            mm.then_inc(net["a0_v_psum"], 1)
        pe.wait_ge(net["a0_qk_copied"], 2 * NG)
        pe.wait_ge(net["a0_v_copied"], NG)

        def scores(n):
            b, j = divmod(n, 8)
            if n >= 2:
                pe.wait_ge(net["a0_exp_done"], n - 1)
            for half in range(j // 4, 2):
                lo = max(P * j, GW * half)
                mm = pe.matmul(net.pairs[2 + n % 2][:, lo:GW * (half + 1)],
                               self.kT[:, n * P:(n + 1) * P],
                               self.qT[:, 1024 * b + lo:1024 * b + GW * (half + 1)], start=True, stop=True)
            mm.then_inc(net["a0_scores"], 1)

        def values(n):
            b, j = divmod(n, 8)
            pe.wait_ge(net["a0_v_scaled"], n + 1)
            for half in range(j // 4, 2):
                if j == 0 and b:
                    pe.wait_ge(net["y_ready"], half + 1)
                lo = max(P * j, GW * half)
                mm = pe.matmul(bank[half][:, lo - GW * half:GW], self.v_scaled[:, n % 2, :],
                               self.exp[:, n % 2, lo:GW * (half + 1)], start=(j == 0), stop=(j == 3 + 4 * half))
                if j == 3 + 4 * half:
                    mm.then_inc(net["out_ready"], 1)
            if j != 7:
                mm.then_inc(net["a0_pv_done"], 1)

        scores(0)
        for n in range(NT):
            if n + 1 < NT:
                scores(n + 1)
            values(n)
            if n % 8 == 7:
                for g in (n // 8 * 2, n // 8 * 2 + 1):
                    net.norm_pe_back(pe, g)
                    net.norm_pe_forth(pe, g)

    def act(self, act, ch):
        net = self.net
        act.wait_ge(net["w0_loaded"], 16 * 9)
        for i in range(2 * NG):
            act.wait_ge(net["a0_qk_psum"], i + 1)
            dst = (self.qT, self.kT)[i // NG][:, (i % NG) * GW:(i % NG + 1) * GW]
            act.activation(dst, net.bank[4 + i % 2], ACT.Identity, bias=self.b[:, i // NG:i // NG + 1]) \
               .then_inc(net["a0_qk_copied"], 1)
        for n in range(NT):
            j = n % 8
            act.wait_ge(net["a0_negmax"], n + 1)
            if n >= 2:
                self.pv_wait(act, n - 2)
            act.activation(self.exp[:, n % 2, P * j:1024], net.pairs[2 + n % 2][:, P * j:1024], ACT.Exp,
                           bias=self.negmax[:, n:n + 1], accum_out=self.total[:, n:n + 1]) \
               .then_inc(net["a0_exp_done"], 1)
            if n % 8 == 7:
                net.norm_act(act, n // 8 * 2)
                net.norm_act(act, n // 8 * 2 + 1)

    def dve(self, dve, ch):
        net = self.net
        dve.wait_ge(net["w0_loaded"], 16 * 9)
        for g in range(NG):
            dve.wait_ge(net["a0_v_psum"], g + 1)
            dve.tensor_tensor(out=self.v[:, g * GT:(g + 1) * GT, :],
                              in0=net.bank[6 + g % 2].rearrange("p (t d) -> p t d", t=GT),
                              in1=bc(self.bv, 1, GT), op=ALU.add).then_inc(net["a0_v_copied"], 1)

        def maxima(n):
            j = n % 8
            s = net.pairs[2 + n % 2]
            dve.wait_ge(net["a0_scores"], n + 1)
            ch.link(dve.tensor_tensor(out=s[:, P * j:P * j + P], in0=s[:, P * j:P * j + P], in1=self.mask,
                                      op=ALU.add))
            ch.link(dve.reduce_max(self.negmax[:, NT + n:NT + n + 1], s[:, P * j:1024], AX.X))
            dve.tensor_scalar(self.negmax[:, n:n + 1], self.negmax[:, NT + n:NT + n + 1], -1.0, None,
                              ALU.mult).then_inc(net["a0_negmax"], 1)

        maxima(0)
        for n in range(NT):
            if n + 1 < NT:
                maxima(n + 1)
            dve.wait_ge(net["a0_exp_done"], n + 1)
            ch.link(dve.tensor_scalar(self.total[:, NT + n:NT + n + 1], self.total[:, n:n + 1],
                                      float(np.float32(np.sqrt(128.0))), None, ALU.mult))
            ch.link(dve.reciprocal(self.total[:, NT + n:NT + n + 1], self.total[:, NT + n:NT + n + 1]))
            if n >= 2:
                self.pv_wait(dve, n - 2)
            dve.tensor_scalar(self.v_scaled[:, n % 2, :], self.v[:, n, :], self.total[:, NT + n:NT + n + 1],
                              None, ALU.mult).then_inc(net["a0_v_scaled"], 1)
            if n % 8 == 7:
                net.norm_dve(dve, ch, n // 8 * 2, twice=True)
                net.norm_dve(dve, ch, n // 8 * 2 + 1, twice=True)

    def pool(self, pool, ch):
        pool.memset(self.net.zeros[:], 0.0).then_inc(self.net["zeroed"], 1)
        pool.wait_ge(self.net["w0_loaded"], 16 * 9)
        for g in range(NG):
            self.net.norm_pool(pool, g)


class ProductKeys:
    LAYER = 1

    def __init__(self, net):
        self.net = net
        w = net.late
        w.at = 0
        self.wq = w.take(TOK)
        self.wqT = w.take(PC, P)
        self.keysT = w.take(PC, PKEYS)
        self.down = w.take(1024)
        self.up = w.take(8, P)
        self.gamma, self.beta = w.take(PC), w.take(PC)
        self.iota = net.const.take(PKEYS)
        self.coef_y = net.const.take(PC // 2, PTOP)
        self.invn = net.const.take(P)
        a = Arena(net.work)
        self.xc, self.xcT = a.take(NT, P), a.take(TOK)
        self.z = self.xc
        self.cov = a.take(P)
        self.meancol = a.take(2)
        self.scale = a.take(2, PC)
        self.ks = a.take(PC, PKEYS)
        self.m = a.take(512)
        self.brow = a.take(512)
        self.sim = a.take(2, PC * PKEYS)
        self.top = a.take(PC, PTOP)
        self.idx = a.take(PC * PTOP).bitcast(U32)
        self.idxf = a.take(PC * PTOP)
        self.coef = a.take(PC, PTOP)
        self.sums, self.left, self.chosen, self.prob = (a.take(PH, PTOP, PTOP) for _ in range(4))
        self.best = a.take(PH, PTOP)
        self.d8, self.e8 = a.take(PC, PTOP), a.take(PC, PTOP)
        self.z8, self.rz8 = a.take(PH), a.take(PH)
        self.dd, self.ed = a.take(PC, PKEYS), a.take(2, PC * PKEYS)
        self.fx = a.take(2, PH * PKEYS)
        self.onehot = a.take(PC * PTOP, PKEYS)
        self.nq = a.take(2, PC * PKEYS)
        self.expo = self.xc.rearrange("p (a t) d -> p a (t d)", a=2)
        self.rank, self.wgt = a.take(2, 1024), a.take(2, 1024)
        m = net.mid
        m.at = 0
        self.gelu, self.gw = m.take(8, GW), m.take(8, GW)

    def pe(self, pe):
        net, bank, x = self.net, self.net.bank, self.net.x
        xT = net.xT[1]
        net.layer_start(pe, 1)
        pe.wait_ge(net["w1_loaded"], 16 * 10)
        pe.wait_ge(net["zeroed"], 1)
        for t in range(NT):
            mm = pe.matmul(bank[4][:, 0:P], self.invn, x[:, t, :], start=(t == 0), stop=(t == NT - 1))
        mm.then_inc(net["p_mean"], 1)
        pe.wait_ge(net["p_centred"], 1)
        for t in range(NT):
            mm = pe.matmul(bank[5][:, 0:P], self.xc[:, t, :], self.xc[:, t, :], start=(t == 0), stop=(t == NT - 1))
        mm.then_inc(net["p_cov"], 1)
        pe.wait_ge(net["p_cov_scaled"], 1)
        for i in range(4):
            mm = pe.matmul(bank[4 + i], self.cov, self.wq[:, i * GW:(i + 1) * GW], start=True, stop=True)
            mm.then_inc(net["p_cw"], 1)
        pe.wait_ge(net["p_z"], 4)
        z = self.z.rearrange("p a b -> p (a b)")
        for c in range(PC):
            mm = pe.matmul(bank[0][:, c:c + 1], z[:, c * P:(c + 1) * P], net.ones[:, 0:1], start=True, stop=True)
        mm.then_inc(net["p_var"], 1)
        for c in range(PC):
            mm = pe.matmul(bank[3][0:1, c * PKEYS:(c + 1) * PKEYS], self.beta[:, c:c + 1], self.keysT[:, c, :],
                           start=True, stop=True)
        mm.then_inc(net["p_beta"], 1)
        pe.wait_ge(net["p_keys_scaled"], 1)
        for c in range(PC):
            mm = pe.matmul(bank[1][:, c * PKEYS:(c + 1) * PKEYS], self.wqT[:, c, :], self.ks[:, c, :],
                           start=True, stop=True)
        mm.then_inc(net["p_m"], 1)
        pe.wait_ge(net["p_m_copied"], 2)

        for g in range(NG):
            n = NG + g
            for c in range(8):
                if g or c:
                    pe.wait_ge(net["p_gelu"], 8 * g + c)
                pe.matmul(bank[4], self.down[:, c * P:(c + 1) * P], xT[:, g * GW:(g + 1) * GW],
                          start=True, stop=True).then_inc(net["p_h"], 1)
            for k in range(GT):
                t = g * GT + k
                if t:
                    pe.wait_ge(net["p_sim_copied"], t)
                pe.matmul(bank[5], self.xcT[:, t * P:(t + 1) * P], self.m, start=True, stop=False)
                pe.matmul(bank[5], net.ones[0:1, :], self.brow[0:1, :], start=False, stop=True) \
                  .then_inc(net["p_sim"], 1)
                for h in range(PH):
                    pe.wait_ge(net["p_weights"], t * PH + h + 1)
                    if h == 0 and t:
                        pe.wait_ge(net["p_gw"], t)
                    if h == 0:
                        for half in range(2):
                            pe.matmul(bank[6 + half], net.zeros[0:1, 0:P], net.zeros[0:1, :], start=True, stop=False)
                    for c in range(8):
                        mm = pe.matmul(net.pairs[3][:, c * P:(c + 1) * P], self.wgt[:, h % 2, c * P:(c + 1) * P],
                                       net.ident, start=False, stop=False,
                                       skip_group_check=True)
                    if h == PH - 1:
                        for half in range(2):
                            mm = pe.matmul(bank[6 + half], net.zeros[0:1, 0:P], net.zeros[0:1, :],
                                           start=False, stop=True)
                    mm.then_inc(net["p_summed"], 1)
            pe.wait_ge(net["p_gw"], GT * (g + 1))
            if g >= 2:
                pe.wait_ge(net["y_ready"], n - 1)
            for c in range(8):
                mm = pe.matmul(bank[g % 2], self.up[:, c, :], self.gw[:, c, :], start=(c == 0), stop=(c == 7))
            mm.then_inc(net["out_ready"], 1)
            net.norm_pe_back(pe, n)
            net.norm_pe_forth(pe, n)

    def act(self, act, ch):
        net = self.net
        net.layer_start(act, 1)
        act.wait_ge(net["p_m"], 1)
        act.activation(self.m, net.bank[1], ACT.Copy).then_inc(net["p_m_copied"], 1)
        act.wait_ge(net["p_beta"], 1)
        act.activation(self.brow[0:1, :], net.bank[3][0:1, :], ACT.Copy).then_inc(net["p_m_copied"], 1)
        for g in range(NG):
            if g:
                act.wait_ge(net["p_gw"], GT * g)
            for c in range(8):
                act.wait_ge(net["p_h"], 8 * g + c + 1)
                act.activation(self.gelu[:, c, :], net.bank[4], ACT.Gelu_apprx_tanh).then_inc(net["p_gelu"], 1)
            for k in range(GT):
                t = g * GT + k
                act.wait_ge(net["p_sim"], t + 1)
                if t >= 2:
                    act.wait_ge(net["p_weights"], PH * (t - 1))
                act.activation(self.sim[:, t % 2, :], net.bank[5], ACT.Copy).then_inc(net["p_sim_copied"], 1)
                act.wait_ge(net["p_diffs"], t + 1)
                act.activation(flat(self.e8), flat(self.d8), ACT.Exp).then_inc(net["p_e8"], 1)
                act.activation(self.ed[:, t % 2, :], flat(self.dd), ACT.Exp).then_inc(net["p_ed"], 1)
            net.norm_act(act, NG + g)

    def dve(self, dve, ch):
        net, x = self.net, self.net.x
        net.layer_start(dve, 1)
        dve.wait_ge(net["w1_loaded"], 16 * 10)
        dve.wait_ge(net["p_mean"], 1)
        ch.link(dve.tensor_tensor(out=self.xc, in0=x, in1=bc(net.bank[4][:, 0:P], 1, NT), op=ALU.subtract))
        ch.link(dve.reduce_sum(self.meancol[:, 0:1], net.xT[1][:], AX.X))
        ch.link(dve.tensor_scalar(self.meancol[:, 1:2], self.meancol[:, 0:1], 1.0 / TOK, None, ALU.mult))
        dve.tensor_scalar(self.xcT, net.xT[1][:], self.meancol[:, 1:2], None, ALU.subtract) \
           .then_inc(net["p_centred"], 1)
        dve.wait_ge(net["p_cov"], 1)
        dve.tensor_scalar(self.cov, net.bank[5][:, 0:P], 1.0 / TOK, None, ALU.mult).then_inc(net["p_cov_scaled"], 1)
        z = self.z.rearrange("p a b -> p (a b)")
        for i in range(4):
            dve.wait_ge(net["p_cw"], i + 1)
            dve.tensor_tensor(out=z[:, i * GW:(i + 1) * GW], in0=net.bank[4 + i], in1=self.wq[:, i * GW:(i + 1) * GW],
                              op=ALU.mult).then_inc(net["p_z"], 1)
        dve.wait_ge(net["p_var"], 1)
        dve.tensor_scalar(self.scale[:, 0, :], net.bank[0][:, 0:PC], 0.0, 1e-5, ALU.max, ALU.add) \
           .then_inc(net["p_varsum"], 1)
        dve.wait_ge(net["p_rstd"], 1)
        ch.link(dve.tensor_tensor(out=self.scale[:, 1, :], in0=self.scale[:, 1, :], in1=self.gamma, op=ALU.mult))
        dve.tensor_tensor(out=self.ks, in0=self.keysT, in1=bc(self.scale[:, 1, :], 2, PKEYS), op=ALU.mult) \
           .then_inc(net["p_keys_scaled"], 1)
        dve.tensor_copy(self.coef[:, PH:PC, :], self.coef_y)

        for g in range(NG):
            for k in range(GT):
                t = g * GT + k
                self.route(dve, ch, t)
                for h in range(PH):
                    i = t * PH + h
                    dve.wait_ge(net["p_pairs"], i + 1)
                    if i >= 2:
                        dve.wait_ge(net["p_summed"], i - 1)
                    dve.scalar_tensor_tensor(out=self.wgt[:, h % 2, :], in0=self.rank[:, h % 2, :], scalar=8.0,
                                             in1=self.expo[:, h % 2, :], op0=ALU.is_gt, op1=ALU.mult) \
                       .then_inc(net["p_weights"], 1)
                dve.wait_ge(net["p_summed"], PH * (t + 1))
                if k == 0:
                    dve.wait_ge(net["p_gelu"], 8 * (g + 1))
                    if g:
                        dve.wait_ge(net["out_ready"], NG + g)
                dve.tensor_tensor(out=self.gw[:, :, k * P:(k + 1) * P],
                                  in0=net.pairs[3][:, :].rearrange("p (c t) -> p c t", c=8),
                                  in1=self.gelu[:, :, k * P:(k + 1) * P], op=ALU.mult).then_inc(net["p_gw"], 1)
            net.norm_dve(dve, ch, NG + g)

    def route(self, dve, ch, t):
        net = self.net
        sim = self.sim[:, t % 2, :].rearrange("p (c v) -> p c v", c=PC)
        dve.wait_ge(net["p_sim_copied"], t + 1)
        for c in range(PC):
            ins = dve.max(self.top[:, c, :], sim[:, c, :])
        ch.link(ins)
        dve.tensor_tensor(out=self.d8, in0=self.top, in1=self.top[:, :, 0:1].broadcast_to([P, PC, PTOP]),
                          op=ALU.subtract)
        dve.tensor_tensor(out=self.dd, in0=sim, in1=self.top[:, :, 0:1].broadcast_to([P, PC, PKEYS]),
                          op=ALU.subtract).then_inc(net["p_diffs"], 1)
        for c in range(PC):
            ins = dve.max_index(self.idx[:, c * PTOP:(c + 1) * PTOP], self.top[:, c, :], sim[:, c, :])
        ch.link(dve.tensor_tensor(out=self.sums, in0=bc(self.top[:, 0:PH, :], 3, PTOP),
                                  in1=bc(self.top[:, PH:PC, :], 2, PTOP), op=ALU.add))
        dve.tensor_copy(self.idxf, self.idx)
        for h in range(PH):
            ins = dve.max(self.best[:, h, :], self.sums[:, h, :, :].rearrange("p i j -> p (i j)"))
        ch.link(ins)
        for h in range(PH):
            ins = dve.match_replace(self.left[:, h, :, :].rearrange("p i j -> p (i j)"), self.best[:, h, :],
                                    self.sums[:, h, :, :].rearrange("p i j -> p (i j)"), NEG)
        ch.link(ins)

        def f(ap):
            return ap.rearrange("p h i j -> p (h i j)")

        ch.link(dve.tensor_tensor(out=f(self.chosen), in0=f(self.sums), in1=f(self.left), op=ALU.not_equal))
        dve.tensor_reduce(self.coef[:, 0:PH, :], self.chosen, AX.X, ALU.add)
        dve.wait_ge(net["p_e8"], t + 1)
        ch.link(dve.tensor_tensor(out=self.prob, in0=bc(self.e8[:, 0:PH, :], 3, PTOP),
                                  in1=bc(self.e8[:, PH:PC, :], 2, PTOP), op=ALU.mult))
        ch.link(dve.tensor_tensor(out=f(self.prob), in0=f(self.prob), in1=f(self.chosen), op=ALU.mult))
        ch.link(dve.tensor_reduce(self.z8, self.prob.rearrange("p h i j -> p h (i j)"), AX.X, ALU.add))
        ch.link(dve.reciprocal(self.rz8, self.z8))
        dve.wait_ge(net["p_ed"], t + 1)
        ed = self.ed[:, t % 2, :].rearrange("p (c v) -> p c v", c=PC)
        dve.tensor_tensor(out=self.fx[:, t % 2, :].rearrange("p (h v) -> p h v", h=PH), in0=ed[:, 0:PH, :],
                          in1=bc(self.rz8, 2, PKEYS), op=ALU.mult)
        ch.link(dve.tensor_tensor(out=self.onehot, in0=bc(self.iota, 1, PC * PTOP), in1=bc(self.idxf, 2, PKEYS),
                                  op=ALU.is_equal))
        ch.link(dve.tensor_tensor(out=self.onehot, in0=self.onehot, in1=bc(flat(self.coef), 2, PKEYS),
                                  op=ALU.mult))
        dve.tensor_reduce(self.nq[:, t % 2, :].rearrange("p (c v) -> p c v", c=PC),
                          self.onehot.rearrange("p (c j) v -> p c v j", c=PC), AX.X, ALU.add) \
           .then_inc(net["p_routed"], 1)

    def pool(self, pool, ch):
        net = self.net
        pool.wait_ge(net["p_varsum"], 1)
        pool.tensor_tensor(out=self.scale[:, 1, :], in0=self.scale[:, 0, :], in1=net.minus_half, op=ALU.pow) \
            .then_inc(net["p_rstd"], 1)
        for t in range(NT):
            pool.wait_ge(net["p_routed"], t + 1)
            for h in range(PH):
                i = t * PH + h
                if i >= 2:
                    pool.wait_ge(net["p_weights"], i - 1)
                nq = self.nq[:, t % 2, :].rearrange("p (c v) -> p c v", c=PC)
                ed = self.ed[:, t % 2, :].rearrange("p (c v) -> p c v", c=PC)
                fx = self.fx[:, t % 2, :].rearrange("p (h v) -> p h v", h=PH)
                r = self.rank[:, h % 2, :].rearrange("p (x y) -> p x y", x=PKEYS)
                e = self.expo[:, h % 2, :].rearrange("p (x y) -> p x y", x=PKEYS)
                pool.tensor_tensor(out=r, in0=bc(nq[:, h, :], 2, PKEYS), in1=bc(nq[:, PH + h, :], 1, PKEYS),
                                   op=ALU.add)
                pool.tensor_tensor(out=e, in0=bc(fx[:, h, :], 2, PKEYS), in1=bc(ed[:, PH + h, :], 1, PKEYS),
                                   op=ALU.mult).then_inc(net["p_pairs"], 1)
            if t % GT == GT - 1:
                net.norm_pool(pool, NG + t // GT)


class Lightning:
    LAYER = 2

    def __init__(self, net):
        self.net = net
        w = net.late
        w.at = 0
        self.wq, self.wqr = w.take(8, P), w.take(8, P)
        self.wk, self.wkr = w.take(2, P), w.take(2, P)
        self.wv = w.take(2 * P)
        self.wo = w.take(8, P)
        self.cos, self.sin = w.take(1024), w.take(1024)
        self.decay = w.take(16, P)
        self.qdec = w.take(8, P)
        self.kdec = w.take(16)
        self.blk = w.take(8)
        a = Arena(net.work)
        self.q = a.take(8, GW)
        self.k = a.take(2, GW)
        self.turned = a.take(2, GW)
        self.v, self.ktok = a.take(GT, 2 * P), a.take(GT, 2 * P)
        self.qd = a.take(2, 8, P)
        self.vd = a.take(2, 16, HD)
        self.s = a.take(2, GW)
        self.o = a.take(8, GW)
        self.state = a.take(8, HD)

    def pe(self, pe):
        net, bank = self.net, self.net.bank
        xT = net.xT[0]
        net.layer_start(pe, 2)
        pe.wait_ge(net["w2_loaded"], 16 * 12)
        for g in range(NG):
            n = 2 * NG + g
            xg = xT[:, g * GW:(g + 1) * GW]
            for c in range(10):
                i = 10 * g + c
                w, wr = (self.wq[:, c, :], self.wqr[:, c, :]) if c < 8 else (self.wk[:, c - 8, :], self.wkr[:, c - 8, :])
                if i >= 2:
                    pe.wait_ge(net["l_rotated"], i - 1)
                if c == 1 and g:
                    pe.wait_ge(net["l_o_copied"], 8 * g)
                pe.matmul(bank[4 + 2 * (c % 2)], w, xg, start=True, stop=True)
                pe.matmul(bank[5 + 2 * (c % 2)], wr, xg, start=True, stop=True).then_inc(net["l_qk"], 1)
            pe.wait_ge(net["l_rotated"], 10 * (g + 1))
            for k in range(GT):
                t = g * GT + k
                mm = pe.matmul(net.pairs[3][:, k * 2 * P:(k + 1) * 2 * P], xT[:, t * P:(t + 1) * P], self.wv,
                               start=True, stop=True)
            mm.then_inc(net["l_v"], 1)
            pe.wait_ge(net["l_summed"], 10 * (g + 1))
            for k in range(GT):
                for pr in range(2):
                    o = k * 2 * P + pr * P
                    mm = pe.transpose(net.pairs[2][:, o:o + P], self.k[:, pr, k * P:(k + 1) * P], net.ident)
            mm.then_inc(net["l_kt"], 1)
            pe.wait_ge(net["l_vk_copied"], 2 * (g + 1))
            for k in range(GT):
                t = g * GT + k
                for kv in range(NKV):
                    i = t * NKV + kv
                    pr, half = divmod(kv, 2)
                    rows = slice(half * HD, half * HD + HD)
                    if i >= 2:
                        pe.wait_ge(net["l_decayed"], i - 1)
                    pe.matmul(bank[4 + kv % 2], self.k[rows, pr, k * P:(k + 1) * P],
                              self.q[rows, pr * 4:pr * 4 + 4, k * P:(k + 1) * P], start=True, stop=True) \
                      .then_inc(net["l_scores"], 1)
                    if kv:
                        self.output(pe, t, kv - 1)
                self.output(pe, t, 3)
                if t % 8 != 7:
                    pe.wait_ge(net["l_vd"], t + 1)
                    if t:
                        pe.wait_ge(net["l_state"], t - t // 8)
                    if n:
                        pe.wait_ge(net["normed"], n)
                    for kv in range(NKV):
                        pr, half = divmod(kv, 2)
                        mm = pe.matmul(bank[2][half * HD:half * HD + HD, pr * 256:pr * 256 + 256],
                                       self.ktok[:, k, kv * HD:(kv + 1) * HD],
                                       self.vd[:, t % 2, kv * 4:kv * 4 + 4, :].rearrange("p a b -> p (a b)"),
                                       start=True, stop=True)
                    mm.then_inc(net["l_added"], 1)
            pe.wait_ge(net["l_o_copied"], 8 * (g + 1))
            if n >= 2:
                pe.wait_ge(net["y_ready"], n - 1)
            for c in range(8):
                mm = pe.matmul(bank[g % 2], self.wo[:, c, :], self.o[:, c, :], start=(c == 0), stop=(c == 7))
            mm.then_inc(net["out_ready"], 1)
            net.norm_pe_back(pe, n)
            net.norm_pe_forth(pe, n)

    def output(self, pe, t, kv):
        net = self.net
        k = t % GT
        pr, half = divmod(kv, 2)
        rows = slice(half * HD, half * HD + HD)
        out = net.bank[6 + pr][rows, :]
        first = t % 8 == 0
        if t and half == 0:
            pe.wait_ge(net["l_o_copied"], 2 * (t - 1) + pr + 1)
        if not first:
            pe.wait_ge(net["l_qd"], t + 1)
            pe.wait_ge(net["l_state"], t - t // 8)
            for m in range(4):
                pe.matmul(out[:, m * P:(m + 1) * P], self.state[rows, pr * 4 + m, :],
                          self.qd[rows, t % 2, pr * 4 + m, :], start=(m == 0), stop=False, skip_group_check=True)
        pe.wait_ge(net["l_decayed"], t * NKV + kv + 1)
        mm = pe.matmul(out, self.v[:, k, kv * HD:(kv + 1) * HD], self.s[:, kv % 2, :], start=first, stop=True,
                       skip_group_check=True)
        mm.then_inc(net["l_out"], 1)

    def act(self, act, ch):
        net = self.net
        net.layer_start(act, 2)
        for g in range(NG):
            act.wait_ge(net["l_v"], g + 1)
            if g:
                act.wait_ge(net["out_ready"], 2 * NG + g)
            act.activation(self.v.rearrange("p a b -> p (a b)"), net.pairs[3][:, :], ACT.Copy) \
               .then_inc(net["l_vk_copied"], 1)
            act.wait_ge(net["l_kt"], g + 1)
            act.activation(self.ktok.rearrange("p a b -> p (a b)"), net.pairs[2][:, :], ACT.Copy) \
               .then_inc(net["l_vk_copied"], 1)
            for k in range(GT):
                t = g * GT + k
                for pr in range(2):
                    act.wait_ge(net["l_out"], t * NKV + 2 * pr + 2)
                    act.activation(self.o[:, pr * 4:pr * 4 + 4, k * P:(k + 1) * P],
                                   net.bank[6 + pr].rearrange("p (a b) -> p a b", a=4), ACT.Copy) \
                       .then_inc(net["l_o_copied"], 1)
            net.norm_act(act, 2 * NG + g)

    def dve(self, dve, ch):
        net = self.net
        net.layer_start(dve, 2)
        dve.wait_ge(net["w2_loaded"], 16 * 12)
        for g in range(NG):
            pos = (g % 2) * GW
            if g:
                dve.wait_ge(net["out_ready"], 2 * NG + g)
            for c in range(10):
                i = 10 * g + c
                b = 4 + 2 * (c % 2)
                dve.wait_ge(net["l_qk"], i + 1)
                dst = self.q[:, c, :] if c < 8 else self.k[:, c - 8, :]
                dve.tensor_tensor(out=dst, in0=net.bank[b], in1=self.cos[:, pos:pos + GW], op=ALU.mult)
                if i >= 2:
                    dve.wait_ge(net["l_summed"], i - 1)
                dve.tensor_tensor(out=self.turned[:, c % 2, :], in0=net.bank[b + 1], in1=self.sin[:, pos:pos + GW],
                                  op=ALU.mult).then_inc(net["l_rotated"], 1)
            for k in range(GT):
                t = g * GT + k
                for kv in range(NKV):
                    i = t * NKV + kv
                    dve.wait_ge(net["l_scores"], i + 1)
                    if i >= 2:
                        dve.wait_ge(net["l_out"], i - 1)
                    dve.tensor_tensor(out=self.s[:, kv % 2, :], in0=net.bank[4 + kv % 2],
                                      in1=self.decay[:, kv * 4:kv * 4 + 4, :].rearrange("p a b -> p (a b)"),
                                      op=ALU.mult).then_inc(net["l_decayed"], 1)
                if t % 8 != 7:
                    state = self.state.rearrange("p a b -> p (a b)")
                    dve.wait_ge(net["l_out"], (t + 1) * NKV)
                    dve.wait_ge(net["l_added"], t + 1 - t // 8)
                    if t % 8 == 0:
                        dve.tensor_copy(state, net.bank[2]).then_inc(net["l_state"], 1)
                    else:
                        ch.link(dve.tensor_tensor(out=self.state, in0=self.state, in1=bc(self.blk, 2, HD),
                                                  op=ALU.mult))
                        dve.tensor_tensor(out=state, in0=state, in1=net.bank[2], op=ALU.add) \
                           .then_inc(net["l_state"], 1)
            net.norm_dve(dve, ch, 2 * NG + g)

    def pool(self, pool, ch):
        net = self.net
        pool.wait_ge(net["w2_loaded"], 16 * 12)
        net.layer_start(pool, 2)
        for g in range(NG):
            for c in range(10):
                dst = self.q[:, c, :] if c < 8 else self.k[:, c - 8, :]
                pool.wait_ge(net["l_rotated"], 10 * g + c + 1)
                pool.tensor_tensor(out=dst, in0=dst, in1=self.turned[:, c % 2, :], op=ALU.add) \
                    .then_inc(net["l_summed"], 1)
            pool.wait_ge(net["l_summed"], 10 * (g + 1))
            pool.wait_ge(net["l_vk_copied"], 2 * g + 1)
            for k in range(GT):
                t = g * GT + k
                if t >= 2:
                    pool.wait_ge(net["l_out"], (t - 1) * NKV)
                    pool.wait_ge(net["l_added"], t - 1 - (t - 1) // 8)
                pool.tensor_tensor(out=self.qd[:, t % 2, :, :], in0=self.q[:, :, k * P:(k + 1) * P], in1=self.qdec,
                                   op=ALU.mult).then_inc(net["l_qd"], 1)
                for kv in range(NKV):
                    ins = pool.tensor_tensor(out=self.vd[:, t % 2, kv * 4:kv * 4 + 4, :],
                                             in0=bc(self.v[:, k, kv * HD:(kv + 1) * HD], 1, 4),
                                             in1=bc(self.kdec[:, kv * 4:kv * 4 + 4], 2, HD), op=ALU.mult)
                ins.then_inc(net["l_vd"], 1)
            net.norm_pool(pool, 2 * NG + g)


class Gates:

    def __init__(self, net, arena, layer, experts, keep, renorm, tag):
        self.net, self.layer, self.experts, self.keep, self.renorm, self.tag = net, layer, experts, keep, renorm, tag
        self.wide = experts + 8 - keep
        a = arena
        self.logit = a.take(GT, 16)
        self.peak, self.total = a.take(GT), a.take(GT)
        self.weights = a.take(GT, 24)
        self.top, self.kept, self.left = a.take(GT, 8), a.take(GT, 8), a.take(GT, 24)
        self.gate = a.take(GT, 16)
        self.gateT = a.take(GW)
        self.spread = a.take(experts, GW)

    def pe(self, pe, g, xT, w, b):
        net, E = self.net, self.experts
        n = self.layer * NG + g
        if g:
            pe.wait_ge(net[self.tag + "_spread"], E * g)
        for k in range(GT):
            t = g * GT + k
            out = net.bank[6][:, k * 16:k * 16 + E]
            mm = pe.matmul(out, xT[:, t * P:(t + 1) * P], w, start=True, stop=(b is None))
            if b is not None:
                mm = pe.matmul(out, net.ones[0:1, :], b, start=False, stop=True)
        mm.then_inc(net[self.tag + "_logits"], 1)
        pe.wait_ge(net[self.tag + "_gates"], g + 1)
        for k in range(GT):
            mm = pe.transpose(net.bank[7][0:16, k * P:(k + 1) * P], self.gate[:, k, :], net.ident)
        mm.then_inc(net[self.tag + "_gatesT"], 1)
        pe.wait_ge(net[self.tag + "_gatesT_copied"], g + 1)
        for e in range(E):
            i = g * E + e
            if e >= 2:
                pe.wait_ge(net[self.tag + "_spread"], i - 1)
            pe.matmul(net.bank[6 + e % 2], self.sel[0:16, e, :], self.gateT[0:16, :], start=True, stop=True) \
              .then_inc(net[self.tag + "_wide"], 1)

    def act(self, act, g):
        net, E = self.net, self.experts
        act.wait_ge(net[self.tag + "_shifted"], g + 1)
        act.activation(self.weights[:, :, 0:E], self.logit[:, :, 0:E], ACT.Exp).then_inc(net[self.tag + "_exp"], 1)
        act.wait_ge(net[self.tag + "_gatesT"], g + 1)
        if g:
            act.wait_ge(net["out_ready"], self.layer * NG + g)
        act.activation(self.gateT[0:16, :], net.bank[7][0:16, :], ACT.Copy) \
           .then_inc(net[self.tag + "_gatesT_copied"], 1)
        for e in range(E):
            act.wait_ge(net[self.tag + "_wide"], g * E + e + 1)
            act.activation(self.spread[:, e, :], net.bank[6 + e % 2], ACT.Copy).then_inc(net[self.tag + "_spread"], 1)

    def dve_fill(self, dve):
        for i in range(8 - self.keep):
            dve.memset(self.weights[:, :, self.experts + i:self.experts + i + 1], -1.0 - i)
            dve.memset(self.kept[:, :, self.keep + i:self.keep + i + 1], -1.0 - i)
        dve.memset(self.gate[:, :, 0:15], 0.0)
        return dve.memset(self.gate[:, :, 15:16], 1.0)

    def dve(self, dve, ch, g):
        net, E, keep, wide = self.net, self.experts, self.keep, self.wide
        dve.wait_ge(net[self.tag + "_logits"], g + 1)
        raw = net.bank[6][:, 0:GT * 16].rearrange("p (k e) -> p k e", k=GT)[:, :, 0:E]
        ch.link(dve.reduce_max(self.peak, raw, AX.X))
        dve.tensor_tensor(out=self.logit[:, :, 0:E], in0=raw, in1=bc(self.peak, 2, E), op=ALU.subtract) \
           .then_inc(net[self.tag + "_shifted"], 1)
        dve.wait_ge(net[self.tag + "_exp"], g + 1)
        w = self.weights[:, :, 0:E]
        ch.link(dve.reduce_sum(self.total, w, AX.X))
        ch.link(dve.reciprocal(self.total, self.total))
        ch.link(dve.tensor_tensor(out=w, in0=w, in1=bc(self.total, 2, E), op=ALU.mult))
        for k in range(GT):
            ins = dve.max(self.top[:, k, :], self.weights[:, k, 0:E])
        ch.link(ins)
        ch.link(dve.tensor_copy(self.kept[:, :, 0:keep], self.top[:, :, 0:keep]))
        for k in range(GT):
            ins = dve.match_replace(self.left[:, k, 0:wide], self.kept[:, k, :], self.weights[:, k, 0:wide], -99.0)
        ch.link(ins)
        ch.link(dve.tensor_tensor(out=self.left[:, :, 0:E], in0=w, in1=self.left[:, :, 0:E], op=ALU.not_equal))
        last = dve.tensor_tensor(out=self.gate[:, :, 0:E], in0=w, in1=self.left[:, :, 0:E], op=ALU.mult)
        if self.renorm is not None:
            ch.link(last)
            ch.link(dve.reduce_sum(self.total, self.gate[:, :, 0:E], AX.X))
            ch.link(dve.tensor_scalar(self.total, self.total, self.renorm, None, ALU.add))
            ch.link(dve.reciprocal(self.total, self.total))
            last = dve.tensor_tensor(out=self.gate[:, :, 0:E], in0=self.gate[:, :, 0:E],
                                     in1=bc(self.total, 2, E), op=ALU.mult)
        last.then_inc(net[self.tag + "_gates"], 1)


class GeluExperts:
    LAYER = 3

    def __init__(self, net):
        self.net = net
        w = net.mid
        w.at = 0
        self.w1, self.w2 = w.take(C1, P), w.take(C1, P)
        self.b1 = w.take(C1)
        self.gw = w.take(16)
        self.gb = w.take(16)
        self.b2 = w.take(P)
        a = Arena(net.work)
        self.gates = Gates(net, a, 3, E1, 3, None, "g1")
        self.gates.sel = a.take(E1, P)
        self.h, self.hg = a.take(3, GW), a.take(3, GW)

    def pe(self, pe):
        net, bank = self.net, self.net.bank
        xT = net.xT[1]
        net.layer_start(pe, 3)
        pe.wait_ge(net["w3_loaded"], 16 * 7)
        for g in range(NG):
            n = 3 * NG + g
            self.gates.pe(pe, g, xT, self.gw[:, 0:E1], self.gb[0:1, 0:E1])
            for c in range(C1 + 1):
                i = C1 * g + c
                if c < C1:
                    if i >= 2:
                        pe.wait_ge(net["e1_act"], i - 1)
                    pe.matmul(bank[4 + i % 2], self.w1[:, c, :], xT[:, g * GW:(g + 1) * GW], start=True, stop=True) \
                      .then_inc(net["e1_up"], 1)
                if c:
                    j = i - 1
                    if c == 1 and n >= 2:
                        pe.wait_ge(net["y_ready"], n - 1)
                    if c - 1 < C1S:
                        pe.wait_ge(net["e1_act"], j + 1)
                        src = self.h[:, j % 3, :]
                    else:
                        pe.wait_ge(net["e1_gated"], j + 1 - C1S * (g + 1))
                        src = self.hg[:, j % 3, :]
                    pe.matmul(bank[g % 2], self.w2[:, c - 1, :], src, start=(c == 1), stop=False) \
                      .then_inc(net["e1_down"], 1)
            pe.matmul(bank[g % 2], self.b2[0:16, :], self.gates.gateT[0:16, :], start=False, stop=True) \
              .then_inc(net["out_ready"], 1)
            net.norm_pe_back(pe, n)
            net.norm_pe_forth(pe, n)

    def act(self, act, ch):
        net = self.net
        net.layer_start(act, 3)
        act.wait_ge(net["w3_loaded"], 16 * 7)
        act.wait_ge(net["g1_filled"], 1)
        for g in range(NG):
            self.gates.act(act, g)
            for c in range(C1):
                i = C1 * g + c
                act.wait_ge(net["e1_up"], i + 1)
                if i >= 3:
                    act.wait_ge(net["e1_down"], i - 2)
                act.activation(self.h[:, i % 3, :], net.bank[4 + i % 2], ACT.Gelu, bias=self.b1[:, c:c + 1]) \
                   .then_inc(net["e1_act"], 1)
            net.norm_act(act, 3 * NG + g)

    def dve(self, dve, ch):
        net = self.net
        net.layer_start(dve, 3)
        dve.wait_ge(net["w3_loaded"], 16 * 7)
        self.gates.dve_fill(dve).then_inc(net["g1_filled"], 1)
        dve.wait_ge(net["g1_filled"], 1)
        for g in range(NG):
            self.gates.dve(dve, ch, g)
            for c in range(C1S, C1):
                i = C1 * g + c
                e = (c - C1S) // 2
                dve.wait_ge(net["e1_act"], i + 1)
                dve.wait_ge(net["g1_spread"], E1 * g + e + 1)
                if i >= 3:
                    dve.wait_ge(net["e1_down"], i - 2)
                dve.tensor_tensor(out=self.hg[:, i % 3, :], in0=self.h[:, i % 3, :],
                                  in1=self.gates.spread[:, e, :], op=ALU.mult).then_inc(net["e1_gated"], 1)
            net.norm_dve(dve, ch, 3 * NG + g, twice=True)

    def pool(self, pool, ch):
        for g in range(NG):
            self.net.norm_pool(pool, 3 * NG + g)


class Forgetting:
    LAYER = 4
    SLOTS = 4

    def __init__(self, net):
        self.net = net
        w = net.const
        self.wq, self.wk = w.take(4, P), w.take(4, P)
        self.wv, self.wo, self.wf = w.take(P), w.take(P), w.take(16)
        self.onerow = w.take(2)
        self.mask_n, self.mask_t = w.take(P), w.take(P)
        a = Arena(net.work)
        self.q, self.k = a.take(4, TOK), a.take(4, TOK)
        self.v = a.take(NT, FH, FD + 1)
        self.e = a.take(2, 1024)
        self.fneg = self.e.rearrange("p a b -> p (a b)")
        q2 = self.q.rearrange("p a b -> p (a b)")
        self.z, self.zabs, self.fl = (q2[:, i * TOK:(i + 1) * TOK] for i in range(3))
        self.m = a.take(2, FH)
        self.negm = a.take(2, FH)
        self.mrow = a.take(2, P)
        self.rz = a.take(FH)
        self.o = a.take(P)
        self.oT = a.take(GW)
        net.const.take(0) if False else None

    def pe(self, pe):
        net, bank = self.net, self.net.bank
        xT = net.xT[0]
        net.layer_start(pe, 4)
        pe.wait_ge(net["w4_loaded"], 16 * 8)
        for g in range(NG):
            pe.matmul(bank[4 + g][0:16, :], self.wf, xT[:, g * GW:(g + 1) * GW], start=True, stop=True) \
              .then_inc(net["f_z"], 1)
        for i in range(2 * NG):
            pass
        for g in range(NG):
            if g >= 2:
                pe.wait_ge(net["f_v_copied"], g - 1)
            for k in range(GT):
                t = g * GT + k
                mm = pe.matmul(bank[g % 2][:, k * P:(k + 1) * P], xT[:, t * P:(t + 1) * P], self.wv,
                               start=True, stop=True)
            mm.then_inc(net["f_v"], 1)
        for i in range(32):
            g, s = i % 4, (i // 4) % 4
            w = (self.wk, self.wq)[i // 16]
            if i < 4:
                pe.wait_ge(net["f_z_copied"], i + 1)
            else:
                pe.wait_ge(net["f_qk_copied"], i - 3)
            pe.matmul(bank[4 + i % 4], w[:, s, :], xT[:, g * GW:(g + 1) * GW], start=True, stop=True) \
              .then_inc(net["f_qk"], 1)
        pe.wait_ge(net["f_qk_copied"], 32)
        pe.wait_ge(net["f_v_copied"], NG)
        pe.wait_ge(net["f_rows"], 16 * 4)
        for h in range(FH):
            self.natural(pe, 0, h)
        self.turn_max(pe, 0)
        for t in range(NT):
            n = 4 * NG + t // GT
            k = t % GT
            for h in range(FH):
                if t + 1 < NT:
                    self.natural(pe, t + 1, h)
                self.turned(pe, t, h)
                if h:
                    self.values(pe, t, h - 1)
            self.values(pe, t, FH - 1)
            pe.wait_ge(net["f_o"], t + 1)
            if k == 0 and n >= 2:
                pe.wait_ge(net["y_ready"], n - 1)
            pe.transpose(bank[n % 2][:, k * P:(k + 1) * P], self.o, net.ident).then_inc(net["f_oT"], 1)
            if k == GT - 1:
                pe.wait_ge(net["f_oT_copied"], t // GT + 1)
                pe.matmul(bank[n % 2], self.wo, self.oT, start=True, stop=True).then_inc(net["out_ready"], 1)
                net.norm_pe_back(pe, n)
                net.norm_pe_forth(pe, n)
            if t + 1 < NT:
                self.turn_max(pe, t + 1)

    def natural(self, pe, t, h):
        net = self.net
        b, it = divmod(t, 8)
        s, q = divmod(h, 4)
        rows = slice(32 * q, 32 * q + FD + 1)
        if t or h:
            pe.wait_ge(net["f_max"], t * FH + h)
        width = (it + 1) * P
        for lo in list(range(0, width - P, GW)) + [width - P]:
            hi = min(lo + GW, width - P) if lo < width - P else width
            pe.matmul(net.pairs[2][:, lo:hi], self.q[rows, s, t * P:(t + 1) * P],
                      self.k[rows, s, b * 1024 + lo:b * 1024 + hi], start=True, stop=(hi < width))
        mm = pe.matmul(net.pairs[2][:, width - P:width], net.ident, self.mask_n, start=False, stop=True)
        mm.then_inc(net["f_scores"], 1)

    def turn_max(self, pe, t):
        net = self.net
        n = 4 * NG + t // GT
        pe.wait_ge(net["f_negmax"], t + 1)
        if t:
            pe.wait_ge(net["f_o"], t)
        pe.transpose(self.obank(t)[0:16, 288:416], self.negm[:, t % 2, :], net.ident).then_inc(net["f_mT"], 1)

    def obank(self, t):
        return self.net.bank[1 - (t // GT) % 2]

    def turned(self, pe, t, h):
        net = self.net
        b, it = divmod(t, 8)
        s, q = divmod(h, 4)
        rows = slice(32 * q, 32 * q + FD + 2)
        i = t * FH + h
        if h == 0:
            pe.wait_ge(net["f_mrows"], 16 * 4 * (t + 1))
        if i:
            pe.wait_ge(net["f_exp"], i)
        for j in range(it + 1):
            mm = pe.matmul(net.pairs[3][:, j * P:(j + 1) * P], self.k[rows, s, (b * 8 + j) * P:(b * 8 + j + 1) * P],
                           self.q[rows, s, t * P:(t + 1) * P], start=True, stop=(j < it), skip_group_check=True)
        mm = pe.matmul(net.pairs[3][:, it * P:(it + 1) * P], net.ident, self.mask_t, start=False, stop=True,
                       skip_group_check=True)
        mm.then_inc(net["f_shifted"], 1)

    def values(self, pe, t, h):
        net = self.net
        b, it = divmod(t, 8)
        n = 4 * NG + t // GT
        i = t * FH + h
        pe.wait_ge(net["f_exp"], i + 1)
        if h == 0:
            if t >= 2:
                pe.wait_ge(net["f_o"], t - 1)
            if n and t % GT == 0:
                pe.wait_ge(net["y_ready"], n)
        o = self.obank(t)[:, (t % 2) * 144 + h * 9:(t % 2) * 144 + h * 9 + 9]
        for j in range(it + 1):
            mm = pe.matmul(o, self.e[:, i % 2, j * P:(j + 1) * P], self.v[:, b * 8 + j, h, :],
                           start=(j == 0), stop=(j == it), skip_group_check=True)
        mm.then_inc(net["f_values"], 1)

    def act(self, act, ch):
        net = self.net
        net.layer_start(act, 4)
        act.wait_ge(net["w4_loaded"], 16 * 8)
        act.wait_ge(net["f_zabs"], 1)
        ch.link(act.activation(self.zabs[0:16, :], self.zabs[0:16, :], ACT.Exp))
        act.activation(self.zabs[0:16, :], self.zabs[0:16, :], ACT.Ln, bias=1.0).then_inc(net["f_ln"], 1)
        for i in range(32):
            g, s = i % 4, (i // 4) % 4
            act.wait_ge(net["f_qk"], i + 1)
            dst = (self.k, self.q)[i // 16][:, s, g * GW:(g + 1) * GW]
            if i == 16:
                act.wait_ge(net["f_cum"], 2)
            col = (1, 0)[i // 16]
            act.activation(dst, net.bank[4 + i % 4], ACT.Identity, bias=self.onerow[:, col:col + 1],
                           scale=(1.0, float(FD) ** -0.5)[i // 16]).then_inc(net["f_qk_copied"], 1)
        for t in range(NT):
            b, it = divmod(t, 8)
            for h in range(FH):
                i = t * FH + h
                if i == 0:
                    act.wait_ge(net["f_rows"], 16 * 4)
                act.wait_ge(net["f_shifted"], i + 1)
                if i >= 2:
                    act.wait_ge(net["f_values"], i - 1)
                act.activation(self.e[:, i % 2, 0:(it + 1) * P], net.pairs[3][:, 0:(it + 1) * P], ACT.Exp) \
                   .then_inc(net["f_exp"], 1)
            act.wait_ge(net["f_oT"], t + 1)
            if t % GT == GT - 1:
                g = t // GT
                if g:
                    act.wait_ge(net["out_ready"], 4 * NG + g)
                act.activation(self.oT, net.bank[(4 * NG + g) % 2], ACT.Copy).then_inc(net["f_oT_copied"], 1)
                net.norm_act(act, 4 * NG + g)

    def dve(self, dve, ch):
        net = self.net
        net.layer_start(dve, 4)
        dve.wait_ge(net["w4_loaded"], 16 * 8)
        for g in range(NG):
            dve.wait_ge(net["f_z"], g + 1)
            ins = dve.tensor_copy(self.z[0:16, g * GW:(g + 1) * GW], net.bank[4 + g][0:16, :])
            ins.then_inc(net["f_z_copied"], 1)
        dve.wait_ge(net["f_z_copied"], NG)
        z, za, fl = self.z[0:16, :], self.zabs[0:16, :], self.fl[0:16, :]
        dve.scalar_tensor_tensor(out=za, in0=z, scalar=-1.0, in1=z, op0=ALU.mult, op1=ALU.min) \
           .then_inc(net["f_zabs"], 1)
        ch.link(dve.tensor_scalar(fl, z, -1.0, 0.0, ALU.mult, ALU.max))
        ch.link(dve.memset(self.v, 1.0))
        for g in range(NG):
            dve.wait_ge(net["f_v"], g + 1)
            dve.tensor_copy(self.v[:, g * GT:(g + 1) * GT, :, 0:FD],
                            net.bank[g % 2].rearrange("p (t h d) -> p t h d", t=GT, h=FH)) \
               .then_inc(net["f_v_copied"], 1)
        dve.wait_ge(net["f_ln"], 1)
        ch.link(dve.tensor_tensor(out=fl, in0=fl, in1=za, op=ALU.add))
        ch.link(dve.memset(z, 1.0))
        for b in range(2):
            c = slice(b * 1024, (b + 1) * 1024)
            dve.tensor_tensor_scan(self.fneg[0:16, c], z[:, c], fl[:, c], 0.0, ALU.mult, ALU.add) \
               .then_inc(net["f_cum"], 1)
        self.maxima(dve, ch, 0)
        for t in range(NT):
            if t + 1 < NT:
                self.maxima(dve, ch, t + 1)
            dve.wait_ge(net["f_values"], FH * (t + 1))
            o = self.obank(t)[:, (t % 2) * 144:(t % 2) * 144 + 144].rearrange("p (h e) -> p h e", h=FH)
            if t:
                dve.wait_ge(net["f_oT"], t)
            ch.link(dve.reciprocal(self.rz, o[:, :, FD]))
            dve.tensor_tensor(out=self.o.rearrange("p (h d) -> p h d", h=FH), in0=o[:, :, 0:FD],
                              in1=bc(self.rz, 2, FD), op=ALU.mult).then_inc(net["f_o"], 1)
            if t % GT == GT - 1:
                net.norm_dve(dve, ch, 4 * NG + t // GT)
            if t + 1 < NT:
                self.rows(dve, t + 1)

    def maxima(self, dve, ch, t):
        net = self.net
        it = t % 8
        for h in range(FH):
            dve.wait_ge(net["f_scores"], t * FH + h + 1)
            dve.reduce_max(self.m[:, t % 2, h:h + 1], net.pairs[2][:, 0:(it + 1) * P], AX.X) \
               .then_inc(net["f_max"], 1)
        dve.wait_ge(net["f_max"], (t + 1) * FH)
        dve.tensor_scalar(self.negm[:, t % 2, :], self.m[:, t % 2, :], -1.0, None, ALU.mult) \
           .then_inc(net["f_negmax"], 1)
        if t == 0:
            self.rows(dve, 0)

    def rows(self, dve, t):
        net = self.net
        dve.wait_ge(net["f_mT"], t + 1)
        if t >= 2:
            dve.wait_ge(net["f_mrows"], 16 * 4 * (t - 1))
        dve.tensor_copy(self.mrow[0:16, t % 2, :], self.obank(t)[0:16, 288:416]).then_inc(net["f_mcopied"], 1)

    def pool(self, pool, ch):
        for g in range(NG):
            self.net.norm_pool(pool, 4 * NG + g)

    def sync(self, sp):
        net = self.net
        sp.wait_ge(net["f_cum"], 2)
        sp.wait_ge(net["f_qk_copied"], 16)
        for s in range(4):
            sp.dma_start(self.k[8:128:32, s, :], self.fneg[4 * s:4 * s + 4, :]).then_inc(net["f_rows"], 16)
        sp.wait_ge(net["f_qk_copied"], 32)
        for t in range(NT):
            sp.wait_ge(net["f_mcopied"], t + 1)
            for s in range(4):
                sp.dma_start(self.q[9:128:32, s, t * P:(t + 1) * P], self.mrow[4 * s:4 * s + 4, t % 2, :]) \
                  .then_inc(net["f_mrows"], 16)


class SiluExperts:
    LAYER = 5

    def __init__(self, net):
        self.net = net
        w = net.mid
        w.at = 0
        self.wg, self.wu, self.wd = w.take(C2, P), w.take(C2, P), w.take(C2, P)
        self.wr = w.take(16)
        a = Arena(net.work)
        self.gates = Gates(net, a, 5, E2, 2, 1e-20, "g2")
        self.gates.sel = w.take(E2, P)
        self.s, self.h, self.hg = a.take(2, GW), a.take(3, GW), a.take(3, GW)

    def pe(self, pe):
        net, bank = self.net, self.net.bank
        xT = net.xT[1]
        net.layer_start(pe, 5)
        pe.wait_ge(net["w5_loaded"], 16 * 5)
        for g in range(NG):
            n = 5 * NG + g
            xg = xT[:, g * GW:(g + 1) * GW]
            self.gates.pe(pe, g, xT, self.wr[:, 0:E2], None)
            if g == 0:
                pass
            pe.wait_ge(net["g2_spread"], E2 * (g + 1))
            for c in range(C2 + 1):
                i = C2 * g + c
                if c < C2:
                    if i >= 2:
                        pe.wait_ge(net["e2_prod"], i - 1)
                    pe.matmul(bank[4 + 2 * (i % 2)], self.wg[:, c, :], xg, start=True, stop=True) \
                      .then_inc(net["e2_gate"], 1)
                    pe.matmul(bank[5 + 2 * (i % 2)], self.wu[:, c, :], xg, start=True, stop=True) \
                      .then_inc(net["e2_up"], 1)
                if c:
                    j = i - 1
                    if c == 1:
                        pe.wait_ge(net["y_ready"], n - 1)
                    if c - 1 < 2 * E2:
                        pe.wait_ge(net["e2_gated"], j + 1 - 2 * g)
                        src = self.hg[:, j % 3, :]
                    else:
                        pe.wait_ge(net["e2_prod"], j + 1)
                        src = self.h[:, j % 3, :]
                    mm = pe.matmul(bank[g % 2], self.wd[:, c - 1, :], src, start=(c == 1), stop=False)
                    mm.then_inc(net["e2_down"], 1)
            pe.matmul(bank[g % 2], net.zeros[0:1, 0:P], net.zeros[0:1, :], start=False, stop=True) \
              .then_inc(net["out_ready"], 1)
            net.norm_pe_back(pe, n)
            net.norm_pe_forth(pe, n)

    def act(self, act, ch):
        net = self.net
        net.layer_start(act, 5)
        act.wait_ge(net["g2_filled"], 1)
        for g in range(NG):
            self.gates.act(act, g)
            for c in range(C2):
                i = C2 * g + c
                act.wait_ge(net["e2_gate"], i + 1)
                if i >= 2:
                    act.wait_ge(net["e2_prod"], i - 1)
                act.activation(self.s[:, i % 2, :], net.bank[4 + 2 * (i % 2)], ACT.Silu).then_inc(net["e2_silu"], 1)
            net.norm_act(act, 5 * NG + g)

    def dve(self, dve, ch):
        net = self.net
        net.layer_start(dve, 5)
        self.gates.dve_fill(dve).then_inc(net["g2_filled"], 1)
        dve.wait_ge(net["g2_filled"], 1)
        for g in range(NG):
            self.gates.dve(dve, ch, g)
            for c in range(C2):
                i = C2 * g + c
                dve.wait_ge(net["e2_silu"], i + 1)
                dve.wait_ge(net["e2_up"], i + 1)
                if i >= 3:
                    dve.wait_ge(net["e2_down"], i - 2)
                dve.tensor_tensor(out=self.h[:, i % 3, :], in0=self.s[:, i % 2, :], in1=net.bank[5 + 2 * (i % 2)],
                                  op=ALU.mult).then_inc(net["e2_prod"], 1)
            net.norm_dve(dve, ch, 5 * NG + g)

    def pool(self, pool, ch):
        net = self.net
        net.layer_start(pool, 5)
        for g in range(NG):
            pool.wait_ge(net["g2_spread"], E2 * (g + 1))
            for c in range(2 * E2):
                i = C2 * g + c
                pool.wait_ge(net["e2_prod"], i + 1)
                if i >= 3:
                    pool.wait_ge(net["e2_down"], i - 2)
                pool.tensor_tensor(out=self.hg[:, i % 3, :], in0=self.h[:, i % 3, :],
                                   in1=self.gates.spread[:, c // 2, :], op=ALU.mult).then_inc(net["e2_gated"], 1)
            net.norm_pool(pool, 5 * NG + g)


class LinearAttention:
    LAYER = 6

    def __init__(self, net):
        self.net = net
        w = net.const
        self.w = w.take(3 * P)
        self.b = w.take(3 * P)
        self.wp = w.take(P)
        self.bp = w.take(1)
        self.blocks = w.take(P)
        a = Arena(net.work)
        self.qkv = a.take(NT, 3 * P)
        self.sq = a.take(2, 2 * P)
        self.norm = a.take(2, 2, 32)
        self.qT = a.take(TOK)
        self.kv = a.take(2, P)
        self.oT = a.take(2, GW)

    def pe(self, pe):
        net, bank = self.net, self.net.bank
        xT = net.xT[0]
        net.layer_start(pe, 6)
        pe.wait_ge(net["w6_loaded"], 16 * 5)
        for t in range(NT + 2):
            if t < NT:
                if t >= 2:
                    pe.wait_ge(net["u_copied"], t - 1)
                pe.matmul(bank[4 + t % 2][:, 0:3 * P], xT[:, t * P:(t + 1) * P], self.w, start=True, stop=False)
                pe.matmul(bank[4 + t % 2][:, 0:3 * P], net.ones[0:1, :], self.b[0:1, :], start=False, stop=True) \
                  .then_inc(net["u_qkv"], 1)
            u = t - 2
            if u >= 0:
                b = u // 8
                pe.wait_ge(net["u_unit"], u + 1)
                if u >= 1:
                    pe.wait_ge(net["u_qT_copied"], u)
                pe.transpose(bank[6][:, 0:P], self.qkv[:, u, 0:P], net.ident).then_inc(net["u_qT"], 1)
                mm = pe.matmul(bank[7 * (1 - b)][:, 0:P], self.qkv[:, u, P:2 * P], self.qkv[:, u, 2 * P:3 * P],
                               start=(u % 8 == 0), stop=(u % 8 == 7), skip_group_check=True)
                if u % 8 == 7:
                    mm.then_inc(net["u_kv"], 1)
        for g in range(NG):
            n = 6 * NG + g
            pe.wait_ge(net["u_masked"], 2)
            pe.wait_ge(net["u_qT_copied"], NT)
            if g >= 2:
                pe.wait_ge(net["u_oT_copied"], g - 1)
            pe.matmul(bank[4 + g % 2], self.kv[:, g // 2, :], self.qT[:, g * GW:(g + 1) * GW],
                      start=True, stop=True).then_inc(net["u_o"], 1)
            pe.wait_ge(net["u_oT_copied"], g + 1)
            pe.wait_ge(net["y_ready"], n - 1)
            pe.matmul(bank[g % 2], self.wp, self.oT[:, g % 2, :], start=True, stop=True).then_inc(net["out_ready"], 1)
            net.norm_pe_back(pe, n)
            net.norm_pe_forth(pe, n)

    def act(self, act, ch):
        net = self.net
        net.layer_start(act, 6)
        for t in range(NT):
            act.wait_ge(net["u_qkv"], t + 1)
            act.activation(self.qkv[:, t, :], net.bank[4 + t % 2][:, 0:3 * P], ACT.Copy).then_inc(net["u_copied"], 1)
            act.wait_ge(net["u_copied"], t + 1)
            if t >= 2:
                act.wait_ge(net["u_unit"], t - 1)
            act.activation(self.sq[:, t % 2, :], self.qkv[:, t, 0:2 * P], ACT.Square).then_inc(net["u_sq"], 1)
            if t >= 2:
                act.wait_ge(net["u_qT"], t - 1)
                act.activation(self.qT[:, (t - 2) * P:(t - 1) * P], net.bank[6][:, 0:P], ACT.Copy) \
                   .then_inc(net["u_qT_copied"], 1)
        for t in range(NT - 2, NT):
            act.wait_ge(net["u_qT"], t + 1)
            act.activation(self.qT[:, t * P:(t + 1) * P], net.bank[6][:, 0:P], ACT.Copy) \
               .then_inc(net["u_qT_copied"], 1)
        for g in range(NG):
            act.wait_ge(net["u_o"], g + 1)
            if g >= 2:
                act.wait_ge(net["out_ready"], 6 * NG + g - 1)
            act.activation(self.oT[:, g % 2, :], net.bank[4 + g % 2], ACT.Copy).then_inc(net["u_oT_copied"], 1)
            net.norm_act(act, 6 * NG + g)

    def dve(self, dve, ch):
        net = self.net
        net.layer_start(dve, 6)
        dve.wait_ge(net["w6_loaded"], 16 * 5)
        for t in range(NT):
            dve.wait_ge(net["u_sq"], t + 1)
            dve.reduce_sum(self.norm[:, 0, t % 2, :], self.sq[:, t % 2, :].rearrange("p (h d) -> p h d", d=FD),
                           AX.X).then_inc(net["u_sums"], 1)
            r = self.norm[:, 1, t % 2, :]
            dve.wait_ge(net["u_roots"], t + 1)
            ch.link(dve.tensor_scalar(r, r, 1e-12, None, ALU.max))
            ch.link(dve.reciprocal(r, r))
            qk = self.qkv[:, t, 0:2 * P].rearrange("p (h d) -> p h d", d=FD)
            dve.tensor_tensor(out=qk, in0=qk, in1=bc(r, 2, FD), op=ALU.mult).then_inc(net["u_unit"], 1)
        for b in range(2):
            dve.wait_ge(net["u_kv"], b + 1)
            dve.tensor_tensor(out=self.kv[:, b, :], in0=net.bank[7 * (1 - b)][:, 0:P], in1=self.blocks,
                              op=ALU.mult).then_inc(net["u_masked"], 1)
        for g in range(NG):
            net.norm_dve(dve, ch, 6 * NG + g, scalar=self.bp[:, 0:1])

    def pool(self, pool, ch):
        net = self.net
        for t in range(NT):
            pool.wait_ge(net["u_sums"], t + 1)
            pool.tensor_tensor(out=self.norm[:, 1, t % 2, :], in0=self.norm[:, 0, t % 2, :], in1=net.half,
                               op=ALU.pow).then_inc(net["u_roots"], 1)
        for g in range(NG):
            net.norm_pool(pool, 6 * NG + g)


class TaskVectors:
    LAYER = 7

    def __init__(self, net):
        self.net = net
        w = net.late
        w.at = 0
        self.tw1 = w.take(E3, GW)
        self.w1 = w.take(GW)
        self.w2 = w.take(GW)
        self.gw1 = w.take(P)
        self.gw2 = w.take(8)
        self.gb1, self.gb2 = w.take(1), w.take(8)
        self.b1, self.tb1 = w.take(C3), w.take(C3, E3)
        self.b2, self.tb2 = w.take(1), w.take(E3)
        w = net.mid
        w.at = 0
        self.tw2 = w.take(E3, GW)
        a = Arena(net.work)
        self.h = a.take(2, GW)
        self.hsum = a.take(NG)
        self.hb = a.take(2)
        self.hrep = a.take(2, P)
        self.g = a.take(2, 8)
        self.tmp = a.take(C3, E3)
        self.tmp2 = a.take(E3)
        self.m1, self.m2 = a.take(2, GW), a.take(2, GW)
        self.mb1, self.mb2 = a.take(2, C3), a.take(2)
        self.u = a.take(3, GW)

    def pe(self, pe):
        net, bank = self.net, self.net.bank
        xT = net.xT[1]
        net.layer_start(pe, 7)
        pe.wait_ge(net["w7_loaded"], 16 * 12)
        for g in range(NG):
            pe.matmul(bank[4 + g], self.gw1, xT[:, g * GW:(g + 1) * GW], start=True, stop=True) \
              .then_inc(net["t_gate_h"], 1)
        for b in range(2):
            pe.wait_ge(net["t_mean"], b + 1)
            if b == 0:
                pe.wait_ge(net["y_ready"], 7 * NG)
            pe.matmul(bank[b][:, 0:8], self.hrep[:, b, :], self.gw2, start=True, stop=True) \
              .then_inc(net["t_gate"], 1)
        for g in range(NG):
            n = 7 * NG + g
            b = g // 2
            pe.wait_ge(net["t_merged"], b + 1)
            for c in range(C3 + 1):
                i = C3 * g + c
                if c < C3:
                    if i >= 2:
                        pe.wait_ge(net["t_act"], i - 1)
                    pe.matmul(bank[4 + i % 2], self.m1[:, b, c * P:(c + 1) * P], xT[:, g * GW:(g + 1) * GW],
                              start=True, stop=True).then_inc(net["t_up"], 1)
                if c:
                    j = i - 1
                    pe.wait_ge(net["t_act"], j + 1)
                    if c == 1:
                        pe.wait_ge(net["y_ready"], n - 1)
                        pe.wait_ge(net["t_gated"], 2)
                    mm = pe.matmul(bank[g % 2], self.m2[:, b, (c - 1) * P:c * P], self.u[:, j % 3, :],
                                   start=(c == 1), stop=False)
                    mm.then_inc(net["t_down"], 1)
            pe.matmul(bank[g % 2], net.zeros[0:1, 0:P], net.zeros[0:1, :], start=False, stop=True) \
              .then_inc(net["out_ready"], 1)
            net.norm_pe_back(pe, n)

    def act(self, act, ch):
        net = self.net
        net.layer_start(act, 7)
        act.wait_ge(net["w7_loaded"], 16 * 12)
        for g in range(NG):
            act.wait_ge(net["t_gate_h"], g + 1)
            if g >= 2:
                act.wait_ge(net["t_relu"], g - 1)
            act.activation(self.h[:, g % 2, :], net.bank[4 + g], ACT.Relu, bias=self.gb1[:, 0:1],
                           accum_out=self.hsum[:, g:g + 1]).then_inc(net["t_relu"], 1)
        for g in range(NG):
            b = g // 2
            act.wait_ge(net["t_merged"], b + 1)
            for c in range(C3):
                i = C3 * g + c
                act.wait_ge(net["t_up"], i + 1)
                if i >= 3:
                    act.wait_ge(net["t_down"], i - 2)
                act.activation(self.u[:, i % 3, :], net.bank[4 + i % 2], ACT.Gelu_apprx_tanh,
                               bias=self.mb1[:, b, c:c + 1]).then_inc(net["t_act"], 1)

    def dve(self, dve, ch):
        net = self.net
        net.layer_start(dve, 7)
        dve.wait_ge(net["w7_loaded"], 16 * 12)
        for b in range(2):
            dve.wait_ge(net["t_relu"], 2 * b + 2)
            ch.link(dve.tensor_tensor(out=self.hb[:, b:b + 1], in0=self.hsum[:, 2 * b:2 * b + 1],
                                      in1=self.hsum[:, 2 * b + 1:2 * b + 2], op=ALU.add))
            ch.link(dve.memset(self.hrep[:, b, :], 1.0 / 1024))
            dve.tensor_scalar(self.hrep[:, b, :], self.hrep[:, b, :], self.hb[:, b:b + 1], None, ALU.mult) \
               .then_inc(net["t_mean"], 1)
        for b in range(2):
            g = self.g[:, b, :]
            dve.wait_ge(net["t_gate"], b + 1)
            dve.tensor_tensor(out=g, in0=net.bank[b][:, 0:8], in1=self.gb2, op=ALU.add) \
               .then_inc(net["t_gated"], 1)
            dve.wait_ge(net["t_gated"], b + 1)
            ch.link(dve.tensor_tensor(out=self.tmp, in0=self.tb1, in1=bc(g, 1, C3), op=ALU.mult))
            ch.link(dve.tensor_tensor(out=self.tmp2, in0=self.tb2, in1=g, op=ALU.mult))
            ch.link(dve.reduce_sum(self.mb1[:, b, :], self.tmp, AX.X))
            ch.link(dve.tensor_tensor(out=self.mb1[:, b, :], in0=self.mb1[:, b, :], in1=self.b1, op=ALU.add))
            ch.link(dve.reduce_sum(self.mb2[:, b:b + 1], self.tmp2, AX.X))
            ch.link(dve.tensor_tensor(out=self.mb2[:, b:b + 1], in0=self.mb2[:, b:b + 1], in1=self.b2, op=ALU.add))
            m1, m2 = self.m1[:, b, :], self.m2[:, b, :]
            for e in range(E3):
                dve.scalar_tensor_tensor(out=m1, in0=self.tw1[:, e, :], scalar=g[:, e:e + 1],
                                         in1=(m1 if e else self.w1), op0=ALU.mult, op1=ALU.add) \
                   .then_inc(net["t_merge1"], 1)
                if e:
                    dve.wait_ge(net["t_merge2"], b * E3 + e)
                ins = dve.scalar_tensor_tensor(out=m2, in0=self.tw2[:, e, :], scalar=g[:, e:e + 1],
                                               in1=(m2 if e else self.w2), op0=ALU.mult, op1=ALU.add)
                ins.then_inc(net["t_merge2"], 1)
                dve.wait_ge(net["t_merge1"], b * E3 + e + 1)
            dve.wait_ge(net["t_merge2"], (b + 1) * E3)
            dve.tensor_copy(self.tmp2, self.tmp2).then_inc(net["t_merged"], 1)
        for g in range(NG):
            n = 7 * NG + g
            net.norm_dve(dve, ch, n, scalar=self.mb2[:, g // 2:g // 2 + 1])

    def pool(self, pool, ch):
        for g in range(NG):
            self.net.norm_pool(pool, 7 * NG + g)


LAYERS = (QueryAttention, ProductKeys, Lightning, GeluExperts, Forgetting, SiluExperts, LinearAttention, TaskVectors)
CONST_COLS = 5400
LATE_COLS = 9120
MID_COLS = 8900
WORK_COLS = 22400


def build(nc, io, out):
    with ExitStack() as ctx:
        net = Net(nc, ctx, io)
        layers = [make(net) for make in LAYERS]
        query, keys, light, gelu, forget, silu, linear, tasks = layers
        block = ctx.enter_context(nc.Block())

        def load(eng, name, dst, src):
            eng.dma_start(dst, io[src]).then_inc(net[name], 16)

        @block.sync
        def _(sp):
            loads0 = [(net.xT[0][:], "xT"), (query.w, "a0_w"), (query.b, "a0_b"), (query.bv, "a0_bv"),
                      (query.mask, "a0_mask"), (net.ident, "ident"), (net.ones, "ones"),
                      (net.minus_half, "minus_half"), (net.half, "half")]
            loads1 = [(keys.wq, "p_wq"), (keys.wqT, "p_wqT"), (keys.keysT, "p_keysT"), (keys.down, "p_down"),
                      (keys.up, "p_up"), (keys.gamma, "p_gamma"), (keys.beta, "p_beta"), (keys.iota, "p_iota"),
                      (keys.coef_y, "p_coef"), (keys.invn, "p_invn")]
            loads4 = [(forget.wq, "f_wq"), (forget.wk, "f_wk"), (forget.wv, "f_wv"), (forget.wo, "f_wo"),
                      (forget.wf, "f_wf"), (forget.onerow, "f_onerow"), (forget.mask_n, "f_mask_n"),
                      (forget.mask_t, "a0_mask")]
            loads6 = [(linear.w, "u_w"), (linear.b[0:1, :], "u_b"), (linear.wp, "u_wp"), (linear.bp, "u_bp"),
                      (linear.blocks, "u_blocks")]
            loads2 = [(light.wq, "l_wq"), (light.wqr, "l_wqr"), (light.wk, "l_wk"), (light.wkr, "l_wkr"),
                      (light.wv, "l_wv"), (light.wo, "l_wo"), (light.cos, "l_cos"), (light.sin, "l_sin"),
                      (light.decay, "l_decay"), (light.qdec, "l_qdec"), (light.kdec, "l_kdec"),
                      (light.blk, "l_blk")]
            loads3 = [(gelu.w1, "e1_w1"), (gelu.w2, "e1_w2"), (gelu.b1, "e1_b1"),
                      (gelu.gw[:, 0:E1], "e1_gw"), (gelu.gb[0:1, 0:E1], "e1_gb"), (gelu.b2[0:16, :], "e1_b2"),
                      (gelu.gates.sel[0:16, :, :], "sel15")]
            loads5 = [(silu.wg, "e2_wg"), (silu.wu, "e2_wu"), (silu.wd, "e2_wd"), (silu.wr[:, 0:E2], "e2_wr"),
                      (silu.gates.sel[0:16, :, :], "sel8")]
            loads7 = [(tasks.tw1, "t_tw1"), (tasks.w1, "t_w1"), (tasks.w2, "t_w2"), (tasks.gw1, "t_gw1"),
                      (tasks.gw2, "t_gw2"), (tasks.gb1, "t_gb1"), (tasks.gb2, "t_gb2"), (tasks.b1, "t_b1"),
                      (tasks.tb1, "t_tb1"), (tasks.b2, "t_b2"), (tasks.tb2, "t_tb2")]
            for n, loads in ((0, loads0), (1, loads1), (4, loads4), (6, loads6)):
                for dst, src in loads:
                    load(sp, f"w{n}_loaded", dst, src)
            sp.wait_ge(net["out_ready"], 2 * NG)
            for dst, src in loads2:
                load(sp, "w2_loaded", dst, src)
            for dst, src in loads3[:-1]:
                load(sp, "w3_loaded", dst, src)
            sp.wait_ge(net["out_ready"], 3 * NG)
            load(sp, "w3_loaded", *loads3[-1])
            for dst, src in loads7:
                load(sp, "w7_loaded", dst, src)
            sp.wait_ge(net["xT_done"], 4 * NG)
            for dst, src in loads5:
                load(sp, "w5_loaded", dst, src)
            forget.sync(sp)
            sp.wait_ge(net["out_ready"], 6 * NG)
            load(sp, "w7_loaded", tasks.tw2, "t_tw2")
            for g in range(NG):
                sp.wait_ge(net["normed"], 7 * NG + g + 1)
                sp.dma_start(out[:, g * GT:(g + 1) * GT, :], net.x[:, g * GT:(g + 1) * GT, :]) \
                  .then_inc(net["stored"], 16)
            sp.wait_ge(net["stored"], 16 * NG)

        @block.tensor
        def _(pe):
            for layer in layers:
                layer.pe(pe)

        @block.scalar
        def _(act):
            ch = Chain(act, net["act_chain"])
            for layer in layers:
                layer.act(act, ch)

        @block.vector
        def _(dve):
            ch = Chain(dve, net["dve_chain"])
            for layer in layers:
                layer.dve(dve, ch)

        @block.gpsimd
        def _(pool):
            ch = Chain(pool, net["pool_chain"])
            for layer in layers:
                layer.pool(pool, ch)


def constants():
    f = np.float32
    i = np.arange(P)
    above = np.where(i[None, :] < i[:, None], f(NEG), f(0))
    slopes = np.array([2.0 ** (-8.0 / 16 * (h + 1)) for h in range(16)], f)
    t = np.arange(P, dtype=f)
    inv = 1.0 / 10000.0 ** (np.arange(0, HD, 2, dtype=np.float64) / HD)
    angle = np.concatenate([np.outer(np.arange(1024, dtype=np.float64), inv)] * 2, axis=-1).T
    sign = np.where(np.arange(HD) < HD // 2, -1.0, 1.0)[:, None]
    diff = t[None, :] - t[:, None]
    decay = np.where(diff[:, None, :] >= 0, np.exp(-slopes[None, :, None] * np.maximum(diff, 0)[:, None, :]), f(0))
    head = np.array([[4 * (2 * (c // 4) + half) + c % 4 for c in range(8)] for half in range(2)])
    rows = np.repeat(head, HD, axis=0)
    onerow = np.zeros((P, 2), f)
    onerow[8::32, 0] = 1
    onerow[9::32, 1] = 1
    sel = np.zeros((16, 15, P), f)
    for e in range(15):
        sel[e, e] = 1
    return {
        "minus_half": np.full((P, 16), -0.5, f), "half": np.full((P, 32), 0.5, f),
        "ident": np.eye(P, dtype=f), "ones": np.ones((P, P), f), "a0_mask": above.astype(f),
        "f_mask_n": np.ascontiguousarray(above.T).astype(f),
        "p_iota": np.broadcast_to(np.arange(PKEYS, dtype=f), (P, PKEYS)),
        "p_coef": np.broadcast_to(8 - np.arange(8, dtype=f), (P, 8, 8)),
        "p_invn": np.full((P, P), 1.0 / TOK, f),
        "l_cos": np.tile(np.cos(angle), (2, 1)).astype(f), "l_sin": np.tile(np.sin(angle) * sign, (2, 1)).astype(f),
        "l_decay": decay.astype(f),
        "l_qdec": np.exp(-slopes[rows][:, :, None] * (t + 1)[None, None, :]).astype(f),
        "l_kdec": np.exp(-slopes[None, :] * (P - 1 - t)[:, None]).astype(f),
        "l_blk": np.exp(-slopes[rows] * f(P)).astype(f),
        "f_onerow": onerow, "sel15": sel, "sel8": sel[:, 0:8],
        "u_blocks": np.kron(np.eye(16), np.ones((8, 8))).astype(f),
    }


def kernel(**inputs):
    import concourse.bacc as bacc
    from concourse.bass_utils import run_bass_kernel_spmd as run

    w = {k: np.asarray(v) for k, v in inputs.items()}

    def tiles(a, n):
        return a.reshape(n, P, -1).transpose(1, 0, 2)

    a0, pk, l1, e1 = "L0_attn_", "L0_ffn_", "L1_attn_", "L1_ffn_"
    f2, e2, u3, t3 = "L2_attn_", "L2_ffn_", "L3_attn_", "L3_ffn_"
    arr = dict(constants())
    arr["xT"] = w[a0 + "minibatch"].reshape(TOK, P).T
    arr["a0_w"] = np.stack([w[a0 + "Wq"], w[a0 + "Wk"], w[a0 + "Wv"]], axis=1)
    arr["a0_b"] = np.stack([w[a0 + "bq"], w[a0 + "bk"]], axis=1)
    arr["a0_bv"] = np.broadcast_to(w[a0 + "bv"], (P, P))

    wq = w[pk + "w_q"]
    arr["p_wq"] = wq
    arr["p_wqT"] = wq.reshape(P, PC, P).transpose(2, 1, 0)
    arr["p_keysT"] = w[pk + "keys"].transpose(3, 2, 0, 1).reshape(P, PC, PKEYS)
    arr["p_down"] = w[pk + "down_embed"].T
    arr["p_up"] = tiles(w[pk + "up_embed"], 8)
    arr["p_gamma"] = w[pk + "bn_gamma"].reshape(PC, P).T
    arr["p_beta"] = w[pk + "bn_beta"].reshape(PC, P).T

    swap = np.concatenate([np.arange(32, 64), np.arange(0, 32)])
    lq = w[l1 + "Wq"].reshape(2, 2, 4, HD, P)
    lk = w[l1 + "Wk"].reshape(2, 2, HD, P)

    def qside(a):
        return a.transpose(4, 0, 2, 1, 3).reshape(P, 8, P)

    def kside(a):
        return a.transpose(3, 0, 1, 2).reshape(P, 2, P)

    arr["l_wq"], arr["l_wqr"] = qside(lq), qside(lq[:, :, :, swap])
    arr["l_wk"], arr["l_wkr"] = kside(lk), kside(lk[:, :, swap])
    arr["l_wv"] = w[l1 + "Wv"].T
    arr["l_wo"] = w[l1 + "Wo"].reshape(P, 2, 2, 4, HD).transpose(2, 4, 1, 3, 0).reshape(P, 8, P)

    rw1 = w[e1 + "rW1"].transpose(1, 0, 2).reshape(P, E1 * 2 * P)
    arr["e1_w1"] = np.concatenate([w[e1 + "sW1"][0], rw1], axis=1)
    arr["e1_w2"] = tiles(np.concatenate([w[e1 + "sW2"][0], w[e1 + "rW2"].reshape(-1, P)], axis=0), C1)
    arr["e1_b1"] = np.concatenate([w[e1 + "sb1"].reshape(-1), w[e1 + "rb1"].reshape(-1)]).reshape(C1, P).T
    arr["e1_b2"] = np.concatenate([w[e1 + "rb2"], w[e1 + "sb2"]], axis=0)
    arr["e1_gw"], arr["e1_gb"] = w[e1 + "gW"], w[e1 + "gb"].reshape(1, E1)

    def slots(a):
        out = np.zeros((P, 4, 4, 32), a.dtype)
        out[:, :, :, 0:FD] = a.reshape(P, 4, 4, FD)
        return out.reshape(P, 4, P)

    arr["f_wq"], arr["f_wk"] = slots(w[f2 + "Wq"]), slots(w[f2 + "Wk"])
    arr["f_wv"], arr["f_wo"], arr["f_wf"] = w[f2 + "Wv"], w[f2 + "Wo"], w[f2 + "Wf"]

    def experts(routed, shared):
        return np.concatenate([routed.transpose(1, 0, 2).reshape(P, -1), shared], axis=1)

    arr["e2_wg"] = experts(w[e2 + "Wg"], w[e2 + "Sg"])
    arr["e2_wu"] = experts(w[e2 + "Wu"], w[e2 + "Su"])
    arr["e2_wd"] = tiles(np.concatenate([w[e2 + "Wd"].reshape(-1, P), w[e2 + "Sd"]], axis=0), C2)
    arr["e2_wr"] = w[e2 + "Wr"]

    arr["u_w"], arr["u_b"] = w[u3 + "qkv_w"], w[u3 + "qkv_b"].reshape(1, 3 * P)
    arr["u_wp"], arr["u_bp"] = w[u3 + "proj_w"], w[u3 + "proj_b"].reshape(P, 1)

    arr["t_tw1"] = w[t3 + "TW1"].transpose(2, 0, 1)
    arr["t_w1"] = w[t3 + "W1"].T
    arr["t_w2"] = w[t3 + "W2"].T.reshape(C3, P, P).transpose(1, 0, 2)
    arr["t_tw2"] = w[t3 + "TW2"].transpose(2, 0, 1).reshape(C3, P, E3, P).transpose(1, 2, 0, 3)
    arr["t_gw1"], arr["t_gw2"] = w[t3 + "gate_w1"].T, w[t3 + "gate_w2"].T
    arr["t_gb1"] = w[t3 + "gate_b1"].reshape(P, 1)
    arr["t_gb2"] = np.broadcast_to(w[t3 + "gate_b2"], (P, E3))
    arr["t_b1"] = w[t3 + "b1"].reshape(C3, P).T
    arr["t_tb1"] = w[t3 + "Tb1"].reshape(E3, C3, P).transpose(2, 1, 0)
    arr["t_b2"] = w[t3 + "b2"].reshape(P, 1)
    arr["t_tb2"] = w[t3 + "Tb2"].T

    shaped = {
        "e1_w1": (P, C1, P), "e2_wg": (P, C2, P), "e2_wu": (P, C2, P), "t_w2": (P, GW), "t_tw2": (P, E3, GW)}
    nc = bacc.Bacc("TRN2", target_bir_lowering=False, num_devices=1)
    arrays, io = {}, {}
    for name, a in arr.items():
        a = np.ascontiguousarray(a.reshape(shaped.get(name, a.shape)))
        arrays[f"in_{name}"] = a
        io[name] = nc.dram_tensor(f"in_{name}", a.shape, mybir.dt.from_np(a.dtype), kind="ExternalInput").ap()
    out = nc.dram_tensor("out_x", (P, NT, P), F32, kind="ExternalOutput").ap()
    build(nc, io, out)
    r = run(nc, [arrays], core_ids=[0])
    return r.results[0]["out_x"].transpose(1, 0, 2).reshape(2, 1024, P)
```

```python
from contextlib import ExitStack

import numpy as np

import concourse.bass as bass
from concourse import mybir

F32 = mybir.dt.float32
BF16 = mybir.dt.bfloat16
U32 = mybir.dt.uint32
ALU = mybir.AluOpType
ACT = mybir.ActivationFunctionType
AX = mybir.AxisListType

P = 128
NT = 16
NG = 4
GT = 4
GW = 512
TOK = 2048
LN_EPS = 1e-5
NEG = -1.0e30

PH, PKEYS, PTOP = 8, 32, 8
PC = 2 * PH
NKV, HD = 4, 64
FH, FD = 16, 8
E1, C1S, C1 = 15, 4, 34
E2, C2 = 8, 18
E3, C3 = 8, 4


class Arena:

    def __init__(self, tensor):
        self.tensor, self.at = tensor, 0

    def take(self, *shape):
        n = int(np.prod(shape))
        ap = self.tensor[:, self.at:self.at + n]
        self.at += n
        assert self.at <= self.tensor.shape[1], (self.at, self.tensor.shape)
        if len(shape) == 2:
            ap = ap.rearrange("p (a b) -> p a b", a=shape[0])
        if len(shape) == 3:
            ap = ap.rearrange("p (a b c) -> p a b c", a=shape[0], b=shape[1])
        return ap


class Chain:

    def __init__(self, engine, semaphore):
        self.engine, self.semaphore, self.count = engine, semaphore, 0

    def link(self, ins):
        self.count += 1
        ins.then_inc(self.semaphore, 1)
        self.engine.wait_ge(self.semaphore, self.count)


def bc(ap, axis, n):
    a = ap.unsqueeze(axis)
    shape = list(a.shape)
    shape[axis] = n
    return a.broadcast_to(shape)


def flat(ap):
    return ap.rearrange("p a b -> p (a b)")


class Net:

    def __init__(self, nc, ctx, io):
        self.nc, self.ctx, self.io = nc, ctx, io
        self.signals = {}

        def sb(name, n):
            return ctx.enter_context(nc.sbuf_tensor(name, [P, n], F32))

        self.pairs = [ctx.enter_context(nc.psum_tensor(f"banks{2 * i}{2 * i + 1}", [P, 2 * GW], F32))
                      for i in range(4)]
        self.bank = [self.pairs[i // 2][:, (i % 2) * GW:(i % 2 + 1) * GW] for i in range(8)]
        self.xT = [sb("xT0", TOK), sb("xT1", TOK)]
        self.x = sb("x_tokens", TOK)[:, :].rearrange("p (t d) -> p t d", t=NT)
        self.yT = sb("yT", GW)
        self.stats = sb("stats", GT * 6)[:, :].rearrange("p (a b) -> p a b", a=GT)
        self.moments = sb("moments", GT * 2)[:, :].rearrange("p (a b) -> p a b", a=GT)
        self.rstd, self.var = sb("rstd", GT), sb("variance_eps", GT)
        self.const = Arena(sb("constants", CONST_COLS))
        self.late = Arena(sb("late_weights", LATE_COLS))
        self.mid = Arena(sb("expert_weights", MID_COLS))
        self.work = sb("work", WORK_COLS)
        self.ident = self.const.take(P)
        self.ones = self.const.take(P)
        self.zeros = ctx.enter_context(nc.sbuf_tensor("zeros", [1, GW], BF16))
        self.minus_half, self.half = self.const.take(16), self.const.take(32)
        self.minus_half4 = self.minus_half[:, 0:GT]

    def __getitem__(self, name):
        if name not in self.signals:
            self.signals[name] = self.ctx.enter_context(self.nc.semaphore(name))
        return self.signals[name]

    def bias(self, layer, g):
        return None

    def norm_pe_back(self, pe, n):
        pe.wait_ge(self["y_ready"], n + 1)
        if n:
            pe.wait_ge(self["normed"], n)
        for k in range(GT):
            mm = pe.transpose(self.bank[2][:, k * P:(k + 1) * P], self.yT[:, k * P:(k + 1) * P], self.ident)
        mm.then_inc(self["y_tokens"], 1)

    def norm_pe_forth(self, pe, n):
        g = n % NG
        pe.wait_ge(self["normed"], n + 1)
        if n:
            pe.wait_ge(self["xT_done"], n)
        for k in range(GT):
            mm = pe.transpose(self.bank[3][:, k * P:(k + 1) * P], self.x[:, g * GT + k, :], self.ident)
        mm.then_inc(self["xT_in_psum"], 1)

    def norm_act(self, act, n):
        g = n % NG
        act.wait_ge(self["xT_in_psum"], n + 1)
        act.activation(self.xT[(n // NG + 1) % 2][:, g * GW:(g + 1) * GW], self.bank[3], ACT.Copy) \
           .then_inc(self["xT_done"], 1)

    def norm_dve(self, dve, ch, n, scalar=0.0, op=ALU.add, twice=False, bank=None):
        g = n % NG
        xT = self.xT[(n // NG) % 2][:, g * GW:(g + 1) * GW]
        out = self.bank[g % 2 if bank is None else bank]
        dve.wait_ge(self["out_ready"], n + 1)
        if twice:
            ins = dve.scalar_tensor_tensor(out=self.yT[:], in0=xT, scalar=2.0, in1=out, op0=ALU.mult, op1=ALU.add)
        else:
            ins = dve.scalar_tensor_tensor(out=self.yT[:], in0=out, scalar=scalar, in1=xT, op0=op, op1=ALU.add)
        ins.then_inc(self["y_ready"], 1)
        dve.wait_ge(self["y_tokens"], n + 1)
        for k in range(GT):
            ins = dve.bn_stats(self.stats[:, k, :], self.bank[2][:, k * P:(k + 1) * P])
        ch.link(ins)
        for k in range(GT):
            ins = dve.bn_aggr(self.moments[:, k, :], self.stats[:, k, :])
        ch.link(ins)
        dve.tensor_scalar(self.var[:], self.moments[:, :, 1], LN_EPS, None, ALU.add).then_inc(self["variance"], 1)
        dve.wait_ge(self["rstd_done"], n + 1)
        for k in range(GT):
            ins = dve.tensor_scalar(self.x[:, g * GT + k, :], self.bank[2][:, k * P:(k + 1) * P],
                                    self.moments[:, k, 0:1], self.rstd[:, k:k + 1], ALU.subtract, ALU.mult)
        ins.then_inc(self["normed"], 1)

    def norm_pool(self, pool, n):
        pool.wait_ge(self["variance"], n + 1)
        pool.tensor_tensor(out=self.rstd[:], in0=self.var[:], in1=self.minus_half4, op=ALU.pow) \
            .then_inc(self["rstd_done"], 1)

    def layer_start(self, eng, layer):
        if layer:
            eng.wait_ge(self["xT_done"], NG * layer)


class QueryAttention:
    LAYER = 0

    def __init__(self, net):
        self.net = net
        a = Arena(net.work)
        self.qT, self.kT = a.take(TOK), a.take(TOK)
        self.v = a.take(NT, P)
        self.exp = a.take(2, 1024)
        self.v_scaled = a.take(2, P)
        self.negmax = a.take(2 * NT)
        self.total = a.take(2 * NT)
        w = net.const
        self.w = net.late.take(3, P) if False else a.take(3, P)
        self.b = a.take(2)
        self.bv = a.take(P)
        self.mask = net.mask = w.take(P)

    def pv_wait(self, eng, n):
        if n % 8 == 7:
            eng.wait_ge(self.net["out_ready"], 2 * (n // 8) + 2)
        else:
            eng.wait_ge(self.net["a0_pv_done"], n + 1 - n // 8)

    def pe(self, pe):
        net, bank = self.net, self.net.bank
        xT = net.xT[0]
        pe.wait_ge(net["w0_loaded"], 16 * 9)
        for i in range(2 * NG):
            if i >= 2:
                pe.wait_ge(net["a0_qk_copied"], i - 1)
            pe.matmul(bank[4 + i % 2], self.w[:, i // NG, :], xT[:, (i % NG) * GW:(i % NG + 1) * GW],
                      start=True, stop=True).then_inc(net["a0_qk_psum"], 1)
        for g in range(NG):
            if g >= 2:
                pe.wait_ge(net["a0_v_copied"], g - 1)
            for k in range(GT):
                t = g * GT + k
                mm = pe.matmul(bank[6 + g % 2][:, k * P:(k + 1) * P], xT[:, t * P:(t + 1) * P],
                               self.w[:, 2, :], start=True, stop=True)
            mm.then_inc(net["a0_v_psum"], 1)
        pe.wait_ge(net["a0_qk_copied"], 2 * NG)
        pe.wait_ge(net["a0_v_copied"], NG)

        def scores(n):
            b, j = divmod(n, 8)
            if n >= 2:
                pe.wait_ge(net["a0_exp_done"], n - 1)
            for half in range(j // 4, 2):
                lo = max(P * j, GW * half)
                mm = pe.matmul(net.pairs[2 + n % 2][:, lo:GW * (half + 1)],
                               self.kT[:, n * P:(n + 1) * P],
                               self.qT[:, 1024 * b + lo:1024 * b + GW * (half + 1)], start=True, stop=True)
            mm.then_inc(net["a0_scores"], 1)

        def values(n):
            b, j = divmod(n, 8)
            pe.wait_ge(net["a0_v_scaled"], n + 1)
            for half in range(j // 4, 2):
                if j == 0 and b:
                    pe.wait_ge(net["y_ready"], half + 1)
                lo = max(P * j, GW * half)
                mm = pe.matmul(bank[half][:, lo - GW * half:GW], self.v_scaled[:, n % 2, :],
                               self.exp[:, n % 2, lo:GW * (half + 1)], start=(j == 0), stop=(j == 3 + 4 * half))
                if j == 3 + 4 * half:
                    mm.then_inc(net["out_ready"], 1)
            if j != 7:
                mm.then_inc(net["a0_pv_done"], 1)

        scores(0)
        for n in range(NT):
            if n + 1 < NT:
                scores(n + 1)
            values(n)
            if n % 8 == 7:
                for g in (n // 8 * 2, n // 8 * 2 + 1):
                    net.norm_pe_back(pe, g)
                    net.norm_pe_forth(pe, g)

    def act(self, act, ch):
        net = self.net
        act.wait_ge(net["w0_loaded"], 16 * 9)
        for i in range(2 * NG):
            act.wait_ge(net["a0_qk_psum"], i + 1)
            dst = (self.qT, self.kT)[i // NG][:, (i % NG) * GW:(i % NG + 1) * GW]
            act.activation(dst, net.bank[4 + i % 2], ACT.Identity, bias=self.b[:, i // NG:i // NG + 1]) \
               .then_inc(net["a0_qk_copied"], 1)
        for n in range(NT):
            j = n % 8
            act.wait_ge(net["a0_negmax"], n + 1)
            if n >= 2:
                self.pv_wait(act, n - 2)
            act.activation(self.exp[:, n % 2, P * j:1024], net.pairs[2 + n % 2][:, P * j:1024], ACT.Exp,
                           bias=self.negmax[:, n:n + 1], accum_out=self.total[:, n:n + 1]) \
               .then_inc(net["a0_exp_done"], 1)
            if n % 8 == 7:
                net.norm_act(act, n // 8 * 2)
                net.norm_act(act, n // 8 * 2 + 1)

    def dve(self, dve, ch):
        net = self.net
        dve.wait_ge(net["w0_loaded"], 16 * 9)
        for g in range(NG):
            dve.wait_ge(net["a0_v_psum"], g + 1)
            dve.tensor_tensor(out=self.v[:, g * GT:(g + 1) * GT, :],
                              in0=net.bank[6 + g % 2].rearrange("p (t d) -> p t d", t=GT),
                              in1=bc(self.bv, 1, GT), op=ALU.add).then_inc(net["a0_v_copied"], 1)

        def maxima(n):
            j = n % 8
            s = net.pairs[2 + n % 2]
            dve.wait_ge(net["a0_scores"], n + 1)
            ch.link(dve.tensor_tensor(out=s[:, P * j:P * j + P], in0=s[:, P * j:P * j + P], in1=self.mask,
                                      op=ALU.add))
            ch.link(dve.reduce_max(self.negmax[:, NT + n:NT + n + 1], s[:, P * j:1024], AX.X))
            dve.tensor_scalar(self.negmax[:, n:n + 1], self.negmax[:, NT + n:NT + n + 1], -1.0, None,
                              ALU.mult).then_inc(net["a0_negmax"], 1)

        maxima(0)
        for n in range(NT):
            if n + 1 < NT:
                maxima(n + 1)
            dve.wait_ge(net["a0_exp_done"], n + 1)
            ch.link(dve.tensor_scalar(self.total[:, NT + n:NT + n + 1], self.total[:, n:n + 1],
                                      float(np.float32(np.sqrt(128.0))), None, ALU.mult))
            ch.link(dve.reciprocal(self.total[:, NT + n:NT + n + 1], self.total[:, NT + n:NT + n + 1]))
            if n >= 2:
                self.pv_wait(dve, n - 2)
            dve.tensor_scalar(self.v_scaled[:, n % 2, :], self.v[:, n, :], self.total[:, NT + n:NT + n + 1],
                              None, ALU.mult).then_inc(net["a0_v_scaled"], 1)
            if n % 8 == 7:
                net.norm_dve(dve, ch, n // 8 * 2, twice=True)
                net.norm_dve(dve, ch, n // 8 * 2 + 1, twice=True)

    def pool(self, pool, ch):
        pool.memset(self.net.zeros[:], 0.0).then_inc(self.net["zeroed"], 1)
        pool.wait_ge(self.net["w0_loaded"], 16 * 9)
        for g in range(NG):
            self.net.norm_pool(pool, g)


class ProductKeys:
    LAYER = 1

    def __init__(self, net):
        self.net = net
        w = net.late
        w.at = 0
        self.wq = w.take(TOK)
        self.wqT = w.take(PC, P)
        self.keysT = w.take(PC, PKEYS)
        self.down = w.take(1024)
        self.up = w.take(8, P)
        self.gamma, self.beta = w.take(PC), w.take(PC)
        self.iota = net.const.take(PKEYS)
        self.coef_y = net.const.take(PC // 2, PTOP)
        self.invn = net.const.take(P)
        a = Arena(net.work)
        self.xc, self.xcT = a.take(NT, P), a.take(TOK)
        self.z = self.xc
        self.cov = a.take(P)
        self.meancol = a.take(2)
        self.scale = a.take(2, PC)
        self.ks = a.take(PC, PKEYS)
        self.m = a.take(512)
        self.brow = a.take(512)
        self.sim = a.take(2, PC * PKEYS)
        self.top = a.take(PC, PTOP)
        self.idx = a.take(PC * PTOP).bitcast(U32)
        self.idxf = a.take(PC * PTOP)
        self.coef = a.take(PC, PTOP)
        self.sums, self.left, self.chosen, self.prob = (a.take(PH, PTOP, PTOP) for _ in range(4))
        self.best = a.take(PH, PTOP)
        self.d8, self.e8 = a.take(PC, PTOP), a.take(PC, PTOP)
        self.z8, self.rz8 = a.take(PH), a.take(PH)
        self.dd, self.ed = a.take(PC, PKEYS), a.take(2, PC * PKEYS)
        self.fx = a.take(2, PH * PKEYS)
        self.onehot = a.take(PC * PTOP, PKEYS)
        self.nq = a.take(2, PC * PKEYS)
        self.expo = self.xc.rearrange("p (a t) d -> p a (t d)", a=2)
        self.rank, self.wgt = a.take(2, 1024), a.take(2, 1024)
        m = net.mid
        m.at = 0
        self.gelu, self.gw = m.take(8, GW), m.take(8, GW)

    def pe(self, pe):
        net, bank, x = self.net, self.net.bank, self.net.x
        xT = net.xT[1]
        net.layer_start(pe, 1)
        pe.wait_ge(net["w1_loaded"], 16 * 10)
        pe.wait_ge(net["zeroed"], 1)
        for t in range(NT):
            mm = pe.matmul(bank[4][:, 0:P], self.invn, x[:, t, :], start=(t == 0), stop=(t == NT - 1))
        mm.then_inc(net["p_mean"], 1)
        pe.wait_ge(net["p_centred"], 1)
        for t in range(NT):
            mm = pe.matmul(bank[5][:, 0:P], self.xc[:, t, :], self.xc[:, t, :], start=(t == 0), stop=(t == NT - 1))
        mm.then_inc(net["p_cov"], 1)
        pe.wait_ge(net["p_cov_scaled"], 1)
        for i in range(4):
            mm = pe.matmul(bank[4 + i], self.cov, self.wq[:, i * GW:(i + 1) * GW], start=True, stop=True)
            mm.then_inc(net["p_cw"], 1)
        pe.wait_ge(net["p_z"], 4)
        z = self.z.rearrange("p a b -> p (a b)")
        for c in range(PC):
            mm = pe.matmul(bank[0][:, c:c + 1], z[:, c * P:(c + 1) * P], net.ones[:, 0:1], start=True, stop=True)
        mm.then_inc(net["p_var"], 1)
        for c in range(PC):
            mm = pe.matmul(bank[3][0:1, c * PKEYS:(c + 1) * PKEYS], self.beta[:, c:c + 1], self.keysT[:, c, :],
                           start=True, stop=True)
        mm.then_inc(net["p_beta"], 1)
        pe.wait_ge(net["p_keys_scaled"], 1)
        for c in range(PC):
            mm = pe.matmul(bank[1][:, c * PKEYS:(c + 1) * PKEYS], self.wqT[:, c, :], self.ks[:, c, :],
                           start=True, stop=True)
        mm.then_inc(net["p_m"], 1)
        pe.wait_ge(net["p_m_copied"], 2)

        for g in range(NG):
            n = NG + g
            for c in range(8):
                if g or c:
                    pe.wait_ge(net["p_gelu"], 8 * g + c)
                pe.matmul(bank[4], self.down[:, c * P:(c + 1) * P], xT[:, g * GW:(g + 1) * GW],
                          start=True, stop=True).then_inc(net["p_h"], 1)
            for k in range(GT):
                t = g * GT + k
                if t:
                    pe.wait_ge(net["p_sim_copied"], t)
                pe.matmul(bank[5], self.xcT[:, t * P:(t + 1) * P], self.m, start=True, stop=False)
                pe.matmul(bank[5], net.ones[0:1, :], self.brow[0:1, :], start=False, stop=True) \
                  .then_inc(net["p_sim"], 1)
                for h in range(PH):
                    pe.wait_ge(net["p_weights"], t * PH + h + 1)
                    if h == 0 and t:
                        pe.wait_ge(net["p_gw"], t)
                    if h == 0:
                        for half in range(2):
                            pe.matmul(bank[6 + half], net.zeros[0:1, 0:P], net.zeros[0:1, :], start=True, stop=False)
                    for c in range(8):
                        mm = pe.matmul(net.pairs[3][:, c * P:(c + 1) * P], self.wgt[:, h % 2, c * P:(c + 1) * P],
                                       net.ident, start=False, stop=False,
                                       skip_group_check=True)
                    if h == PH - 1:
                        for half in range(2):
                            mm = pe.matmul(bank[6 + half], net.zeros[0:1, 0:P], net.zeros[0:1, :],
                                           start=False, stop=True)
                    mm.then_inc(net["p_summed"], 1)
            pe.wait_ge(net["p_gw"], GT * (g + 1))
            if g >= 2:
                pe.wait_ge(net["y_ready"], n - 1)
            for c in range(8):
                mm = pe.matmul(bank[g % 2], self.up[:, c, :], self.gw[:, c, :], start=(c == 0), stop=(c == 7))
            mm.then_inc(net["out_ready"], 1)
            net.norm_pe_back(pe, n)
            net.norm_pe_forth(pe, n)

    def act(self, act, ch):
        net = self.net
        net.layer_start(act, 1)
        act.wait_ge(net["p_m"], 1)
        act.activation(self.m, net.bank[1], ACT.Copy).then_inc(net["p_m_copied"], 1)
        act.wait_ge(net["p_beta"], 1)
        act.activation(self.brow[0:1, :], net.bank[3][0:1, :], ACT.Copy).then_inc(net["p_m_copied"], 1)
        for g in range(NG):
            if g:
                act.wait_ge(net["p_gw"], GT * g)
            for c in range(8):
                act.wait_ge(net["p_h"], 8 * g + c + 1)
                act.activation(self.gelu[:, c, :], net.bank[4], ACT.Gelu_apprx_tanh).then_inc(net["p_gelu"], 1)
            for k in range(GT):
                t = g * GT + k
                act.wait_ge(net["p_sim"], t + 1)
                if t >= 2:
                    act.wait_ge(net["p_weights"], PH * (t - 1))
                act.activation(self.sim[:, t % 2, :], net.bank[5], ACT.Copy).then_inc(net["p_sim_copied"], 1)
                act.wait_ge(net["p_diffs"], t + 1)
                act.activation(flat(self.e8), flat(self.d8), ACT.Exp).then_inc(net["p_e8"], 1)
                act.activation(self.ed[:, t % 2, :], flat(self.dd), ACT.Exp).then_inc(net["p_ed"], 1)
            net.norm_act(act, NG + g)

    def dve(self, dve, ch):
        net, x = self.net, self.net.x
        net.layer_start(dve, 1)
        dve.wait_ge(net["w1_loaded"], 16 * 10)
        dve.wait_ge(net["p_mean"], 1)
        ch.link(dve.tensor_tensor(out=self.xc, in0=x, in1=bc(net.bank[4][:, 0:P], 1, NT), op=ALU.subtract))
        ch.link(dve.reduce_sum(self.meancol[:, 0:1], net.xT[1][:], AX.X))
        ch.link(dve.tensor_scalar(self.meancol[:, 1:2], self.meancol[:, 0:1], 1.0 / TOK, None, ALU.mult))
        dve.tensor_scalar(self.xcT, net.xT[1][:], self.meancol[:, 1:2], None, ALU.subtract) \
           .then_inc(net["p_centred"], 1)
        dve.wait_ge(net["p_cov"], 1)
        dve.tensor_scalar(self.cov, net.bank[5][:, 0:P], 1.0 / TOK, None, ALU.mult).then_inc(net["p_cov_scaled"], 1)
        z = self.z.rearrange("p a b -> p (a b)")
        for i in range(4):
            dve.wait_ge(net["p_cw"], i + 1)
            dve.tensor_tensor(out=z[:, i * GW:(i + 1) * GW], in0=net.bank[4 + i], in1=self.wq[:, i * GW:(i + 1) * GW],
                              op=ALU.mult).then_inc(net["p_z"], 1)
        dve.wait_ge(net["p_var"], 1)
        dve.tensor_scalar(self.scale[:, 0, :], net.bank[0][:, 0:PC], 0.0, 1e-5, ALU.max, ALU.add) \
           .then_inc(net["p_varsum"], 1)
        dve.wait_ge(net["p_rstd"], 1)
        ch.link(dve.tensor_tensor(out=self.scale[:, 1, :], in0=self.scale[:, 1, :], in1=self.gamma, op=ALU.mult))
        dve.tensor_tensor(out=self.ks, in0=self.keysT, in1=bc(self.scale[:, 1, :], 2, PKEYS), op=ALU.mult) \
           .then_inc(net["p_keys_scaled"], 1)
        dve.tensor_copy(self.coef[:, PH:PC, :], self.coef_y)

        for g in range(NG):
            for k in range(GT):
                t = g * GT + k
                self.route(dve, ch, t)
                for h in range(PH):
                    i = t * PH + h
                    dve.wait_ge(net["p_pairs"], i + 1)
                    if i >= 2:
                        dve.wait_ge(net["p_summed"], i - 1)
                    dve.scalar_tensor_tensor(out=self.wgt[:, h % 2, :], in0=self.rank[:, h % 2, :], scalar=8.0,
                                             in1=self.expo[:, h % 2, :], op0=ALU.is_gt, op1=ALU.mult) \
                       .then_inc(net["p_weights"], 1)
                dve.wait_ge(net["p_summed"], PH * (t + 1))
                if k == 0:
                    dve.wait_ge(net["p_gelu"], 8 * (g + 1))
                    if g:
                        dve.wait_ge(net["out_ready"], NG + g)
                dve.tensor_tensor(out=self.gw[:, :, k * P:(k + 1) * P],
                                  in0=net.pairs[3][:, :].rearrange("p (c t) -> p c t", c=8),
                                  in1=self.gelu[:, :, k * P:(k + 1) * P], op=ALU.mult).then_inc(net["p_gw"], 1)
            net.norm_dve(dve, ch, NG + g)

    def route(self, dve, ch, t):
        net = self.net
        sim = self.sim[:, t % 2, :].rearrange("p (c v) -> p c v", c=PC)
        dve.wait_ge(net["p_sim_copied"], t + 1)
        for c in range(PC):
            ins = dve.max(self.top[:, c, :], sim[:, c, :])
        ch.link(ins)
        dve.tensor_tensor(out=self.d8, in0=self.top, in1=self.top[:, :, 0:1].broadcast_to([P, PC, PTOP]),
                          op=ALU.subtract)
        dve.tensor_tensor(out=self.dd, in0=sim, in1=self.top[:, :, 0:1].broadcast_to([P, PC, PKEYS]),
                          op=ALU.subtract).then_inc(net["p_diffs"], 1)
        for c in range(PC):
            ins = dve.max_index(self.idx[:, c * PTOP:(c + 1) * PTOP], self.top[:, c, :], sim[:, c, :])
        ch.link(dve.tensor_tensor(out=self.sums, in0=bc(self.top[:, 0:PH, :], 3, PTOP),
                                  in1=bc(self.top[:, PH:PC, :], 2, PTOP), op=ALU.add))
        dve.tensor_copy(self.idxf, self.idx)
        for h in range(PH):
            ins = dve.max(self.best[:, h, :], self.sums[:, h, :, :].rearrange("p i j -> p (i j)"))
        ch.link(ins)
        for h in range(PH):
            ins = dve.match_replace(self.left[:, h, :, :].rearrange("p i j -> p (i j)"), self.best[:, h, :],
                                    self.sums[:, h, :, :].rearrange("p i j -> p (i j)"), NEG)
        ch.link(ins)

        def f(ap):
            return ap.rearrange("p h i j -> p (h i j)")

        ch.link(dve.tensor_tensor(out=f(self.chosen), in0=f(self.sums), in1=f(self.left), op=ALU.not_equal))
        dve.tensor_reduce(self.coef[:, 0:PH, :], self.chosen, AX.X, ALU.add)
        dve.wait_ge(net["p_e8"], t + 1)
        ch.link(dve.tensor_tensor(out=self.prob, in0=bc(self.e8[:, 0:PH, :], 3, PTOP),
                                  in1=bc(self.e8[:, PH:PC, :], 2, PTOP), op=ALU.mult))
        ch.link(dve.tensor_tensor(out=f(self.prob), in0=f(self.prob), in1=f(self.chosen), op=ALU.mult))
        ch.link(dve.tensor_reduce(self.z8, self.prob.rearrange("p h i j -> p h (i j)"), AX.X, ALU.add))
        ch.link(dve.reciprocal(self.rz8, self.z8))
        dve.wait_ge(net["p_ed"], t + 1)
        ed = self.ed[:, t % 2, :].rearrange("p (c v) -> p c v", c=PC)
        dve.tensor_tensor(out=self.fx[:, t % 2, :].rearrange("p (h v) -> p h v", h=PH), in0=ed[:, 0:PH, :],
                          in1=bc(self.rz8, 2, PKEYS), op=ALU.mult)
        ch.link(dve.tensor_tensor(out=self.onehot, in0=bc(self.iota, 1, PC * PTOP), in1=bc(self.idxf, 2, PKEYS),
                                  op=ALU.is_equal))
        ch.link(dve.tensor_tensor(out=self.onehot, in0=self.onehot, in1=bc(flat(self.coef), 2, PKEYS),
                                  op=ALU.mult))
        dve.tensor_reduce(self.nq[:, t % 2, :].rearrange("p (c v) -> p c v", c=PC),
                          self.onehot.rearrange("p (c j) v -> p c v j", c=PC), AX.X, ALU.add) \
           .then_inc(net["p_routed"], 1)

    def pool(self, pool, ch):
        net = self.net
        pool.wait_ge(net["p_varsum"], 1)
        pool.tensor_tensor(out=self.scale[:, 1, :], in0=self.scale[:, 0, :], in1=net.minus_half, op=ALU.pow) \
            .then_inc(net["p_rstd"], 1)
        for t in range(NT):
            pool.wait_ge(net["p_routed"], t + 1)
            for h in range(PH):
                i = t * PH + h
                if i >= 2:
                    pool.wait_ge(net["p_weights"], i - 1)
                nq = self.nq[:, t % 2, :].rearrange("p (c v) -> p c v", c=PC)
                ed = self.ed[:, t % 2, :].rearrange("p (c v) -> p c v", c=PC)
                fx = self.fx[:, t % 2, :].rearrange("p (h v) -> p h v", h=PH)
                r = self.rank[:, h % 2, :].rearrange("p (x y) -> p x y", x=PKEYS)
                e = self.expo[:, h % 2, :].rearrange("p (x y) -> p x y", x=PKEYS)
                pool.tensor_tensor(out=r, in0=bc(nq[:, h, :], 2, PKEYS), in1=bc(nq[:, PH + h, :], 1, PKEYS),
                                   op=ALU.add)
                pool.tensor_tensor(out=e, in0=bc(fx[:, h, :], 2, PKEYS), in1=bc(ed[:, PH + h, :], 1, PKEYS),
                                   op=ALU.mult).then_inc(net["p_pairs"], 1)
            if t % GT == GT - 1:
                net.norm_pool(pool, NG + t // GT)


class Lightning:
    LAYER = 2

    def __init__(self, net):
        self.net = net
        w = net.late
        w.at = 0
        self.wq, self.wqr = w.take(8, P), w.take(8, P)
        self.wk, self.wkr = w.take(2, P), w.take(2, P)
        self.wv = w.take(2 * P)
        self.wo = w.take(8, P)
        self.cos, self.sin = w.take(1024), w.take(1024)
        self.decay = w.take(16, P)
        self.qdec = w.take(8, P)
        self.kdec = w.take(16)
        self.blk = w.take(8)
        a = Arena(net.work)
        self.q = a.take(8, GW)
        self.k = a.take(2, GW)
        self.turned = a.take(2, GW)
        self.v, self.ktok = a.take(GT, 2 * P), a.take(GT, 2 * P)
        self.qd = a.take(2, 8, P)
        self.vd = a.take(2, 16, HD)
        self.s = a.take(2, GW)
        self.o = a.take(8, GW)
        self.state = a.take(8, HD)

    def pe(self, pe):
        net, bank = self.net, self.net.bank
        xT = net.xT[0]
        net.layer_start(pe, 2)
        pe.wait_ge(net["w2_loaded"], 16 * 12)
        for g in range(NG):
            n = 2 * NG + g
            xg = xT[:, g * GW:(g + 1) * GW]
            for c in range(10):
                i = 10 * g + c
                w, wr = (self.wq[:, c, :], self.wqr[:, c, :]) if c < 8 else (self.wk[:, c - 8, :], self.wkr[:, c - 8, :])
                if i >= 2:
                    pe.wait_ge(net["l_rotated"], i - 1)
                if c == 1 and g:
                    pe.wait_ge(net["l_o_copied"], 8 * g)
                pe.matmul(bank[4 + 2 * (c % 2)], w, xg, start=True, stop=True)
                pe.matmul(bank[5 + 2 * (c % 2)], wr, xg, start=True, stop=True).then_inc(net["l_qk"], 1)
            pe.wait_ge(net["l_rotated"], 10 * (g + 1))
            for k in range(GT):
                t = g * GT + k
                mm = pe.matmul(net.pairs[3][:, k * 2 * P:(k + 1) * 2 * P], xT[:, t * P:(t + 1) * P], self.wv,
                               start=True, stop=True)
            mm.then_inc(net["l_v"], 1)
            pe.wait_ge(net["l_summed"], 10 * (g + 1))
            for k in range(GT):
                for pr in range(2):
                    o = k * 2 * P + pr * P
                    mm = pe.transpose(net.pairs[2][:, o:o + P], self.k[:, pr, k * P:(k + 1) * P], net.ident)
            mm.then_inc(net["l_kt"], 1)
            pe.wait_ge(net["l_vk_copied"], 2 * (g + 1))
            for k in range(GT):
                t = g * GT + k
                for kv in range(NKV):
                    i = t * NKV + kv
                    pr, half = divmod(kv, 2)
                    rows = slice(half * HD, half * HD + HD)
                    if i >= 2:
                        pe.wait_ge(net["l_decayed"], i - 1)
                    pe.matmul(bank[4 + kv % 2], self.k[rows, pr, k * P:(k + 1) * P],
                              self.q[rows, pr * 4:pr * 4 + 4, k * P:(k + 1) * P], start=True, stop=True) \
                      .then_inc(net["l_scores"], 1)
                    if kv:
                        self.output(pe, t, kv - 1)
                self.output(pe, t, 3)
                if t % 8 != 7:
                    pe.wait_ge(net["l_vd"], t + 1)
                    if t:
                        pe.wait_ge(net["l_state"], t - t // 8)
                    if n:
                        pe.wait_ge(net["normed"], n)
                    for kv in range(NKV):
                        pr, half = divmod(kv, 2)
                        mm = pe.matmul(bank[2][half * HD:half * HD + HD, pr * 256:pr * 256 + 256],
                                       self.ktok[:, k, kv * HD:(kv + 1) * HD],
                                       self.vd[:, t % 2, kv * 4:kv * 4 + 4, :].rearrange("p a b -> p (a b)"),
                                       start=True, stop=True)
                    mm.then_inc(net["l_added"], 1)
            pe.wait_ge(net["l_o_copied"], 8 * (g + 1))
            if n >= 2:
                pe.wait_ge(net["y_ready"], n - 1)
            for c in range(8):
                mm = pe.matmul(bank[g % 2], self.wo[:, c, :], self.o[:, c, :], start=(c == 0), stop=(c == 7))
            mm.then_inc(net["out_ready"], 1)
            net.norm_pe_back(pe, n)
            net.norm_pe_forth(pe, n)

    def output(self, pe, t, kv):
        net = self.net
        k = t % GT
        pr, half = divmod(kv, 2)
        rows = slice(half * HD, half * HD + HD)
        out = net.bank[6 + pr][rows, :]
        first = t % 8 == 0
        if t and half == 0:
            pe.wait_ge(net["l_o_copied"], 2 * (t - 1) + pr + 1)
        if not first:
            pe.wait_ge(net["l_qd"], t + 1)
            pe.wait_ge(net["l_state"], t - t // 8)
            for m in range(4):
                pe.matmul(out[:, m * P:(m + 1) * P], self.state[rows, pr * 4 + m, :],
                          self.qd[rows, t % 2, pr * 4 + m, :], start=(m == 0), stop=False, skip_group_check=True)
        pe.wait_ge(net["l_decayed"], t * NKV + kv + 1)
        mm = pe.matmul(out, self.v[:, k, kv * HD:(kv + 1) * HD], self.s[:, kv % 2, :], start=first, stop=True,
                       skip_group_check=True)
        mm.then_inc(net["l_out"], 1)

    def act(self, act, ch):
        net = self.net
        net.layer_start(act, 2)
        for g in range(NG):
            act.wait_ge(net["l_v"], g + 1)
            if g:
                act.wait_ge(net["out_ready"], 2 * NG + g)
            act.activation(self.v.rearrange("p a b -> p (a b)"), net.pairs[3][:, :], ACT.Copy) \
               .then_inc(net["l_vk_copied"], 1)
            act.wait_ge(net["l_kt"], g + 1)
            act.activation(self.ktok.rearrange("p a b -> p (a b)"), net.pairs[2][:, :], ACT.Copy) \
               .then_inc(net["l_vk_copied"], 1)
            for k in range(GT):
                t = g * GT + k
                for pr in range(2):
                    act.wait_ge(net["l_out"], t * NKV + 2 * pr + 2)
                    act.activation(self.o[:, pr * 4:pr * 4 + 4, k * P:(k + 1) * P],
                                   net.bank[6 + pr].rearrange("p (a b) -> p a b", a=4), ACT.Copy) \
                       .then_inc(net["l_o_copied"], 1)
            net.norm_act(act, 2 * NG + g)

    def dve(self, dve, ch):
        net = self.net
        net.layer_start(dve, 2)
        dve.wait_ge(net["w2_loaded"], 16 * 12)
        for g in range(NG):
            pos = (g % 2) * GW
            if g:
                dve.wait_ge(net["out_ready"], 2 * NG + g)
            for c in range(10):
                i = 10 * g + c
                b = 4 + 2 * (c % 2)
                dve.wait_ge(net["l_qk"], i + 1)
                dst = self.q[:, c, :] if c < 8 else self.k[:, c - 8, :]
                dve.tensor_tensor(out=dst, in0=net.bank[b], in1=self.cos[:, pos:pos + GW], op=ALU.mult)
                if i >= 2:
                    dve.wait_ge(net["l_summed"], i - 1)
                dve.tensor_tensor(out=self.turned[:, c % 2, :], in0=net.bank[b + 1], in1=self.sin[:, pos:pos + GW],
                                  op=ALU.mult).then_inc(net["l_rotated"], 1)
            for k in range(GT):
                t = g * GT + k
                for kv in range(NKV):
                    i = t * NKV + kv
                    dve.wait_ge(net["l_scores"], i + 1)
                    if i >= 2:
                        dve.wait_ge(net["l_out"], i - 1)
                    dve.tensor_tensor(out=self.s[:, kv % 2, :], in0=net.bank[4 + kv % 2],
                                      in1=self.decay[:, kv * 4:kv * 4 + 4, :].rearrange("p a b -> p (a b)"),
                                      op=ALU.mult).then_inc(net["l_decayed"], 1)
                if t % 8 != 7:
                    state = self.state.rearrange("p a b -> p (a b)")
                    dve.wait_ge(net["l_out"], (t + 1) * NKV)
                    dve.wait_ge(net["l_added"], t + 1 - t // 8)
                    if t % 8 == 0:
                        dve.tensor_copy(state, net.bank[2]).then_inc(net["l_state"], 1)
                    else:
                        ch.link(dve.tensor_tensor(out=self.state, in0=self.state, in1=bc(self.blk, 2, HD),
                                                  op=ALU.mult))
                        dve.tensor_tensor(out=state, in0=state, in1=net.bank[2], op=ALU.add) \
                           .then_inc(net["l_state"], 1)
            net.norm_dve(dve, ch, 2 * NG + g)

    def pool(self, pool, ch):
        net = self.net
        pool.wait_ge(net["w2_loaded"], 16 * 12)
        net.layer_start(pool, 2)
        for g in range(NG):
            for c in range(10):
                dst = self.q[:, c, :] if c < 8 else self.k[:, c - 8, :]
                pool.wait_ge(net["l_rotated"], 10 * g + c + 1)
                pool.tensor_tensor(out=dst, in0=dst, in1=self.turned[:, c % 2, :], op=ALU.add) \
                    .then_inc(net["l_summed"], 1)
            pool.wait_ge(net["l_summed"], 10 * (g + 1))
            pool.wait_ge(net["l_vk_copied"], 2 * g + 1)
            for k in range(GT):
                t = g * GT + k
                if t >= 2:
                    pool.wait_ge(net["l_out"], (t - 1) * NKV)
                    pool.wait_ge(net["l_added"], t - 1 - (t - 1) // 8)
                pool.tensor_tensor(out=self.qd[:, t % 2, :, :], in0=self.q[:, :, k * P:(k + 1) * P], in1=self.qdec,
                                   op=ALU.mult).then_inc(net["l_qd"], 1)
                for kv in range(NKV):
                    ins = pool.tensor_tensor(out=self.vd[:, t % 2, kv * 4:kv * 4 + 4, :],
                                             in0=bc(self.v[:, k, kv * HD:(kv + 1) * HD], 1, 4),
                                             in1=bc(self.kdec[:, kv * 4:kv * 4 + 4], 2, HD), op=ALU.mult)
                ins.then_inc(net["l_vd"], 1)
            net.norm_pool(pool, 2 * NG + g)


class Gates:

    def __init__(self, net, arena, layer, experts, keep, renorm, tag):
        self.net, self.layer, self.experts, self.keep, self.renorm, self.tag = net, layer, experts, keep, renorm, tag
        self.wide = experts + 8 - keep
        a = arena
        self.logit = a.take(GT, 16)
        self.peak, self.total = a.take(GT), a.take(GT)
        self.weights = a.take(GT, 24)
        self.top, self.kept, self.left = a.take(GT, 8), a.take(GT, 8), a.take(GT, 24)
        self.gate = a.take(GT, 16)
        self.gateT = a.take(GW)
        self.spread = a.take(experts, GW)

    def pe(self, pe, g, xT, w, b):
        net, E = self.net, self.experts
        n = self.layer * NG + g
        if g:
            pe.wait_ge(net[self.tag + "_spread"], E * g)
        for k in range(GT):
            t = g * GT + k
            out = net.bank[6][:, k * 16:k * 16 + E]
            mm = pe.matmul(out, xT[:, t * P:(t + 1) * P], w, start=True, stop=(b is None))
            if b is not None:
                mm = pe.matmul(out, net.ones[0:1, :], b, start=False, stop=True)
        mm.then_inc(net[self.tag + "_logits"], 1)
        pe.wait_ge(net[self.tag + "_gates"], g + 1)
        for k in range(GT):
            mm = pe.transpose(net.bank[7][0:16, k * P:(k + 1) * P], self.gate[:, k, :], net.ident)
        mm.then_inc(net[self.tag + "_gatesT"], 1)
        pe.wait_ge(net[self.tag + "_gatesT_copied"], g + 1)
        for e in range(E):
            i = g * E + e
            if e >= 2:
                pe.wait_ge(net[self.tag + "_spread"], i - 1)
            pe.matmul(net.bank[6 + e % 2], self.sel[0:16, e, :], self.gateT[0:16, :], start=True, stop=True) \
              .then_inc(net[self.tag + "_wide"], 1)

    def act(self, act, g):
        net, E = self.net, self.experts
        act.wait_ge(net[self.tag + "_shifted"], g + 1)
        act.activation(self.weights[:, :, 0:E], self.logit[:, :, 0:E], ACT.Exp).then_inc(net[self.tag + "_exp"], 1)
        act.wait_ge(net[self.tag + "_gatesT"], g + 1)
        if g:
            act.wait_ge(net["out_ready"], self.layer * NG + g)
        act.activation(self.gateT[0:16, :], net.bank[7][0:16, :], ACT.Copy) \
           .then_inc(net[self.tag + "_gatesT_copied"], 1)
        for e in range(E):
            act.wait_ge(net[self.tag + "_wide"], g * E + e + 1)
            act.activation(self.spread[:, e, :], net.bank[6 + e % 2], ACT.Copy).then_inc(net[self.tag + "_spread"], 1)

    def dve_fill(self, dve):
        for i in range(8 - self.keep):
            dve.memset(self.weights[:, :, self.experts + i:self.experts + i + 1], -1.0 - i)
            dve.memset(self.kept[:, :, self.keep + i:self.keep + i + 1], -1.0 - i)
        dve.memset(self.gate[:, :, 0:15], 0.0)
        return dve.memset(self.gate[:, :, 15:16], 1.0)

    def dve(self, dve, ch, g):
        net, E, keep, wide = self.net, self.experts, self.keep, self.wide
        dve.wait_ge(net[self.tag + "_logits"], g + 1)
        raw = net.bank[6][:, 0:GT * 16].rearrange("p (k e) -> p k e", k=GT)[:, :, 0:E]
        ch.link(dve.reduce_max(self.peak, raw, AX.X))
        dve.tensor_tensor(out=self.logit[:, :, 0:E], in0=raw, in1=bc(self.peak, 2, E), op=ALU.subtract) \
           .then_inc(net[self.tag + "_shifted"], 1)
        dve.wait_ge(net[self.tag + "_exp"], g + 1)
        w = self.weights[:, :, 0:E]
        ch.link(dve.reduce_sum(self.total, w, AX.X))
        ch.link(dve.reciprocal(self.total, self.total))
        ch.link(dve.tensor_tensor(out=w, in0=w, in1=bc(self.total, 2, E), op=ALU.mult))
        for k in range(GT):
            ins = dve.max(self.top[:, k, :], self.weights[:, k, 0:E])
        ch.link(ins)
        ch.link(dve.tensor_copy(self.kept[:, :, 0:keep], self.top[:, :, 0:keep]))
        for k in range(GT):
            ins = dve.match_replace(self.left[:, k, 0:wide], self.kept[:, k, :], self.weights[:, k, 0:wide], -99.0)
        ch.link(ins)
        ch.link(dve.tensor_tensor(out=self.left[:, :, 0:E], in0=w, in1=self.left[:, :, 0:E], op=ALU.not_equal))
        last = dve.tensor_tensor(out=self.gate[:, :, 0:E], in0=w, in1=self.left[:, :, 0:E], op=ALU.mult)
        if self.renorm is not None:
            ch.link(last)
            ch.link(dve.reduce_sum(self.total, self.gate[:, :, 0:E], AX.X))
            ch.link(dve.tensor_scalar(self.total, self.total, self.renorm, None, ALU.add))
            ch.link(dve.reciprocal(self.total, self.total))
            last = dve.tensor_tensor(out=self.gate[:, :, 0:E], in0=self.gate[:, :, 0:E],
                                     in1=bc(self.total, 2, E), op=ALU.mult)
        last.then_inc(net[self.tag + "_gates"], 1)


class GeluExperts:
    LAYER = 3

    def __init__(self, net):
        self.net = net
        w = net.mid
        w.at = 0
        self.w1, self.w2 = w.take(C1, P), w.take(C1, P)
        self.b1 = w.take(C1)
        self.gw = w.take(16)
        self.gb = w.take(16)
        self.b2 = w.take(P)
        a = Arena(net.work)
        self.gates = Gates(net, a, 3, E1, 3, None, "g1")
        self.gates.sel = a.take(E1, P)
        self.h, self.hg = a.take(3, GW), a.take(3, GW)

    def pe(self, pe):
        net, bank = self.net, self.net.bank
        xT = net.xT[1]
        net.layer_start(pe, 3)
        pe.wait_ge(net["w3_loaded"], 16 * 7)
        for g in range(NG):
            n = 3 * NG + g
            self.gates.pe(pe, g, xT, self.gw[:, 0:E1], self.gb[0:1, 0:E1])
            for c in range(C1 + 1):
                i = C1 * g + c
                if c < C1:
                    if i >= 2:
                        pe.wait_ge(net["e1_act"], i - 1)
                    pe.matmul(bank[4 + i % 2], self.w1[:, c, :], xT[:, g * GW:(g + 1) * GW], start=True, stop=True) \
                      .then_inc(net["e1_up"], 1)
                if c:
                    j = i - 1
                    if c == 1 and n >= 2:
                        pe.wait_ge(net["y_ready"], n - 1)
                    if c - 1 < C1S:
                        pe.wait_ge(net["e1_act"], j + 1)
                        src = self.h[:, j % 3, :]
                    else:
                        pe.wait_ge(net["e1_gated"], j + 1 - C1S * (g + 1))
                        src = self.hg[:, j % 3, :]
                    pe.matmul(bank[g % 2], self.w2[:, c - 1, :], src, start=(c == 1), stop=False) \
                      .then_inc(net["e1_down"], 1)
            pe.matmul(bank[g % 2], self.b2[0:16, :], self.gates.gateT[0:16, :], start=False, stop=True) \
              .then_inc(net["out_ready"], 1)
            net.norm_pe_back(pe, n)
            net.norm_pe_forth(pe, n)

    def act(self, act, ch):
        net = self.net
        net.layer_start(act, 3)
        act.wait_ge(net["w3_loaded"], 16 * 7)
        act.wait_ge(net["g1_filled"], 1)
        for g in range(NG):
            self.gates.act(act, g)
            for c in range(C1):
                i = C1 * g + c
                act.wait_ge(net["e1_up"], i + 1)
                if i >= 3:
                    act.wait_ge(net["e1_down"], i - 2)
                act.activation(self.h[:, i % 3, :], net.bank[4 + i % 2], ACT.Gelu, bias=self.b1[:, c:c + 1]) \
                   .then_inc(net["e1_act"], 1)
            net.norm_act(act, 3 * NG + g)

    def dve(self, dve, ch):
        net = self.net
        net.layer_start(dve, 3)
        dve.wait_ge(net["w3_loaded"], 16 * 7)
        self.gates.dve_fill(dve).then_inc(net["g1_filled"], 1)
        dve.wait_ge(net["g1_filled"], 1)
        for g in range(NG):
            self.gates.dve(dve, ch, g)
            for c in range(C1S, C1):
                i = C1 * g + c
                e = (c - C1S) // 2
                dve.wait_ge(net["e1_act"], i + 1)
                dve.wait_ge(net["g1_spread"], E1 * g + e + 1)
                if i >= 3:
                    dve.wait_ge(net["e1_down"], i - 2)
                dve.tensor_tensor(out=self.hg[:, i % 3, :], in0=self.h[:, i % 3, :],
                                  in1=self.gates.spread[:, e, :], op=ALU.mult).then_inc(net["e1_gated"], 1)
            net.norm_dve(dve, ch, 3 * NG + g, twice=True)

    def pool(self, pool, ch):
        for g in range(NG):
            self.net.norm_pool(pool, 3 * NG + g)


class Forgetting:
    LAYER = 4
    TERMS = ((0, 0), (0, 1), (0, 2), (1, 0), (1, 1), (1, 2), (2, 0), (2, 1))
    ROUNDS = 4
    UNITS = 98
    STEPS = 24
    SPLIT_DMAS = 9
    STACK_DMAS = 17

    def __init__(self, net):
        self.net = net
        nc = net.nc
        w = net.const
        self.wq, self.wk = w.take(P), w.take(P)
        self.wv, self.wo, self.wf = w.take(P), w.take(P), w.take(16)
        half = w.take(3 * P // 2).bitcast(BF16)
        self.identb, self.mask_n, self.mask_t = (half[:, i * P:(i + 1) * P] for i in range(3))
        self.mask_n32 = w.take(P)
        a = Arena(net.work)
        both = a.take(4, 4096)
        self.qs = [both[:, i, :].bitcast(BF16).rearrange("p (h t) -> p h t", h=8) for i in (0, 1)]
        self.ks = [both[:, i, :].bitcast(BF16).rearrange("p (h t) -> p h t", h=8) for i in (2, 3)]
        self.rows32 = both
        self.v = a.take(NT * 144 + 32)
        self.e = a.take(2, 4, GW)
        s = Arena(both.rearrange("p a b -> p (a b)"))
        self.full = [s.take(TOK), s.take(TOK), s.take(TOK)]
        self.parts = [[s.take(TOK // 2).bitcast(BF16) for _ in range(3)] for _ in range(3)]
        e2 = self.e.rearrange("p a b c -> p (a b c)")
        self.z, self.zabs = e2[:, 0:TOK], e2[:, TOK:2 * TOK]
        t = net.late
        t.at = 5500
        self.m = t.take(2, 8 * 2, 8)
        self.negm = t.take(GT, 8)
        self.mparts = t.take(GT * 12).bitcast(BF16).rearrange("p (k s h) -> p k s h", k=GT, s=3)
        self.mrows = [t.take(GW // 2).bitcast(BF16) for _ in range(2)]
        self.ot = t.take(2, GW)
        self.rz = t.take(2, GT * 4)
        self.o = t.take(8, P)
        self.oT = t.take(GW)
        self.scratch = [nc.dram_tensor(f"split_{n}", (3, r, TOK), BF16, kind="Internal").ap()
                        for n, r in (("q", P), ("k", P), ("f", 16))]

    def units(self):
        out = [("scores", it, h, 0) for it in range(4) for h in range(8)]
        late = [("scores", it, h, half) for it in range(4, 8) for h in range(8) for half in range(2)]
        out += late[:6] + [("turn", 0, 0, 0)] + late[6:] + [("turn", 1, 0, 0)]
        assert len(out) == self.UNITS
        return out

    def steps(self):
        return [(g, s, j) for g in range(2) for s in range(2) for j in range(4 * g + 4)]

    def pe(self, pe):
        net, bank = self.net, self.net.bank
        xT = net.xT[0]
        net.layer_start(pe, 4)
        pe.wait_ge(net["w4_loaded"], 16 * 6)
        for g in range(NG):
            pe.matmul(bank[4 + g][0:16, :], self.wf, xT[:, g * GW:(g + 1) * GW], start=True, stop=True) \
              .then_inc(net["f_z"], 1)
        for g in range(NG):
            if g >= 2:
                pe.wait_ge(net["f_v_copied"], g - 1)
            for k in range(GT):
                t = g * GT + k
                mm = pe.matmul(bank[g % 2][:, k * P:(k + 1) * P], xT[:, t * P:(t + 1) * P], self.wv,
                               start=True, stop=True)
            mm.then_inc(net["f_v"], 1)
        for i in range(8):
            if i < 4:
                pe.wait_ge(net["f_z_copied"], i + 1)
            else:
                pe.wait_ge(net["f_qk_copied"], i - 3)
            pe.matmul(bank[4 + i % 4], (self.wq, self.wk)[i // 4], xT[:, (i % 4) * GW:(i % 4 + 1) * GW],
                      start=True, stop=True).then_inc(net["f_qk"], 1)
        pe.wait_ge(net["f_qk_copied"], 8)
        pe.wait_ge(net["f_v_copied"], NG)
        units, steps = self.units(), self.steps()
        for i in range(self.UNITS):
            self.unit_pe(pe, 0, i, units[i])
        for r in range(self.ROUNDS):
            done = 0
            for k in range(self.STEPS + 1):
                if k < self.STEPS:
                    self.scores_pe(pe, r, k, steps[k])
                if k:
                    self.values_pe(pe, r, k - 1, steps[k - 1])
                if r + 1 < self.ROUNDS:
                    upto = self.UNITS * min(k + 1, self.STEPS) // self.STEPS
                    for i in range(done, upto):
                        self.unit_pe(pe, r + 1, i, units[i])
                    done = upto
                if 1 < k <= self.STEPS and steps[k - 2][2] == 4 * steps[k - 2][0] + 3:
                    self.turn_out_pe(pe, r, steps[k - 2])
            self.turn_out_pe(pe, r, steps[-1])
            if r % 2:
                self.out_pe(pe, r // 2)

    def unit_pe(self, pe, r, i, unit):
        net = self.net
        kind, it, h, half = unit
        u = r * self.UNITS + i
        bank = net.bank[u % 2]
        if i == 0:
            pe.wait_ge(net[f"f_stacked{r % 2}"], 16 * self.STACK_DMAS * (r // 2 + 1))
        if u >= 2:
            pe.wait_ge(net["f_unit_read"], u - 1)
        if kind == "turn":
            pe.wait_ge(net["f_negmax"], 2 * r + it + 1)
            for k in range(GT):
                mm = pe.transpose(bank.bitcast(BF16)[0:24, k * P:(k + 1) * P],
                                  self.mparts[:, k, :, :].rearrange("p s h -> p (s h)"), self.identb)
            mm.then_inc(net["f_unit"], 1)
            return
        q = self.qs[r % 2][0:96, h, it * P:(it + 1) * P]
        k = self.ks[r % 2][0:96, h, :]
        lo, hi = half * GW, min(half * GW + GW, (it + 1) * P)
        own = it // 4 == half
        rest = hi - P if own else hi
        if rest > lo:
            mm = pe.matmul(bank[:, 0:rest - lo], q, k[:, lo:rest], start=True, stop=True)
        if own:
            pe.matmul(bank[:, rest - lo:hi - lo], q, k[:, rest:hi], start=True, stop=False)
            mm = pe.matmul(bank[:, rest - lo:hi - lo], self.identb, self.mask_n, start=False, stop=True)
        mm.then_inc(net["f_unit"], 1)

    def scores_pe(self, pe, r, k, step):
        net = self.net
        g, s, j = step
        n = r * self.STEPS + k
        lo = max(0, j - 4 * g) * P
        if s == 0 and j == 0:
            pe.wait_ge(net[f"f_mrows{g}"], 48 * (r + 1))
        for q in range(4):
            if q % 2 == 0 and n:
                pe.wait_ge(net["f_exp"], 2 * n - 1 + q // 2)
            bank, h = net.bank[4 + q], 4 * s + q
            kt = self.ks[r % 2][:, h, j * P:(j + 1) * P]
            at = lo
            if j >= 4 * g:
                pe.matmul(bank[:, lo:lo + P], kt, self.qs[r % 2][:, h, g * GW + lo:g * GW + lo + P],
                          start=True, stop=False)
                mm = pe.matmul(bank[:, lo:lo + P], self.identb, self.mask_t, start=False, stop=True)
                at = lo + P
            if at < GW:
                mm = pe.matmul(bank[:, at:GW], kt, self.qs[r % 2][:, h, g * GW + at:(g + 1) * GW],
                               start=True, stop=True)
            if q % 2:
                mm.then_inc(net["f_shifted"], 1)

    def slot(self, r, step):
        return r * 4 + 2 * step[0] + step[1]

    def values_pe(self, pe, r, k, step):
        net = self.net
        g, s, j = step
        n = r * self.STEPS + k
        lo = max(0, j - 4 * g) * P
        slot = self.slot(r, step)
        pe.wait_ge(net["f_exp"], 2 * n + 2)
        if j == 0 and slot >= 2:
            pe.wait_ge(net["f_normed"], slot - 1)
        for q in range(4):
            h = 8 * (r % 2) + 4 * s + q
            at = ((r // 2) * 8 + j) * 144 + h * 9
            mm = pe.matmul(net.bank[2 + slot % 2][32 * q:32 * q + 32, lo:GW], self.v[:, at:at + 32],
                           self.e[:, n % 2, q, lo:GW], start=(j == 0), stop=(j == 4 * g + 3),
                           skip_group_check=True)
        mm.then_inc(net["f_pv"], 1)

    def turn_out_pe(self, pe, r, step):
        net = self.net
        slot = self.slot(r, step)
        pe.wait_ge(net["f_ot_copied"], slot + 1)
        for k in range(GT):
            mm = pe.transpose(net.bank[2 + slot % 2][:, k * P:(k + 1) * P], self.ot[:, slot % 2, k * P:(k + 1) * P],
                              net.ident)
        mm.then_inc(net["f_turned"], 1)

    def out_pe(self, pe, b):
        net = self.net
        pe.wait_ge(net["f_normed"], 8 * (b + 1))
        for g in (2 * b, 2 * b + 1):
            n = 4 * NG + g
            for k in range(GT):
                mm = pe.transpose(net.bank[2][:, k * P:(k + 1) * P], self.o[:, (g % 2) * GT + k, :], net.ident)
            mm.then_inc(net["f_oT"], 1)
            pe.wait_ge(net["f_oT_copied"], g + 1)
            pe.matmul(net.bank[3], self.wo, self.oT, start=True, stop=True).then_inc(net["out_ready"], 1)
            net.norm_pe_back(pe, n)
            net.norm_pe_forth(pe, n)
            if g % 2 == 0:
                pe.wait_ge(net["xT_done"], n + 1)

    def act(self, act, ch):
        net = self.net
        net.layer_start(act, 4)
        act.wait_ge(net["f_zabs"], 1)
        ch.link(act.activation(self.zabs[0:16, :], self.zabs[0:16, :], ACT.Exp))
        act.activation(self.zabs[0:16, :], self.zabs[0:16, :], ACT.Ln, bias=1.0).then_inc(net["f_ln"], 1)
        for i in range(8):
            act.wait_ge(net["f_qk"], i + 1)
            act.activation(self.full[i // 4][:, (i % 4) * GW:(i % 4 + 1) * GW], net.bank[4 + i % 4], ACT.Copy,
                           scale=(float(FD) ** -0.5, 1.0)[i // 4]).then_inc(net["f_qk_copied"], 1)
        steps = self.steps()
        act.wait_ge(net["f_split"], 3)
        for r in range(self.ROUNDS):
            for k in range(self.STEPS):
                g, s, j = steps[k]
                n = r * self.STEPS + k
                lo = max(0, j - 4 * g) * P
                for pair in range(2):
                    act.wait_ge(net["f_shifted"], 2 * n + pair + 1)
                    if n >= 2:
                        act.wait_ge(net["f_pv"], n - 1)
                    act.activation(self.e[:, n % 2, 2 * pair:2 * pair + 2, lo:GW],
                                   net.pairs[2 + pair][:, :].rearrange("p (q t) -> p q t", q=2)[:, :, lo:GW],
                                   ACT.Exp).then_inc(net["f_exp"], 1)
                if k and steps[k - 1][2] == 4 * steps[k - 1][0] + 3:
                    self.copy_slot(act, r, k - 1, steps[k - 1])
            self.copy_slot(act, r, self.STEPS - 1, steps[-1])
            if r % 2:
                for g in (r - 1, r):
                    act.wait_ge(net["f_oT"], g + 1)
                    if g:
                        act.wait_ge(net["out_ready"], 4 * NG + g)
                    act.activation(self.oT, net.bank[2], ACT.Copy).then_inc(net["f_oT_copied"], 1)
                    net.norm_act(act, 4 * NG + g)

    def copy_slot(self, act, r, k, step):
        net = self.net
        slot = self.slot(r, step)
        act.wait_ge(net["f_pv"], r * self.STEPS + k + 1)
        if slot >= 2:
            act.wait_ge(net["f_turned"], slot - 1)
        act.activation(self.ot[:, slot % 2, :], net.bank[2 + slot % 2], ACT.Copy).then_inc(net["f_ot_copied"], 1)

    def dve(self, dve, ch):
        net = self.net
        net.layer_start(dve, 4)
        dve.wait_ge(net["w4_loaded"], 16 * 6)
        z, za, fl = self.z[0:16, :], self.zabs[0:16, :], self.full[2][0:16, :]
        dve.tensor_copy(self.identb, net.ident)
        dve.tensor_copy(self.mask_n, self.mask_n32)
        ch.link(dve.tensor_copy(self.mask_t, net.mask))
        for g in range(NG):
            dve.wait_ge(net["f_z"], g + 1)
            dve.tensor_copy(z[:, g * GW:(g + 1) * GW], net.bank[4 + g][0:16, :]).then_inc(net["f_z_copied"], 1)
        dve.wait_ge(net["f_z_copied"], NG)
        dve.scalar_tensor_tensor(out=za, in0=z, scalar=-1.0, in1=z, op0=ALU.mult, op1=ALU.min) \
           .then_inc(net["f_zabs"], 1)
        ch.link(dve.tensor_scalar(fl, z, -1.0, 0.0, ALU.mult, ALU.max))
        ch.link(dve.memset(self.v, 1.0))
        for g in range(NG):
            dve.wait_ge(net["f_v"], g + 1)
            dve.tensor_copy(self.v[:, g * GT * 144:(g + 1) * GT * 144]
                            .rearrange("p (t h d) -> p t h d", t=GT, h=FH)[:, :, :, 0:FD],
                            net.bank[g % 2].rearrange("p (t h d) -> p t h d", t=GT, h=FH)) \
               .then_inc(net["f_v_copied"], 1)
        dve.wait_ge(net["f_ln"], 1)
        ch.link(dve.tensor_tensor(out=za, in0=fl, in1=za, op=ALU.add))
        ch.link(dve.memset(z, 1.0))
        for b in range(2):
            c = slice(b * 1024, (b + 1) * 1024)
            ins = dve.tensor_tensor_scan(fl[:, c], z[:, c], za[:, c], 0.0, ALU.mult, ALU.add)
        ch.link(ins)
        for i in (0, 1, 2):
            rows = slice(0, (P, P, 16)[i])
            if i < 2:
                dve.wait_ge(net["f_qk_copied"], 4 * (i + 1))
            self.split(dve, ch, self.full[i][rows, :], [p[rows, :] for p in self.parts[i]]) \
                .then_inc(net["f_split"], 1)
        units, steps = self.units(), self.steps()
        for i in range(self.UNITS):
            self.unit_dve(dve, ch, 0, i, units[i])
        for r in range(self.ROUNDS):
            done = 0
            for k in range(self.STEPS + 1):
                if r + 1 < self.ROUNDS:
                    upto = self.UNITS * min(k + 1, self.STEPS) // self.STEPS
                    for i in range(done, upto):
                        self.unit_dve(dve, ch, r + 1, i, units[i])
                    done = upto
                if 1 < k <= self.STEPS and steps[k - 2][2] == 4 * steps[k - 2][0] + 3:
                    self.norm_slot(dve, ch, r, steps[k - 2])
            self.norm_slot(dve, ch, r, steps[-1])
            if r % 2:
                for g in (r - 1, r):
                    net.norm_dve(dve, ch, 4 * NG + g, bank=3)

    def split(self, dve, ch, x, parts):
        for i in range(2):
            ch.link(dve.tensor_copy(parts[i], x))
            ch.link(dve.tensor_tensor(out=x, in0=x, in1=parts[i], op=ALU.subtract))
        return dve.tensor_copy(parts[2], x)

    def unit_dve(self, dve, ch, r, i, unit):
        net = self.net
        kind, it, h, half = unit
        u = r * self.UNITS + i
        bank = net.bank[u % 2]
        if kind == "turn":
            dve.wait_ge(net["f_unit"], u + 1)
            n = 2 * r + it
            if n >= 2:
                dve.wait_ge(net[f"f_mrows{n % 2}"], 48 * (n // 2))
            dve.tensor_copy(self.mrows[n % 2][0:24, :], bank.bitcast(BF16)[0:24, 0:GW]).then_inc(net["f_unit_read"], 1)
            return
        dve.wait_ge(net["f_unit"], u + 1)
        width = min(GW, (it + 1) * P - half * GW)
        dve.reduce_max(self.m[:, r % 2, 2 * it + half, h:h + 1], bank[:, 0:width], AX.X) \
           .then_inc(net["f_unit_read"], 1)
        if h == 7 and it % 4 == 3 and half == it // 4:
            dve.wait_ge(net["f_unit_read"], u + 1)
            g = it // 4
            m = self.m[:, r % 2, 8 * g:8 * g + 8, :].rearrange("p (k s) h -> p k s h", s=2)
            if g:
                ch.link(dve.tensor_tensor(out=self.negm, in0=m[:, :, 0, :], in1=m[:, :, 1, :], op=ALU.max))
                ch.link(dve.tensor_scalar(self.negm, self.negm, -1.0, None, ALU.mult))
            else:
                ch.link(dve.tensor_scalar(self.negm, m[:, :, 0, :], -1.0, None, ALU.mult))
            if r or g:
                dve.wait_ge(net["f_unit"], self.turn_unit(2 * r + g - 1) + 1)
            self.split(dve, ch, self.negm, [self.mparts[:, :, s, :] for s in range(3)]) \
                .then_inc(net["f_negmax"], 1)

    def turn_unit(self, n):
        return (n // 2) * self.UNITS + (self.UNITS - 1 if n % 2 else 38)

    def norm_slot(self, dve, ch, r, step):
        net = self.net
        g, s, _ = step
        slot = self.slot(r, step)
        dve.wait_ge(net["f_turned"], slot + 1)
        o = net.bank[2 + slot % 2].rearrange("p (k q e) -> p k q e", k=GT, q=4)
        rz = self.rz[:, slot % 2, :].rearrange("p (k q) -> p k q", k=GT)
        ch.link(dve.reciprocal(rz, o[:, :, :, FD]))
        if r == 2 and g == 0 and s == 0:
            dve.wait_ge(net["f_oT"], 2)
        h = 8 * (r % 2) + 4 * s
        out = self.o[:, 4 * g:4 * g + 4, h * FD:(h + 4) * FD].rearrange("p k (q d) -> p k q d", q=4)
        dve.tensor_tensor(out=out, in0=o[:, :, :, 0:FD], in1=bc(rz, 3, FD), op=ALU.mult) \
           .then_inc(net["f_normed"], 1)

    def pool(self, pool, ch):
        net = self.net
        ones = float(np.array([0x3F803F80], np.uint32).view(np.float32)[0])
        pool.wait_ge(net["f_sent"], 16 * self.SPLIT_DMAS)
        for i in range(2):
            pool.memset(self.rows32[64:96, i, :], ones)
            pool.memset(self.rows32[96:128, i, :], 0.0)
            pool.memset(self.rows32[64:96, 2 + i, :], 0.0)
            pool.memset(self.rows32[96:128, 2 + i, :], ones).then_inc(net["f_filled"], 1)
        for g in range(NG):
            net.norm_pool(pool, 4 * NG + g)

    def send_splits(self, sp):
        net = self.net
        for i in range(3):
            sp.wait_ge(net["f_split"], i + 1)
            for part in range(3):
                rows = (P, P, 16)[i]
                sp.dma_start(self.scratch[i][part], self.parts[i][part][0:rows, :]).then_inc(net["f_sent"], 16)
        sp.wait_ge(net["f_sent"], 16 * self.SPLIT_DMAS)

    def stack(self, sp, r):
        net = self.net
        b, hh = divmod(r, 2)
        if r >= 2:
            sp.wait_ge(net["f_pv"], self.STEPS * (r - 1))
        toks, heads = slice(b * 1024, b * 1024 + 1024), slice(8 * hh, 8 * hh + 8)
        for n, (i, j) in enumerate(self.TERMS):
            for dst, src in ((self.qs, self.scratch[0][i]), (self.ks, self.scratch[1][j])):
                sp.dma_start(dst[r % 2][8 * n:8 * n + 8, :, :],
                             src.rearrange("(h d) t -> d h t", d=FD)[:, heads, toks]).then_inc(net[f"f_stacked{r % 2}"], 16)
        if r < 2:
            sp.wait_ge(net["f_filled"], r + 1)
        sp.dma_start(self.ks[r % 2][64:67, :, :], self.scratch[2][:, heads, toks]).then_inc(net[f"f_stacked{r % 2}"], 16)

    def send_maxima(self, sp, n):
        net = self.net
        r, g = divmod(n, 2)
        sp.wait_ge(net["f_unit_read"], self.turn_unit(n) + 1)
        for s in range(3):
            sp.dma_start(self.qs[r % 2][96 + s:97 + s, :, g * GW:(g + 1) * GW],
                         self.mrows[n % 2][8 * s:8 * s + 8, :]).then_inc(net[f"f_mrows{g}"], 16)


class SiluExperts:
    LAYER = 5

    def __init__(self, net):
        self.net = net
        w = net.mid
        w.at = 0
        self.wg, self.wu, self.wd = w.take(C2, P), w.take(C2, P), w.take(C2, P)
        self.wr = w.take(16)
        a = Arena(net.work)
        self.gates = Gates(net, a, 5, E2, 2, 1e-20, "g2")
        self.gates.sel = w.take(E2, P)
        self.s, self.h, self.hg = a.take(2, GW), a.take(3, GW), a.take(3, GW)

    def pe(self, pe):
        net, bank = self.net, self.net.bank
        xT = net.xT[1]
        net.layer_start(pe, 5)
        pe.wait_ge(net["w5_loaded"], 16 * 5)
        for g in range(NG):
            n = 5 * NG + g
            xg = xT[:, g * GW:(g + 1) * GW]
            self.gates.pe(pe, g, xT, self.wr[:, 0:E2], None)
            if g == 0:
                pass
            pe.wait_ge(net["g2_spread"], E2 * (g + 1))
            for c in range(C2 + 1):
                i = C2 * g + c
                if c < C2:
                    if i >= 2:
                        pe.wait_ge(net["e2_prod"], i - 1)
                    pe.matmul(bank[4 + 2 * (i % 2)], self.wg[:, c, :], xg, start=True, stop=True) \
                      .then_inc(net["e2_gate"], 1)
                    pe.matmul(bank[5 + 2 * (i % 2)], self.wu[:, c, :], xg, start=True, stop=True) \
                      .then_inc(net["e2_up"], 1)
                if c:
                    j = i - 1
                    if c == 1:
                        pe.wait_ge(net["y_ready"], n - 1)
                    if c - 1 < 2 * E2:
                        pe.wait_ge(net["e2_gated"], j + 1 - 2 * g)
                        src = self.hg[:, j % 3, :]
                    else:
                        pe.wait_ge(net["e2_prod"], j + 1)
                        src = self.h[:, j % 3, :]
                    mm = pe.matmul(bank[g % 2], self.wd[:, c - 1, :], src, start=(c == 1), stop=False)
                    mm.then_inc(net["e2_down"], 1)
            pe.matmul(bank[g % 2], net.zeros[0:1, 0:P], net.zeros[0:1, :], start=False, stop=True) \
              .then_inc(net["out_ready"], 1)
            net.norm_pe_back(pe, n)
            net.norm_pe_forth(pe, n)

    def act(self, act, ch):
        net = self.net
        net.layer_start(act, 5)
        act.wait_ge(net["g2_filled"], 1)
        for g in range(NG):
            self.gates.act(act, g)
            for c in range(C2):
                i = C2 * g + c
                act.wait_ge(net["e2_gate"], i + 1)
                if i >= 2:
                    act.wait_ge(net["e2_prod"], i - 1)
                act.activation(self.s[:, i % 2, :], net.bank[4 + 2 * (i % 2)], ACT.Silu).then_inc(net["e2_silu"], 1)
            net.norm_act(act, 5 * NG + g)

    def dve(self, dve, ch):
        net = self.net
        net.layer_start(dve, 5)
        self.gates.dve_fill(dve).then_inc(net["g2_filled"], 1)
        dve.wait_ge(net["g2_filled"], 1)
        for g in range(NG):
            self.gates.dve(dve, ch, g)
            for c in range(C2):
                i = C2 * g + c
                dve.wait_ge(net["e2_silu"], i + 1)
                dve.wait_ge(net["e2_up"], i + 1)
                if i >= 3:
                    dve.wait_ge(net["e2_down"], i - 2)
                dve.tensor_tensor(out=self.h[:, i % 3, :], in0=self.s[:, i % 2, :], in1=net.bank[5 + 2 * (i % 2)],
                                  op=ALU.mult).then_inc(net["e2_prod"], 1)
            net.norm_dve(dve, ch, 5 * NG + g)

    def pool(self, pool, ch):
        net = self.net
        net.layer_start(pool, 5)
        for g in range(NG):
            pool.wait_ge(net["g2_spread"], E2 * (g + 1))
            for c in range(2 * E2):
                i = C2 * g + c
                pool.wait_ge(net["e2_prod"], i + 1)
                if i >= 3:
                    pool.wait_ge(net["e2_down"], i - 2)
                pool.tensor_tensor(out=self.hg[:, i % 3, :], in0=self.h[:, i % 3, :],
                                   in1=self.gates.spread[:, c // 2, :], op=ALU.mult).then_inc(net["e2_gated"], 1)
            net.norm_pool(pool, 5 * NG + g)


class LinearAttention:
    LAYER = 6

    def __init__(self, net):
        self.net = net
        w = net.const
        self.w = w.take(3 * P)
        self.b = w.take(3 * P)
        self.wp = w.take(P)
        self.bp = w.take(1)
        self.blocks = w.take(P)
        a = Arena(net.work)
        self.qkv = a.take(NT, 3 * P)
        self.sq = a.take(2, 2 * P)
        self.norm = a.take(2, 2, 32)
        self.qT = a.take(TOK)
        self.kv = a.take(2, P)
        self.oT = a.take(2, GW)

    def pe(self, pe):
        net, bank = self.net, self.net.bank
        xT = net.xT[0]
        net.layer_start(pe, 6)
        pe.wait_ge(net["w6_loaded"], 16 * 5)
        for t in range(NT + 2):
            if t < NT:
                if t >= 2:
                    pe.wait_ge(net["u_copied"], t - 1)
                pe.matmul(bank[4 + t % 2][:, 0:3 * P], xT[:, t * P:(t + 1) * P], self.w, start=True, stop=False)
                pe.matmul(bank[4 + t % 2][:, 0:3 * P], net.ones[0:1, :], self.b[0:1, :], start=False, stop=True) \
                  .then_inc(net["u_qkv"], 1)
            u = t - 2
            if u >= 0:
                b = u // 8
                pe.wait_ge(net["u_unit"], u + 1)
                if u >= 1:
                    pe.wait_ge(net["u_qT_copied"], u)
                pe.transpose(bank[6][:, 0:P], self.qkv[:, u, 0:P], net.ident).then_inc(net["u_qT"], 1)
                mm = pe.matmul(bank[7 * (1 - b)][:, 0:P], self.qkv[:, u, P:2 * P], self.qkv[:, u, 2 * P:3 * P],
                               start=(u % 8 == 0), stop=(u % 8 == 7), skip_group_check=True)
                if u % 8 == 7:
                    mm.then_inc(net["u_kv"], 1)
        for g in range(NG):
            n = 6 * NG + g
            pe.wait_ge(net["u_masked"], 2)
            pe.wait_ge(net["u_qT_copied"], NT)
            if g >= 2:
                pe.wait_ge(net["u_oT_copied"], g - 1)
            pe.matmul(bank[4 + g % 2], self.kv[:, g // 2, :], self.qT[:, g * GW:(g + 1) * GW],
                      start=True, stop=True).then_inc(net["u_o"], 1)
            pe.wait_ge(net["u_oT_copied"], g + 1)
            pe.wait_ge(net["y_ready"], n - 1)
            pe.matmul(bank[g % 2], self.wp, self.oT[:, g % 2, :], start=True, stop=True).then_inc(net["out_ready"], 1)
            net.norm_pe_back(pe, n)
            net.norm_pe_forth(pe, n)

    def act(self, act, ch):
        net = self.net
        net.layer_start(act, 6)
        for t in range(NT):
            act.wait_ge(net["u_qkv"], t + 1)
            act.activation(self.qkv[:, t, :], net.bank[4 + t % 2][:, 0:3 * P], ACT.Copy).then_inc(net["u_copied"], 1)
            act.wait_ge(net["u_copied"], t + 1)
            if t >= 2:
                act.wait_ge(net["u_unit"], t - 1)
            act.activation(self.sq[:, t % 2, :], self.qkv[:, t, 0:2 * P], ACT.Square).then_inc(net["u_sq"], 1)
            if t >= 2:
                act.wait_ge(net["u_qT"], t - 1)
                act.activation(self.qT[:, (t - 2) * P:(t - 1) * P], net.bank[6][:, 0:P], ACT.Copy) \
                   .then_inc(net["u_qT_copied"], 1)
        for t in range(NT - 2, NT):
            act.wait_ge(net["u_qT"], t + 1)
            act.activation(self.qT[:, t * P:(t + 1) * P], net.bank[6][:, 0:P], ACT.Copy) \
               .then_inc(net["u_qT_copied"], 1)
        for g in range(NG):
            act.wait_ge(net["u_o"], g + 1)
            if g >= 2:
                act.wait_ge(net["out_ready"], 6 * NG + g - 1)
            act.activation(self.oT[:, g % 2, :], net.bank[4 + g % 2], ACT.Copy).then_inc(net["u_oT_copied"], 1)
            net.norm_act(act, 6 * NG + g)

    def dve(self, dve, ch):
        net = self.net
        net.layer_start(dve, 6)
        dve.wait_ge(net["w6_loaded"], 16 * 5)
        for t in range(NT):
            dve.wait_ge(net["u_sq"], t + 1)
            dve.reduce_sum(self.norm[:, 0, t % 2, :], self.sq[:, t % 2, :].rearrange("p (h d) -> p h d", d=FD),
                           AX.X).then_inc(net["u_sums"], 1)
            r = self.norm[:, 1, t % 2, :]
            dve.wait_ge(net["u_roots"], t + 1)
            ch.link(dve.tensor_scalar(r, r, 1e-12, None, ALU.max))
            ch.link(dve.reciprocal(r, r))
            qk = self.qkv[:, t, 0:2 * P].rearrange("p (h d) -> p h d", d=FD)
            dve.tensor_tensor(out=qk, in0=qk, in1=bc(r, 2, FD), op=ALU.mult).then_inc(net["u_unit"], 1)
        for b in range(2):
            dve.wait_ge(net["u_kv"], b + 1)
            dve.tensor_tensor(out=self.kv[:, b, :], in0=net.bank[7 * (1 - b)][:, 0:P], in1=self.blocks,
                              op=ALU.mult).then_inc(net["u_masked"], 1)
        for g in range(NG):
            net.norm_dve(dve, ch, 6 * NG + g, scalar=self.bp[:, 0:1])

    def pool(self, pool, ch):
        net = self.net
        for t in range(NT):
            pool.wait_ge(net["u_sums"], t + 1)
            pool.tensor_tensor(out=self.norm[:, 1, t % 2, :], in0=self.norm[:, 0, t % 2, :], in1=net.half,
                               op=ALU.pow).then_inc(net["u_roots"], 1)
        for g in range(NG):
            net.norm_pool(pool, 6 * NG + g)


class TaskVectors:
    LAYER = 7

    def __init__(self, net):
        self.net = net
        w = net.late
        w.at = 0
        self.tw1 = w.take(E3, GW)
        self.w1 = w.take(GW)
        self.w2 = w.take(GW)
        self.gw1 = w.take(P)
        self.gw2 = w.take(8)
        self.gb1, self.gb2 = w.take(1), w.take(8)
        self.b1, self.tb1 = w.take(C3), w.take(C3, E3)
        self.b2, self.tb2 = w.take(1), w.take(E3)
        w = net.mid
        w.at = 0
        self.tw2 = w.take(E3, GW)
        a = Arena(net.work)
        self.h = a.take(2, GW)
        self.hsum = a.take(NG)
        self.hb = a.take(2)
        self.hrep = a.take(2, P)
        self.g = a.take(2, 8)
        self.tmp = a.take(C3, E3)
        self.tmp2 = a.take(E3)
        self.m1, self.m2 = a.take(2, GW), a.take(2, GW)
        self.mb1, self.mb2 = a.take(2, C3), a.take(2)
        self.u = a.take(3, GW)

    def pe(self, pe):
        net, bank = self.net, self.net.bank
        xT = net.xT[1]
        net.layer_start(pe, 7)
        pe.wait_ge(net["w7_loaded"], 16 * 12)
        for g in range(NG):
            pe.matmul(bank[4 + g], self.gw1, xT[:, g * GW:(g + 1) * GW], start=True, stop=True) \
              .then_inc(net["t_gate_h"], 1)
        for b in range(2):
            pe.wait_ge(net["t_mean"], b + 1)
            if b == 0:
                pe.wait_ge(net["y_ready"], 7 * NG)
            pe.matmul(bank[b][:, 0:8], self.hrep[:, b, :], self.gw2, start=True, stop=True) \
              .then_inc(net["t_gate"], 1)
        for g in range(NG):
            n = 7 * NG + g
            b = g // 2
            pe.wait_ge(net["t_merged"], b + 1)
            for c in range(C3 + 1):
                i = C3 * g + c
                if c < C3:
                    if i >= 2:
                        pe.wait_ge(net["t_act"], i - 1)
                    pe.matmul(bank[4 + i % 2], self.m1[:, b, c * P:(c + 1) * P], xT[:, g * GW:(g + 1) * GW],
                              start=True, stop=True).then_inc(net["t_up"], 1)
                if c:
                    j = i - 1
                    pe.wait_ge(net["t_act"], j + 1)
                    if c == 1:
                        pe.wait_ge(net["y_ready"], n - 1)
                        pe.wait_ge(net["t_gated"], 2)
                    mm = pe.matmul(bank[g % 2], self.m2[:, b, (c - 1) * P:c * P], self.u[:, j % 3, :],
                                   start=(c == 1), stop=False)
                    mm.then_inc(net["t_down"], 1)
            pe.matmul(bank[g % 2], net.zeros[0:1, 0:P], net.zeros[0:1, :], start=False, stop=True) \
              .then_inc(net["out_ready"], 1)
            net.norm_pe_back(pe, n)

    def act(self, act, ch):
        net = self.net
        net.layer_start(act, 7)
        act.wait_ge(net["w7_loaded"], 16 * 12)
        for g in range(NG):
            act.wait_ge(net["t_gate_h"], g + 1)
            if g >= 2:
                act.wait_ge(net["t_relu"], g - 1)
            act.activation(self.h[:, g % 2, :], net.bank[4 + g], ACT.Relu, bias=self.gb1[:, 0:1],
                           accum_out=self.hsum[:, g:g + 1]).then_inc(net["t_relu"], 1)
        for g in range(NG):
            b = g // 2
            act.wait_ge(net["t_merged"], b + 1)
            for c in range(C3):
                i = C3 * g + c
                act.wait_ge(net["t_up"], i + 1)
                if i >= 3:
                    act.wait_ge(net["t_down"], i - 2)
                act.activation(self.u[:, i % 3, :], net.bank[4 + i % 2], ACT.Gelu_apprx_tanh,
                               bias=self.mb1[:, b, c:c + 1]).then_inc(net["t_act"], 1)

    def dve(self, dve, ch):
        net = self.net
        net.layer_start(dve, 7)
        dve.wait_ge(net["w7_loaded"], 16 * 12)
        for b in range(2):
            dve.wait_ge(net["t_relu"], 2 * b + 2)
            ch.link(dve.tensor_tensor(out=self.hb[:, b:b + 1], in0=self.hsum[:, 2 * b:2 * b + 1],
                                      in1=self.hsum[:, 2 * b + 1:2 * b + 2], op=ALU.add))
            ch.link(dve.memset(self.hrep[:, b, :], 1.0 / 1024))
            dve.tensor_scalar(self.hrep[:, b, :], self.hrep[:, b, :], self.hb[:, b:b + 1], None, ALU.mult) \
               .then_inc(net["t_mean"], 1)
        for b in range(2):
            g = self.g[:, b, :]
            dve.wait_ge(net["t_gate"], b + 1)
            dve.tensor_tensor(out=g, in0=net.bank[b][:, 0:8], in1=self.gb2, op=ALU.add) \
               .then_inc(net["t_gated"], 1)
            dve.wait_ge(net["t_gated"], b + 1)
            ch.link(dve.tensor_tensor(out=self.tmp, in0=self.tb1, in1=bc(g, 1, C3), op=ALU.mult))
            ch.link(dve.tensor_tensor(out=self.tmp2, in0=self.tb2, in1=g, op=ALU.mult))
            ch.link(dve.reduce_sum(self.mb1[:, b, :], self.tmp, AX.X))
            ch.link(dve.tensor_tensor(out=self.mb1[:, b, :], in0=self.mb1[:, b, :], in1=self.b1, op=ALU.add))
            ch.link(dve.reduce_sum(self.mb2[:, b:b + 1], self.tmp2, AX.X))
            ch.link(dve.tensor_tensor(out=self.mb2[:, b:b + 1], in0=self.mb2[:, b:b + 1], in1=self.b2, op=ALU.add))
            m1, m2 = self.m1[:, b, :], self.m2[:, b, :]
            for e in range(E3):
                dve.scalar_tensor_tensor(out=m1, in0=self.tw1[:, e, :], scalar=g[:, e:e + 1],
                                         in1=(m1 if e else self.w1), op0=ALU.mult, op1=ALU.add) \
                   .then_inc(net["t_merge1"], 1)
                if e:
                    dve.wait_ge(net["t_merge2"], b * E3 + e)
                ins = dve.scalar_tensor_tensor(out=m2, in0=self.tw2[:, e, :], scalar=g[:, e:e + 1],
                                               in1=(m2 if e else self.w2), op0=ALU.mult, op1=ALU.add)
                ins.then_inc(net["t_merge2"], 1)
                dve.wait_ge(net["t_merge1"], b * E3 + e + 1)
            dve.wait_ge(net["t_merge2"], (b + 1) * E3)
            dve.tensor_copy(self.tmp2, self.tmp2).then_inc(net["t_merged"], 1)
        for g in range(NG):
            n = 7 * NG + g
            net.norm_dve(dve, ch, n, scalar=self.mb2[:, g // 2:g // 2 + 1])

    def pool(self, pool, ch):
        for g in range(NG):
            self.net.norm_pool(pool, 7 * NG + g)


LAYERS = (QueryAttention, ProductKeys, Lightning, GeluExperts, Forgetting, SiluExperts, LinearAttention, TaskVectors)
CONST_COLS = 4830
LATE_COLS = 9120
MID_COLS = 8900
WORK_COLS = 22850


def build(nc, io, out):
    with ExitStack() as ctx:
        net = Net(nc, ctx, io)
        layers = [make(net) for make in LAYERS]
        query, keys, light, gelu, forget, silu, linear, tasks = layers
        block = ctx.enter_context(nc.Block())

        def load(eng, name, dst, src):
            eng.dma_start(dst, io[src]).then_inc(net[name], 16)

        @block.sync
        def _(sp):
            loads0 = [(net.xT[0][:], "xT"), (query.w, "a0_w"), (query.b, "a0_b"), (query.bv, "a0_bv"),
                      (query.mask, "a0_mask"), (net.ident, "ident"), (net.ones, "ones"),
                      (net.minus_half, "minus_half"), (net.half, "half")]
            loads1 = [(keys.wq, "p_wq"), (keys.wqT, "p_wqT"), (keys.keysT, "p_keysT"), (keys.down, "p_down"),
                      (keys.up, "p_up"), (keys.gamma, "p_gamma"), (keys.beta, "p_beta"), (keys.iota, "p_iota"),
                      (keys.coef_y, "p_coef"), (keys.invn, "p_invn")]
            loads4 = [(forget.wq, "f_wq"), (forget.wk, "f_wk"), (forget.wv, "f_wv"), (forget.wo, "f_wo"),
                      (forget.wf, "f_wf"), (forget.mask_n32, "f_mask_n")]
            loads6 = [(linear.w, "u_w"), (linear.b[0:1, :], "u_b"), (linear.wp, "u_wp"), (linear.bp, "u_bp"),
                      (linear.blocks, "u_blocks")]
            loads2 = [(light.wq, "l_wq"), (light.wqr, "l_wqr"), (light.wk, "l_wk"), (light.wkr, "l_wkr"),
                      (light.wv, "l_wv"), (light.wo, "l_wo"), (light.cos, "l_cos"), (light.sin, "l_sin"),
                      (light.decay, "l_decay"), (light.qdec, "l_qdec"), (light.kdec, "l_kdec"),
                      (light.blk, "l_blk")]
            loads3 = [(gelu.w1, "e1_w1"), (gelu.w2, "e1_w2"), (gelu.b1, "e1_b1"),
                      (gelu.gw[:, 0:E1], "e1_gw"), (gelu.gb[0:1, 0:E1], "e1_gb"), (gelu.b2[0:16, :], "e1_b2"),
                      (gelu.gates.sel[0:16, :, :], "sel15")]
            loads5 = [(silu.wg, "e2_wg"), (silu.wu, "e2_wu"), (silu.wd, "e2_wd"), (silu.wr[:, 0:E2], "e2_wr"),
                      (silu.gates.sel[0:16, :, :], "sel8")]
            loads7 = [(tasks.tw1, "t_tw1"), (tasks.w1, "t_w1"), (tasks.w2, "t_w2"), (tasks.gw1, "t_gw1"),
                      (tasks.gw2, "t_gw2"), (tasks.gb1, "t_gb1"), (tasks.gb2, "t_gb2"), (tasks.b1, "t_b1"),
                      (tasks.tb1, "t_tb1"), (tasks.b2, "t_b2"), (tasks.tb2, "t_tb2")]
            for n, loads in ((0, loads0), (1, loads1), (4, loads4), (6, loads6)):
                for dst, src in loads:
                    load(sp, f"w{n}_loaded", dst, src)
            sp.wait_ge(net["out_ready"], 2 * NG)
            for dst, src in loads2:
                load(sp, "w2_loaded", dst, src)
            for dst, src in loads3[:-1]:
                load(sp, "w3_loaded", dst, src)
            sp.wait_ge(net["out_ready"], 3 * NG)
            load(sp, "w3_loaded", *loads3[-1])
            for dst, src in loads7:
                load(sp, "w7_loaded", dst, src)
            forget.send_splits(sp)
            forget.stack(sp, 0)
            forget.stack(sp, 1)
            for dst, src in loads5:
                load(sp, "w5_loaded", dst, src)
            for n in range(2 * forget.ROUNDS):
                forget.send_maxima(sp, n)
                if n in (3, 5):
                    forget.stack(sp, (n + 1) // 2)
            sp.wait_ge(net["out_ready"], 6 * NG)
            load(sp, "w7_loaded", tasks.tw2, "t_tw2")
            for g in range(NG):
                sp.wait_ge(net["normed"], 7 * NG + g + 1)
                sp.dma_start(out[:, g * GT:(g + 1) * GT, :], net.x[:, g * GT:(g + 1) * GT, :]) \
                  .then_inc(net["stored"], 16)
            sp.wait_ge(net["stored"], 16 * NG)

        @block.tensor
        def _(pe):
            for layer in layers:
                layer.pe(pe)

        @block.scalar
        def _(act):
            ch = Chain(act, net["act_chain"])
            for layer in layers:
                layer.act(act, ch)

        @block.vector
        def _(dve):
            ch = Chain(dve, net["dve_chain"])
            for layer in layers:
                layer.dve(dve, ch)

        @block.gpsimd
        def _(pool):
            ch = Chain(pool, net["pool_chain"])
            for layer in layers:
                layer.pool(pool, ch)


def constants():
    f = np.float32
    i = np.arange(P)
    above = np.where(i[None, :] < i[:, None], f(NEG), f(0))
    slopes = np.array([2.0 ** (-8.0 / 16 * (h + 1)) for h in range(16)], f)
    t = np.arange(P, dtype=f)
    inv = 1.0 / 10000.0 ** (np.arange(0, HD, 2, dtype=np.float64) / HD)
    angle = np.concatenate([np.outer(np.arange(1024, dtype=np.float64), inv)] * 2, axis=-1).T
    sign = np.where(np.arange(HD) < HD // 2, -1.0, 1.0)[:, None]
    diff = t[None, :] - t[:, None]
    decay = np.where(diff[:, None, :] >= 0, np.exp(-slopes[None, :, None] * np.maximum(diff, 0)[:, None, :]), f(0))
    head = np.array([[4 * (2 * (c // 4) + half) + c % 4 for c in range(8)] for half in range(2)])
    rows = np.repeat(head, HD, axis=0)
    sel = np.zeros((16, 15, P), f)
    for e in range(15):
        sel[e, e] = 1
    return {
        "minus_half": np.full((P, 16), -0.5, f), "half": np.full((P, 32), 0.5, f),
        "ident": np.eye(P, dtype=f), "ones": np.ones((P, P), f), "a0_mask": above.astype(f),
        "f_mask_n": np.ascontiguousarray(above.T).astype(f),
        "p_iota": np.broadcast_to(np.arange(PKEYS, dtype=f), (P, PKEYS)),
        "p_coef": np.broadcast_to(8 - np.arange(8, dtype=f), (P, 8, 8)),
        "p_invn": np.full((P, P), 1.0 / TOK, f),
        "l_cos": np.tile(np.cos(angle), (2, 1)).astype(f), "l_sin": np.tile(np.sin(angle) * sign, (2, 1)).astype(f),
        "l_decay": decay.astype(f),
        "l_qdec": np.exp(-slopes[rows][:, :, None] * (t + 1)[None, None, :]).astype(f),
        "l_kdec": np.exp(-slopes[None, :] * (P - 1 - t)[:, None]).astype(f),
        "l_blk": np.exp(-slopes[rows] * f(P)).astype(f),
        "sel15": sel, "sel8": sel[:, 0:8],
        "u_blocks": np.kron(np.eye(16), np.ones((8, 8))).astype(f),
    }


def kernel(**inputs):
    import concourse.bacc as bacc
    from concourse.bass_utils import run_bass_kernel_spmd as run

    w = {k: np.asarray(v) for k, v in inputs.items()}

    def tiles(a, n):
        return a.reshape(n, P, -1).transpose(1, 0, 2)

    a0, pk, l1, e1 = "L0_attn_", "L0_ffn_", "L1_attn_", "L1_ffn_"
    f2, e2, u3, t3 = "L2_attn_", "L2_ffn_", "L3_attn_", "L3_ffn_"
    arr = dict(constants())
    arr["xT"] = w[a0 + "minibatch"].reshape(TOK, P).T
    arr["a0_w"] = np.stack([w[a0 + "Wq"], w[a0 + "Wk"], w[a0 + "Wv"]], axis=1)
    arr["a0_b"] = np.stack([w[a0 + "bq"], w[a0 + "bk"]], axis=1)
    arr["a0_bv"] = np.broadcast_to(w[a0 + "bv"], (P, P))

    wq = w[pk + "w_q"]
    arr["p_wq"] = wq
    arr["p_wqT"] = wq.reshape(P, PC, P).transpose(2, 1, 0)
    arr["p_keysT"] = w[pk + "keys"].transpose(3, 2, 0, 1).reshape(P, PC, PKEYS)
    arr["p_down"] = w[pk + "down_embed"].T
    arr["p_up"] = tiles(w[pk + "up_embed"], 8)
    arr["p_gamma"] = w[pk + "bn_gamma"].reshape(PC, P).T
    arr["p_beta"] = w[pk + "bn_beta"].reshape(PC, P).T

    swap = np.concatenate([np.arange(32, 64), np.arange(0, 32)])
    lq = w[l1 + "Wq"].reshape(2, 2, 4, HD, P)
    lk = w[l1 + "Wk"].reshape(2, 2, HD, P)

    def qside(a):
        return a.transpose(4, 0, 2, 1, 3).reshape(P, 8, P)

    def kside(a):
        return a.transpose(3, 0, 1, 2).reshape(P, 2, P)

    arr["l_wq"], arr["l_wqr"] = qside(lq), qside(lq[:, :, :, swap])
    arr["l_wk"], arr["l_wkr"] = kside(lk), kside(lk[:, :, swap])
    arr["l_wv"] = w[l1 + "Wv"].T
    arr["l_wo"] = w[l1 + "Wo"].reshape(P, 2, 2, 4, HD).transpose(2, 4, 1, 3, 0).reshape(P, 8, P)

    rw1 = w[e1 + "rW1"].transpose(1, 0, 2).reshape(P, E1 * 2 * P)
    arr["e1_w1"] = np.concatenate([w[e1 + "sW1"][0], rw1], axis=1)
    arr["e1_w2"] = tiles(np.concatenate([w[e1 + "sW2"][0], w[e1 + "rW2"].reshape(-1, P)], axis=0), C1)
    arr["e1_b1"] = np.concatenate([w[e1 + "sb1"].reshape(-1), w[e1 + "rb1"].reshape(-1)]).reshape(C1, P).T
    arr["e1_b2"] = np.concatenate([w[e1 + "rb2"], w[e1 + "sb2"]], axis=0)
    arr["e1_gw"], arr["e1_gb"] = w[e1 + "gW"], w[e1 + "gb"].reshape(1, E1)

    arr["f_wq"], arr["f_wk"] = w[f2 + "Wq"], w[f2 + "Wk"]
    arr["f_wv"], arr["f_wo"], arr["f_wf"] = w[f2 + "Wv"], w[f2 + "Wo"], w[f2 + "Wf"]

    def experts(routed, shared):
        return np.concatenate([routed.transpose(1, 0, 2).reshape(P, -1), shared], axis=1)

    arr["e2_wg"] = experts(w[e2 + "Wg"], w[e2 + "Sg"])
    arr["e2_wu"] = experts(w[e2 + "Wu"], w[e2 + "Su"])
    arr["e2_wd"] = tiles(np.concatenate([w[e2 + "Wd"].reshape(-1, P), w[e2 + "Sd"]], axis=0), C2)
    arr["e2_wr"] = w[e2 + "Wr"]

    arr["u_w"], arr["u_b"] = w[u3 + "qkv_w"], w[u3 + "qkv_b"].reshape(1, 3 * P)
    arr["u_wp"], arr["u_bp"] = w[u3 + "proj_w"], w[u3 + "proj_b"].reshape(P, 1)

    arr["t_tw1"] = w[t3 + "TW1"].transpose(2, 0, 1)
    arr["t_w1"] = w[t3 + "W1"].T
    arr["t_w2"] = w[t3 + "W2"].T.reshape(C3, P, P).transpose(1, 0, 2)
    arr["t_tw2"] = w[t3 + "TW2"].transpose(2, 0, 1).reshape(C3, P, E3, P).transpose(1, 2, 0, 3)
    arr["t_gw1"], arr["t_gw2"] = w[t3 + "gate_w1"].T, w[t3 + "gate_w2"].T
    arr["t_gb1"] = w[t3 + "gate_b1"].reshape(P, 1)
    arr["t_gb2"] = np.broadcast_to(w[t3 + "gate_b2"], (P, E3))
    arr["t_b1"] = w[t3 + "b1"].reshape(C3, P).T
    arr["t_tb1"] = w[t3 + "Tb1"].reshape(E3, C3, P).transpose(2, 1, 0)
    arr["t_b2"] = w[t3 + "b2"].reshape(P, 1)
    arr["t_tb2"] = w[t3 + "Tb2"].T

    shaped = {
        "e1_w1": (P, C1, P), "e2_wg": (P, C2, P), "e2_wu": (P, C2, P), "t_w2": (P, GW), "t_tw2": (P, E3, GW)}
    nc = bacc.Bacc("TRN2", target_bir_lowering=False, num_devices=1)
    arrays, io = {}, {}
    for name, a in arr.items():
        a = np.ascontiguousarray(a.reshape(shaped.get(name, a.shape)))
        arrays[f"in_{name}"] = a
        io[name] = nc.dram_tensor(f"in_{name}", a.shape, mybir.dt.from_np(a.dtype), kind="ExternalInput").ap()
    out = nc.dram_tensor("out_x", (P, NT, P), F32, kind="ExternalOutput").ap()
    build(nc, io, out)
    r = run(nc, [arrays], core_ids=[0])
    return r.results[0]["out_x"].transpose(1, 0, 2).reshape(2, 1024, P)
```

```python
from contextlib import ExitStack

import numpy as np

import concourse.bass as bass
from concourse import mybir

F32 = mybir.dt.float32
BF16 = mybir.dt.bfloat16
U32 = mybir.dt.uint32
ALU = mybir.AluOpType
ACT = mybir.ActivationFunctionType
AX = mybir.AxisListType

P = 128
NT = 16
NG = 4
GT = 4
GW = 512
TOK = 2048
LN_EPS = 1e-5
NEG = -1.0e30

PH, PKEYS, PTOP = 8, 32, 8
PC = 2 * PH
NKV, HD = 4, 64
FH, FD = 16, 8
E1, C1S, C1 = 15, 4, 34
E2, C2 = 8, 18
E3, C3 = 8, 4


class Arena:

    def __init__(self, tensor):
        self.tensor, self.at = tensor, 0

    def take(self, *shape):
        n = int(np.prod(shape))
        ap = self.tensor[:, self.at:self.at + n]
        self.at += n
        assert self.at <= self.tensor.shape[1], (self.at, self.tensor.shape)
        if len(shape) == 2:
            ap = ap.rearrange("p (a b) -> p a b", a=shape[0])
        if len(shape) == 3:
            ap = ap.rearrange("p (a b c) -> p a b c", a=shape[0], b=shape[1])
        return ap


class Chain:

    def __init__(self, engine, semaphore):
        self.engine, self.semaphore, self.count = engine, semaphore, 0

    def link(self, ins):
        self.count += 1
        ins.then_inc(self.semaphore, 1)
        self.engine.wait_ge(self.semaphore, self.count)


def bc(ap, axis, n):
    a = ap.unsqueeze(axis)
    shape = list(a.shape)
    shape[axis] = n
    return a.broadcast_to(shape)


def flat(ap):
    return ap.rearrange("p a b -> p (a b)")


class Net:

    def __init__(self, nc, ctx, io):
        self.nc, self.ctx, self.io = nc, ctx, io
        self.signals = {}

        def sb(name, n):
            return ctx.enter_context(nc.sbuf_tensor(name, [P, n], F32))

        self.pairs = [ctx.enter_context(nc.psum_tensor(f"banks{2 * i}{2 * i + 1}", [P, 2 * GW], F32))
                      for i in range(4)]
        self.bank = [self.pairs[i // 2][:, (i % 2) * GW:(i % 2 + 1) * GW] for i in range(8)]
        self.xT = [sb("xT0", TOK), sb("xT1", TOK)]
        self.x = sb("x_tokens", TOK)[:, :].rearrange("p (t d) -> p t d", t=NT)
        self.yT = sb("yT", GW)
        self.stats = sb("stats", GT * 6)[:, :].rearrange("p (a b) -> p a b", a=GT)
        self.moments = sb("moments", GT * 2)[:, :].rearrange("p (a b) -> p a b", a=GT)
        self.rstd, self.var = sb("rstd", GT), sb("variance_eps", GT)
        self.const = Arena(sb("constants", CONST_COLS))
        self.late = Arena(sb("late_weights", LATE_COLS))
        self.mid = Arena(sb("expert_weights", MID_COLS))
        self.work = sb("work", WORK_COLS)
        self.ident = self.const.take(P)
        self.ones = self.const.take(P)
        self.zeros = ctx.enter_context(nc.sbuf_tensor("zeros", [1, GW], BF16))
        self.minus_half, self.half = self.const.take(16), self.const.take(32)
        self.pick = self.const.take(16)
        self.identb = self.const.take(P // 2).bitcast(BF16)
        self.minus_half4 = self.minus_half[:, 0:GT]

    def __getitem__(self, name):
        if name not in self.signals:
            self.signals[name] = self.ctx.enter_context(self.nc.semaphore(name))
        return self.signals[name]

    def norm_pe_back(self, pe, n):
        pe.wait_ge(self["y_ready"], n + 1)
        if n:
            pe.wait_ge(self["normed"], n)
        for k in range(GT):
            mm = pe.transpose(self.bank[2][:, k * P:(k + 1) * P], self.yT[:, k * P:(k + 1) * P], self.ident)
        mm.then_inc(self["y_tokens"], 1)

    def norm_pe_forth(self, pe, n):
        g = n % NG
        pe.wait_ge(self["normed"], n + 1)
        if n:
            pe.wait_ge(self["xT_done"], n)
        for k in range(GT):
            mm = pe.transpose(self.bank[3][:, k * P:(k + 1) * P], self.x[:, g * GT + k, :], self.ident)
        mm.then_inc(self["xT_in_psum"], 1)

    def norm_act(self, act, n):
        g = n % NG
        act.wait_ge(self["xT_in_psum"], n + 1)
        act.activation(self.xT[(n // NG + 1) % 2][:, g * GW:(g + 1) * GW], self.bank[3], ACT.Copy) \
           .then_inc(self["xT_done"], 1)

    def norm_dve(self, dve, ch, n, **how):
        self.norm_dve_y(dve, n, **how)
        self.norm_dve_rest(dve, ch, n)

    def norm_dve_y(self, dve, n, scalar=0.0, op=ALU.add, twice=False, bank=None):
        g = n % NG
        xT = self.xT[(n // NG) % 2][:, g * GW:(g + 1) * GW]
        out = self.bank[g % 2 if bank is None else bank]
        dve.wait_ge(self["out_ready"], n + 1)
        if twice:
            ins = dve.scalar_tensor_tensor(out=self.yT[:], in0=xT, scalar=2.0, in1=out, op0=ALU.mult, op1=ALU.add)
        else:
            ins = dve.scalar_tensor_tensor(out=self.yT[:], in0=out, scalar=scalar, in1=xT, op0=op, op1=ALU.add)
        ins.then_inc(self["y_ready"], 1)

    def norm_dve_rest(self, dve, ch, n):
        self.norm_dve_stats(dve, ch, n)
        self.norm_dve_apply(dve, n)

    def norm_dve_stats(self, dve, ch, n):
        dve.wait_ge(self["y_tokens"], n + 1)
        for k in range(GT):
            ins = dve.bn_stats(self.stats[:, k, :], self.bank[2][:, k * P:(k + 1) * P])
        ch.link(ins)
        for k in range(GT):
            ins = dve.bn_aggr(self.moments[:, k, :], self.stats[:, k, :])
        ch.link(ins)
        dve.tensor_scalar(self.var[:], self.moments[:, :, 1], LN_EPS, None, ALU.add).then_inc(self["variance"], 1)

    def norm_dve_apply(self, dve, n):
        g = n % NG
        dve.wait_ge(self["rstd_done"], n + 1)
        for k in range(GT):
            ins = dve.tensor_scalar(self.x[:, g * GT + k, :], self.bank[2][:, k * P:(k + 1) * P],
                                    self.moments[:, k, 0:1], self.rstd[:, k:k + 1], ALU.subtract, ALU.mult)
        ins.then_inc(self["normed"], 1)

    def norm_pool(self, pool, n):
        pool.wait_ge(self["variance"], n + 1)
        pool.tensor_tensor(out=self.rstd[:], in0=self.var[:], in1=self.minus_half4, op=ALU.pow) \
            .then_inc(self["rstd_done"], 1)

    def layer_start(self, eng, layer):
        if layer:
            eng.wait_ge(self["xT_done"], NG * layer)


class QueryAttention:
    LAYER = 0

    def __init__(self, net):
        self.net = net
        a = Arena(net.work)
        self.qT, self.kT = a.take(TOK), a.take(TOK)
        self.v = a.take(NT, P)
        self.exp = a.take(2, 1024)
        self.v_scaled = a.take(2, P)
        self.negmax = a.take(2 * NT)
        self.total = a.take(2 * NT)
        w = net.const
        self.w = a.take(3, P)
        self.b = a.take(2)
        self.bv = a.take(P)
        self.mask = net.mask = w.take(P)

    def pv_wait(self, eng, n):
        if n % 8 == 7:
            eng.wait_ge(self.net["out_ready"], 2 * (n // 8) + 2)
        else:
            eng.wait_ge(self.net["a0_pv_done"], n + 1 - n // 8)

    def pe(self, pe):
        net, bank = self.net, self.net.bank
        xT = net.xT[0]
        pe.wait_ge(net["w0_loaded"], 16 * 10)
        for i in range(2 * NG):
            if i >= 2:
                pe.wait_ge(net["a0_qk_copied"], i - 1)
            pe.matmul(bank[4 + i % 2], self.w[:, i // NG, :], xT[:, (i % NG) * GW:(i % NG + 1) * GW],
                      start=True, stop=True).then_inc(net["a0_qk_psum"], 1)
        for g in range(NG):
            if g >= 2:
                pe.wait_ge(net["a0_v_copied"], g - 1)
            for k in range(GT):
                t = g * GT + k
                mm = pe.matmul(bank[6 + g % 2][:, k * P:(k + 1) * P], xT[:, t * P:(t + 1) * P],
                               self.w[:, 2, :], start=True, stop=True)
            mm.then_inc(net["a0_v_psum"], 1)
        pe.wait_ge(net["a0_qk_copied"], 2 * NG)
        pe.wait_ge(net["a0_v_copied"], NG)

        def scores(n):
            b, j = divmod(n, 8)
            if n >= 2:
                pe.wait_ge(net["a0_exp_done"], n - 1)
            for half in range(j // 4, 2):
                lo = max(P * j, GW * half)
                mm = pe.matmul(net.pairs[2 + n % 2][:, lo:GW * (half + 1)],
                               self.kT[:, n * P:(n + 1) * P],
                               self.qT[:, 1024 * b + lo:1024 * b + GW * (half + 1)], start=True, stop=True)
            mm.then_inc(net["a0_scores"], 1)

        def values(n):
            b, j = divmod(n, 8)
            pe.wait_ge(net["a0_v_scaled"], n + 1)
            for half in range(j // 4, 2):
                if j == 0 and b:
                    pe.wait_ge(net["y_ready"], half + 1)
                lo = max(P * j, GW * half)
                mm = pe.matmul(bank[half][:, lo - GW * half:GW], self.v_scaled[:, n % 2, :],
                               self.exp[:, n % 2, lo:GW * (half + 1)], start=(j == 0), stop=(j == 3 + 4 * half))
                if j == 3 + 4 * half:
                    mm.then_inc(net["out_ready"], 1)
            if j != 7:
                mm.then_inc(net["a0_pv_done"], 1)

        scores(0)
        for n in range(NT):
            if n + 1 < NT:
                scores(n + 1)
            if n in (8, 9):
                net.norm_pe_back(pe, n - 8)
            values(n)
            if n in (8, 9):
                net.norm_pe_forth(pe, n - 8)
        for g in (2, 3):
            net.norm_pe_back(pe, g)
            net.norm_pe_forth(pe, g)

    def act(self, act, ch):
        net = self.net
        act.wait_ge(net["w0_loaded"], 16 * 10)
        for i in range(2 * NG):
            act.wait_ge(net["a0_qk_psum"], i + 1)
            dst = (self.qT, self.kT)[i // NG][:, (i % NG) * GW:(i % NG + 1) * GW]
            act.activation(dst, net.bank[4 + i % 2], ACT.Identity, bias=self.b[:, i // NG:i // NG + 1]) \
               .then_inc(net["a0_qk_copied"], 1)
        for n in range(NT):
            j = n % 8
            act.wait_ge(net["a0_negmax"], n + 1)
            if n >= 2:
                self.pv_wait(act, n - 2)
            act.activation(self.exp[:, n % 2, P * j:1024], net.pairs[2 + n % 2][:, P * j:1024], ACT.Exp,
                           bias=self.negmax[:, n:n + 1], accum_out=self.total[:, n:n + 1]) \
               .then_inc(net["a0_exp_done"], 1)
            if n in (8, 9):
                net.norm_act(act, n - 8)
        net.norm_act(act, 2)
        net.norm_act(act, 3)

    def dve(self, dve, ch):
        net = self.net
        dve.wait_ge(net["w0_loaded"], 16 * 10)
        for g in range(NG):
            dve.wait_ge(net["a0_v_psum"], g + 1)
            dve.tensor_tensor(out=self.v[:, g * GT:(g + 1) * GT, :],
                              in0=net.bank[6 + g % 2].rearrange("p (t d) -> p t d", t=GT),
                              in1=bc(self.bv, 1, GT), op=ALU.add).then_inc(net["a0_v_copied"], 1)

        def maxima(n):
            j = n % 8
            s = net.pairs[2 + n % 2]
            dve.wait_ge(net["a0_scores"], n + 1)
            ch.link(dve.tensor_tensor(out=s[:, P * j:P * j + P], in0=s[:, P * j:P * j + P], in1=self.mask,
                                      op=ALU.add))
            ch.link(dve.reduce_max(self.negmax[:, NT + n:NT + n + 1], s[:, P * j:1024], AX.X))
            dve.tensor_scalar(self.negmax[:, n:n + 1], self.negmax[:, NT + n:NT + n + 1], -1.0, None,
                              ALU.mult).then_inc(net["a0_negmax"], 1)

        maxima(0)
        for n in range(NT):
            if n + 1 < NT:
                maxima(n + 1)
            if n in (8, 9):
                net.norm_dve_rest(dve, ch, n - 8)
            if n == 8:
                net.norm_dve_y(dve, 1, twice=True)
            dve.wait_ge(net["a0_exp_done"], n + 1)
            ch.link(dve.tensor_scalar(self.total[:, NT + n:NT + n + 1], self.total[:, n:n + 1],
                                      float(np.float32(np.sqrt(128.0))), None, ALU.mult))
            ch.link(dve.reciprocal(self.total[:, NT + n:NT + n + 1], self.total[:, NT + n:NT + n + 1]))
            if n >= 2:
                self.pv_wait(dve, n - 2)
            dve.tensor_scalar(self.v_scaled[:, n % 2, :], self.v[:, n, :], self.total[:, NT + n:NT + n + 1],
                              None, ALU.mult).then_inc(net["a0_v_scaled"], 1)
            if n == 7:
                net.norm_dve_y(dve, 0, twice=True)
        net.norm_dve(dve, ch, 2, twice=True)
        net.norm_dve(dve, ch, 3, twice=True)

    def pool(self, pool, ch):
        pool.memset(self.net.zeros[:], 0.0).then_inc(self.net["tables_made"], 1)
        pool.wait_ge(self.net["w0_loaded"], 16 * 10)
        pool.tensor_copy(self.net.identb, self.net.ident).then_inc(self.net["tables_made"], 1)
        for g in range(NG):
            self.net.norm_pool(pool, g)


class ProductKeys:
    LAYER = 1
    SIM = 3
    OUT, BACK = 2, 5
    Y, STATS, APPLY = 5, 6, 7
    STEPS = ((0,), (1,), (2,), (3,), (4,), (5,), (6, 7), ())

    def __init__(self, net):
        self.net = net
        w = net.late
        w.at = 0
        self.wq = w.take(TOK)
        self.wqT = w.take(PC, P)
        self.keysT = w.take(PC, PKEYS)
        self.down = w.take(1024)
        self.up = w.take(8, P)
        self.gamma, self.beta = w.take(PC), w.take(PC)
        self.iota32 = net.const.take(PKEYS * PTOP)
        self.coef_y = net.const.take(PC // 2, PTOP)
        self.invn = net.const.take(P)
        a = Arena(net.work)
        self.xc, self.xcT = a.take(NT, P), a.take(TOK)
        self.z = self.xc
        self.cov = a.take(P)
        self.meancol = a.take(2)
        self.identb = a.take(P // 2).bitcast(BF16)
        self.scale = a.take(2, PC)
        self.ks = a.take(PC, PKEYS)
        self.m = a.take(512)
        self.brow = a.take(512)
        self.sim = a.take(2, PC * PKEYS)
        self.top = a.take(PC, PTOP)
        self.idx = a.take(PC * PTOP).bitcast(U32)
        self.idxb = a.take(PC * PTOP // 2).bitcast(BF16)
        self.coef = a.take(PC * PTOP // 2).bitcast(BF16).rearrange("p (c j) -> p c j", c=PC)
        self.iota = a.take(PKEYS * PTOP // 2).bitcast(BF16).rearrange("p (v j) -> p v j", v=PKEYS)
        self.spread = a.take(1024).bitcast(BF16).rearrange("p (q e) -> p q e", q=2)
        self.sums, self.left, self.chosen, self.prob = (a.take(PH, PTOP, PTOP) for _ in range(4))
        self.best, self.count = a.take(PH, PTOP), a.take(PH, PTOP)
        self.d8, self.e8 = a.take(PC, PTOP), a.take(PC, PTOP)
        self.z8, self.rz8 = a.take(PH), a.take(PH)
        self.dd, self.ed = a.take(PC, PKEYS), a.take(2, PC * PKEYS)
        self.fx = a.take(2, PH * PKEYS)
        self.onehot = a.take(PC * PTOP * PKEYS // 2).bitcast(BF16).rearrange("p (c v j) -> p c v j", c=PC, v=PKEYS)
        self.half4 = a.take(1024).bitcast(BF16).rearrange("p (c v j) -> p c v j", c=PC, v=PKEYS)
        self.half2 = a.take(512).bitcast(BF16).rearrange("p (c v j) -> p c v j", c=PC, v=PKEYS)
        self.nq = [a.take(256).bitcast(BF16) for _ in range(2)]
        self.nqT = [a.take(256).bitcast(BF16) for _ in range(2)]
        self.expo = self.xc.rearrange("p (a t) d -> p a (t d)", a=2)
        self.wgt = a.take(2, 1024)
        m = net.mid
        m.at = 0
        self.gelu, self.gw = m.take(8, P), m.take(8, GW)
        self.spread32 = m.take(2048)

    def pe(self, pe):
        net, bank, x = self.net, self.net.bank, self.net.x
        xT = net.xT[1]
        net.layer_start(pe, 1)
        pe.wait_ge(net["w1_loaded"], 16 * 11)
        pe.wait_ge(net["tables_made"], 1)
        for t in range(NT):
            mm = pe.matmul(bank[4][:, 0:P], self.invn, x[:, t, :], start=(t == 0), stop=(t == NT - 1))
        mm.then_inc(net["p_mean"], 1)
        pe.wait_ge(net["p_centred"], 1)
        for t in range(NT):
            mm = pe.matmul(bank[5][:, 0:P], self.xc[:, t, :], self.xc[:, t, :], start=(t == 0), stop=(t == NT - 1))
        mm.then_inc(net["p_cov"], 1)
        pe.wait_ge(net["p_cov_scaled"], 1)
        for i in range(4):
            mm = pe.matmul(bank[4 + i], self.cov, self.wq[:, i * GW:(i + 1) * GW], start=True, stop=True)
            mm.then_inc(net["p_cw"], 1)
        pe.wait_ge(net["p_z"], 4)
        z = self.z.rearrange("p a b -> p (a b)")
        for c in range(PC):
            mm = pe.matmul(bank[0][:, c:c + 1], z[:, c * P:(c + 1) * P], net.ones[:, 0:1], start=True, stop=True)
        mm.then_inc(net["p_var"], 1)
        for c in range(PC):
            mm = pe.matmul(bank[3][0:1, c * PKEYS:(c + 1) * PKEYS], self.beta[:, c:c + 1], self.keysT[:, c, :],
                           start=True, stop=True)
        mm.then_inc(net["p_beta"], 1)
        pe.wait_ge(net["p_keys_scaled"], 1)
        for c in range(PC):
            mm = pe.matmul(bank[1][:, c * PKEYS:(c + 1) * PKEYS], self.wqT[:, c, :], self.ks[:, c, :],
                           start=True, stop=True)
        mm.then_inc(net["p_m"], 1)
        pe.wait_ge(net["p_m_copied"], 2)
        pe.wait_ge(net["p_cast"], 1)

        self.sim_pe(pe, 0)
        self.turn_pe(pe, 0)
        self.rank_pe(pe, 0, 0)
        self.sim_pe(pe, 1)
        for t in range(NT):
            g, k = divmod(t, GT)
            for h in range(PH):
                if h + 1 < PH:
                    self.rank_pe(pe, t, h + 1)
                elif t + 1 < NT:
                    self.turn_pe(pe, t + 1)
                    self.rank_pe(pe, t + 1, 0)
                self.sum_pe(pe, t, h)
                if h == self.SIM and t + 2 < NT:
                    self.sim_pe(pe, t + 2)
                if h < 2:
                    self.down_pe(pe, t, h)
                if k == 0 and t and h == self.OUT:
                    self.out_pe(pe, g - 1)
                if k == 0 and t and h == self.BACK:
                    pe.wait_ge(net["p_sim_copied"], min(NT, t + 3))
                    net.norm_pe_back(pe, NG + g - 1)
            if k == 0 and t:
                net.norm_pe_forth(pe, NG + g - 1)
        self.out_pe(pe, NG - 1)
        net.norm_pe_back(pe, 2 * NG - 1)
        net.norm_pe_forth(pe, 2 * NG - 1)

    def turn_pe(self, pe, t):
        net = self.net
        pe.wait_ge(net["p_routed"], t + 1)
        pe.wait_ge(net["p_sim_copied"], min(NT, t + 2) if t else 1)
        pe.wait_ge(net["normed"], NG + max(0, (t - 1) // GT))
        for c in range(4):
            mm = pe.transpose(net.bank[2].bitcast(BF16)[:, c * P:(c + 1) * P],
                              self.nq[t % 2][:, c * P:(c + 1) * P], self.identb)
        mm.then_inc(net["p_nqT"], 1)
        pe.wait_ge(net["p_nqT_copied"], t + 1)

    def sum_pe(self, pe, t, h):
        net, bank = self.net, self.net.bank
        pe.wait_ge(net["p_weights"], t * PH + h + 1)
        if h == 0:
            if t:
                pe.wait_ge(net["p_gw"], t)
            for half in range(2):
                pe.matmul(bank[6 + half], net.zeros[0:1, 0:P], net.zeros[0:1, :], start=True, stop=False)
        for c in range(8):
            mm = pe.matmul(net.pairs[3][:, c * P:(c + 1) * P], self.wgt[:, h % 2, c * P:(c + 1) * P],
                           net.ident, start=False, stop=False, skip_group_check=True)
        if h == PH - 1:
            for half in range(2):
                mm = pe.matmul(bank[6 + half], net.zeros[0:1, 0:P], net.zeros[0:1, :], start=False, stop=True)
        mm.then_inc(net["p_summed"], 1)

    def down_pe(self, pe, t, half):
        net = self.net
        if t or half:
            pe.wait_ge(net["p_gelu"], 2 * t + half)
        pe.wait_ge(net["xT_done"], NG + max(0, (t - 1) // GT))
        for c in range(4):
            mm = pe.matmul(net.bank[3][:, c * P:(c + 1) * P], self.down[:, (4 * half + c) * P:(4 * half + c + 1) * P],
                           net.xT[1][:, t * P:(t + 1) * P], start=True, stop=True)
        mm.then_inc(net["p_h"], 1)

    def out_pe(self, pe, g):
        net = self.net
        pe.wait_ge(net["p_gw"], GT * (g + 1))
        pe.wait_ge(net["p_gelu"], min(2 * NT, 2 * (GT * (g + 1) + 1)))
        for c in range(8):
            mm = pe.matmul(net.bank[3], self.up[:, c, :], self.gw[:, c, :], start=(c == 0), stop=(c == 7))
        mm.then_inc(net["out_ready"], 1)

    def sim_pe(self, pe, t):
        net = self.net
        if t:
            pe.wait_ge(net["p_nqT_copied"], max(1, t - 1))
        pe.matmul(net.bank[2], self.xcT[:, t * P:(t + 1) * P], self.m, start=True, stop=False)
        pe.matmul(net.bank[2], net.ones[0:1, :], self.brow[0:1, :], start=False, stop=True) \
          .then_inc(net["p_sim"], 1)

    def rank_pe(self, pe, t, h):
        net = self.net
        i = t * PH + h
        if i >= 2:
            pe.wait_ge(net["p_weights"], i - 1)
        pair = net.pairs[(2, 0)[h % 2]]
        for half in range(2):
            mm = pe.matmul(pair[:, half * GW:(half + 1) * GW], self.nqT[t % 2][:, h // 2 * P:(h // 2 + 1) * P],
                           self.spread[:, h % 2, half * GW:(half + 1) * GW], start=True, stop=True)
        mm.then_inc(net["p_ranks"], 1)

    def act(self, act, ch):
        net = self.net
        net.layer_start(act, 1)
        act.wait_ge(net["p_m"], 1)
        act.activation(self.m, net.bank[1], ACT.Copy).then_inc(net["p_m_copied"], 1)
        act.wait_ge(net["p_beta"], 1)
        act.activation(self.brow[0:1, :], net.bank[3][0:1, :], ACT.Copy).then_inc(net["p_m_copied"], 1)
        act.wait_ge(net["p_cast"], 1)
        self.sim_act(act, 0)
        self.exp_act(act, 0)
        self.turned_act(act, 0)
        self.sim_act(act, 1)
        for t in range(NT):
            g, k = divmod(t, GT)
            if t + 1 < NT:
                self.exp_act(act, t + 1)
            if k == 1 and g:
                net.norm_act(act, NG + g - 1)
            for half in range(2):
                act.wait_ge(net["p_h"], 2 * t + half + 1)
                if t:
                    act.wait_ge(net["p_gw"], t)
                act.activation(flat(self.gelu)[:, half * GW:(half + 1) * GW], net.bank[3], ACT.Gelu_apprx_tanh) \
                   .then_inc(net["p_gelu"], 1)
            if t + 2 < NT:
                self.sim_act(act, t + 2)
            if t + 1 < NT:
                self.turned_act(act, t + 1)
        net.norm_act(act, 2 * NG - 1)

    def turned_act(self, act, t):
        net = self.net
        act.wait_ge(net["p_nqT"], t + 1)
        if t >= 2:
            act.wait_ge(net["p_ranks"], PH * (t - 1))
        act.activation(self.nqT[t % 2], net.bank[2].bitcast(BF16)[:, 0:GW], ACT.Copy) \
           .then_inc(net["p_nqT_copied"], 1)

    def sim_act(self, act, t):
        net = self.net
        act.wait_ge(net["p_sim"], t + 1)
        if t >= 2:
            act.wait_ge(net["p_routed"], t - 1)
        act.activation(self.sim[:, t % 2, :], net.bank[2], ACT.Copy).then_inc(net["p_sim_copied"], 1)

    def exp_act(self, act, t):
        net = self.net
        if t >= 2:
            act.wait_ge(net["p_pairs"], PH * (t - 1))
        act.wait_ge(net["p_diffs"], t + 1)
        act.activation(flat(self.e8), flat(self.d8), ACT.Exp).then_inc(net["p_e8"], 1)
        act.activation(self.ed[:, t % 2, :], flat(self.dd), ACT.Exp).then_inc(net["p_ed"], 1)

    def dve(self, dve, ch):
        net, x = self.net, self.net.x
        net.layer_start(dve, 1)
        dve.wait_ge(net["w1_loaded"], 16 * 11)
        dve.wait_ge(net["p_mean"], 1)
        ch.link(dve.tensor_tensor(out=self.xc, in0=x, in1=bc(net.bank[4][:, 0:P], 1, NT), op=ALU.subtract))
        ch.link(dve.reduce_sum(self.meancol[:, 0:1], net.xT[1][:], AX.X))
        ch.link(dve.tensor_scalar(self.meancol[:, 1:2], self.meancol[:, 0:1], 1.0 / TOK, None, ALU.mult))
        dve.tensor_scalar(self.xcT, net.xT[1][:], self.meancol[:, 1:2], None, ALU.subtract) \
           .then_inc(net["p_centred"], 1)
        dve.wait_ge(net["p_cov"], 1)
        dve.tensor_scalar(self.cov, net.bank[5][:, 0:P], 1.0 / TOK, None, ALU.mult).then_inc(net["p_cov_scaled"], 1)
        z = self.z.rearrange("p a b -> p (a b)")
        for i in range(4):
            dve.wait_ge(net["p_cw"], i + 1)
            dve.tensor_tensor(out=z[:, i * GW:(i + 1) * GW], in0=net.bank[4 + i], in1=self.wq[:, i * GW:(i + 1) * GW],
                              op=ALU.mult).then_inc(net["p_z"], 1)
        dve.wait_ge(net["p_var"], 1)
        dve.tensor_scalar(self.scale[:, 0, :], net.bank[0][:, 0:PC], 0.0, 1e-5, ALU.max, ALU.add) \
           .then_inc(net["p_varsum"], 1)
        dve.wait_ge(net["p_rstd"], 1)
        ch.link(dve.tensor_tensor(out=self.scale[:, 1, :], in0=self.scale[:, 1, :], in1=self.gamma, op=ALU.mult))
        dve.tensor_tensor(out=self.ks, in0=self.keysT, in1=bc(self.scale[:, 1, :], 2, PKEYS), op=ALU.mult) \
           .then_inc(net["p_keys_scaled"], 1)
        dve.tensor_copy(self.coef[:, PH:PC, :], self.coef_y)
        dve.tensor_copy(self.iota.rearrange("p v j -> p (v j)"), self.iota32)
        dve.tensor_copy(self.identb, net.ident)
        dve.tensor_copy(self.spread.rearrange("p q e -> p (q e)"), self.spread32).then_inc(net["p_cast"], 1)
        dve.wait_ge(net["p_cast"], 1)
        for step in range(8):
            self.route(dve, ch, 0, step)
        for t in range(NT):
            g, k = divmod(t, GT)
            for h in range(PH):
                if k == 0 and t:
                    n = NG + g - 1
                    if h == self.Y:
                        net.norm_dve_y(dve, n, bank=3)
                    elif h == self.STATS:
                        net.norm_dve_stats(dve, ch, n)
                    elif h == self.APPLY:
                        net.norm_dve_apply(dve, n)
                i = t * PH + h
                dve.wait_ge(net["p_pairs"], i + 1)
                dve.wait_ge(net["p_ranks"], i + 1)
                if i >= 2:
                    dve.wait_ge(net["p_summed"], i - 1)
                dve.scalar_tensor_tensor(out=self.wgt[:, h % 2, :], in0=net.pairs[(2, 0)[h % 2]][:, :],
                                         scalar=8.0, in1=self.expo[:, h % 2, :], op0=ALU.is_gt,
                                         op1=ALU.mult).then_inc(net["p_weights"], 1)
                if t + 1 < NT:
                    for step in self.STEPS[h]:
                        self.route(dve, ch, t + 1, step)
                if h == 0 and t:
                    self.gate_dve(dve, t - 1)
        self.gate_dve(dve, NT - 1)
        net.norm_dve(dve, ch, 2 * NG - 1, bank=3)

    def gate_dve(self, dve, t):
        net = self.net
        g, k = divmod(t, GT)
        dve.wait_ge(net["p_summed"], PH * (t + 1))
        dve.wait_ge(net["p_gelu"], 2 * (t + 1))
        if k == 0 and g:
            dve.wait_ge(net["out_ready"], NG + g)
        dve.tensor_tensor(out=self.gw[:, :, k * P:(k + 1) * P],
                          in0=net.pairs[3][:, :].rearrange("p (c t) -> p c t", c=8),
                          in1=self.gelu, op=ALU.mult).then_inc(net["p_gw"], 1)

    def route(self, dve, ch, t, step):
        net = self.net
        sim = self.sim[:, t % 2, :].rearrange("p (c v) -> p c v", c=PC)

        def f(ap):
            return ap.rearrange("p h i j -> p (h i j)")

        if step == 0:
            dve.wait_ge(net["p_sim_copied"], t + 1)
            for c in range(PC):
                ins = dve.max(self.top[:, c, :], sim[:, c, :])
            ch.link(ins)
            dve.tensor_tensor(out=self.d8, in0=self.top, in1=self.top[:, :, 0:1].broadcast_to([P, PC, PTOP]),
                              op=ALU.subtract)
            dve.tensor_tensor(out=self.dd, in0=sim, in1=self.top[:, :, 0:1].broadcast_to([P, PC, PKEYS]),
                              op=ALU.subtract).then_inc(net["p_diffs"], 1)
        elif step == 1:
            for c in range(PC):
                dve.max_index(self.idx[:, c * PTOP:(c + 1) * PTOP], self.top[:, c, :], sim[:, c, :])
            ch.link(dve.tensor_tensor(out=self.sums, in0=bc(self.top[:, 0:PH, :], 3, PTOP),
                                      in1=bc(self.top[:, PH:PC, :], 2, PTOP), op=ALU.add))
        elif step == 2:
            dve.tensor_copy(self.idxb, self.idx)
            for h in range(PH):
                ins = dve.max(self.best[:, h, :], self.sums[:, h, :, :].rearrange("p i j -> p (i j)"))
            ch.link(ins)
            for h in range(PH):
                ins = dve.match_replace(self.left[:, h, :, :].rearrange("p i j -> p (i j)"), self.best[:, h, :],
                                        self.sums[:, h, :, :].rearrange("p i j -> p (i j)"), NEG)
            ch.link(ins)
        elif step == 3:
            ch.link(dve.tensor_tensor(out=f(self.chosen), in0=f(self.sums), in1=f(self.left), op=ALU.not_equal))
            dve.tensor_reduce(self.count, self.chosen, AX.X, ALU.add)
            dve.wait_ge(net["p_e8"], t + 1)
            ch.link(dve.tensor_tensor(out=self.prob, in0=bc(self.e8[:, 0:PH, :], 3, PTOP),
                                      in1=bc(self.e8[:, PH:PC, :], 2, PTOP), op=ALU.mult))
            dve.tensor_copy(self.coef[:, 0:PH, :], self.count)
            ch.link(dve.tensor_tensor(out=f(self.prob), in0=f(self.prob), in1=f(self.chosen), op=ALU.mult))
        elif step == 4:
            ch.link(dve.tensor_reduce(self.z8, self.prob.rearrange("p h i j -> p h (i j)"), AX.X, ALU.add))
            ch.link(dve.reciprocal(self.rz8, self.z8))
            dve.wait_ge(net["p_ed"], t + 1)
            ed = self.ed[:, t % 2, :].rearrange("p (c v) -> p c v", c=PC)
            if t >= 2:
                dve.wait_ge(net["p_pairs"], PH * (t - 1))
            dve.tensor_tensor(out=self.fx[:, t % 2, :].rearrange("p (h v) -> p h v", h=PH), in0=ed[:, 0:PH, :],
                              in1=bc(self.rz8, 2, PKEYS), op=ALU.mult).then_inc(net["p_factors"], 1)
        elif step == 5:
            idx = self.idxb.rearrange("p (c j) -> p c j", c=PC)
            for s in range(2):
                c = slice(s * PH, (s + 1) * PH)
                ins = dve.tensor_tensor(out=self.onehot[:, c], in0=bc(self.iota, 1, PH),
                                        in1=bc(idx[:, c, :], 2, PKEYS), op=ALU.is_equal)
            ch.link(ins)
        elif step == 6:
            for s in range(2):
                c = slice(s * PH, (s + 1) * PH)
                ins = dve.tensor_tensor(out=self.onehot[:, c], in0=self.onehot[:, c],
                                        in1=bc(self.coef[:, c, :], 2, PKEYS), op=ALU.mult)
            ch.link(ins)
        else:
            ch.link(dve.tensor_tensor(out=self.half4, in0=self.onehot[:, :, :, 0:4], in1=self.onehot[:, :, :, 4:8],
                                      op=ALU.add))
            ch.link(dve.tensor_tensor(out=self.half2, in0=self.half4[:, :, :, 0:2], in1=self.half4[:, :, :, 2:4],
                                      op=ALU.add))
            nq = self.nq[t % 2].rearrange("p (h s v) -> p s h v", h=PH, s=2)
            h2 = self.half2.rearrange("p (s h) v j -> p s h v j", s=2)
            dve.tensor_tensor(out=nq, in0=h2[:, :, :, :, 0], in1=h2[:, :, :, :, 1], op=ALU.add) \
               .then_inc(net["p_routed"], 1)

    def pool(self, pool, ch):
        net = self.net
        pool.wait_ge(net["p_varsum"], 1)
        pool.tensor_tensor(out=self.scale[:, 1, :], in0=self.scale[:, 0, :], in1=net.minus_half, op=ALU.pow) \
            .then_inc(net["p_rstd"], 1)
        for t in range(NT):
            pool.wait_ge(net["p_factors"], t + 1)
            for h in range(PH):
                i = t * PH + h
                if i >= 2:
                    pool.wait_ge(net["p_weights"], i - 1)
                ed = self.ed[:, t % 2, :].rearrange("p (c v) -> p c v", c=PC)
                fx = self.fx[:, t % 2, :].rearrange("p (h v) -> p h v", h=PH)
                e = self.expo[:, h % 2, :].rearrange("p (x y) -> p x y", x=PKEYS)
                pool.tensor_tensor(out=e, in0=bc(fx[:, h, :], 2, PKEYS), in1=bc(ed[:, PH + h, :], 1, PKEYS),
                                   op=ALU.mult).then_inc(net["p_pairs"], 1)
                if t % GT == 0 and t and h == self.APPLY - 1:
                    net.norm_pool(pool, NG + t // GT - 1)
        net.norm_pool(pool, 2 * NG - 1)


class Lightning:
    LAYER = 2
    ORDER = (8, 9, 0, 1, 2, 3, 4, 5, 6, 7)

    def __init__(self, net):
        self.net = net
        w = net.late
        w.at = 0
        self.wq, self.wqr = w.take(8, P), w.take(8, P)
        self.wk, self.wkr = w.take(2, P), w.take(2, P)
        self.wv = w.take(2 * P)
        self.wo = w.take(8, P)
        self.kdec = w.take(16)
        self.blk = w.take(8)
        self.decay = w.take(16, P)
        self.qdec = w.take(8, P)
        self.cos, self.sin = w.take(1024), w.take(1024)
        a = Arena(net.work)
        self.q = a.take(8, GW)
        self.k = a.take(2, GW)
        self.turned = a.take(2, GW)
        self.v, self.ktok = a.take(GT, 2 * P), a.take(GT, 2 * P)
        self.qd = a.take(2, 8, P)
        self.vd = a.take(2, 16, HD)
        self.s = a.take(2, GW)
        self.o = a.take(8, GW)
        self.state = a.take(2, 8, P)

    def pe(self, pe):
        net, bank = self.net, self.net.bank
        xT = net.xT[0]
        net.layer_start(pe, 2)
        pe.wait_ge(net["w2_loaded"], 16 * 10)
        for g in range(NG):
            n = 2 * NG + g
            xg = xT[:, g * GW:(g + 1) * GW]
            for k in range(GT):
                t = g * GT + k
                mm = pe.matmul(net.pairs[3][:, k * 2 * P:(k + 1) * 2 * P], xT[:, t * P:(t + 1) * P], self.wv,
                               start=True, stop=True)
            mm.then_inc(net["l_v"], 1)
            for p, c in enumerate(self.ORDER):
                i = 10 * g + p
                w, wr = (self.wq[:, c, :], self.wqr[:, c, :]) if c < 8 else (self.wk[:, c - 8, :], self.wkr[:, c - 8, :])
                if i >= 2:
                    pe.wait_ge(net["l_rotated"], i - 1)
                if p == 1:
                    pe.wait_ge(net["l_vk_copied"], 2 * g + 1)
                pe.matmul(bank[4 + 2 * (p % 2)], w, xg, start=True, stop=True)
                pe.matmul(bank[5 + 2 * (p % 2)], wr, xg, start=True, stop=True).then_inc(net["l_qk"], 1)
                if g and p == 0:
                    net.norm_pe_back(pe, n - 1)
                if g and p == 4:
                    net.norm_pe_forth(pe, n - 1)
            pe.wait_ge(net["l_rotated"], 10 * (g + 1))
            pe.wait_ge(net["l_summed"], 10 * g + 2)
            for k in range(GT):
                for pr in range(2):
                    o = k * 2 * P + pr * P
                    mm = pe.transpose(net.pairs[2][:, o:o + P], self.k[:, pr, k * P:(k + 1) * P], net.ident)
            mm.then_inc(net["l_kt"], 1)
            pe.wait_ge(net["l_vk_copied"], 2 * (g + 1))
            for k in range(GT):
                t = g * GT + k
                if t % 8 != 7:
                    self.added(pe, t)
                for kv in range(NKV):
                    i = t * NKV + kv
                    pr, half = divmod(kv, 2)
                    rows = slice(half * HD, half * HD + HD)
                    if k == 0 and half == 0:
                        pe.wait_ge(net["l_summed"], 10 * g + 2 + 4 * (pr + 1))
                    if i >= 2:
                        pe.wait_ge(net["l_decayed"], i - 1)
                    pe.matmul(bank[4 + kv % 2], self.k[rows, pr, k * P:(k + 1) * P],
                              self.q[rows, pr * 4:pr * 4 + 4, k * P:(k + 1) * P], start=True, stop=True) \
                      .then_inc(net["l_scores"], 1)
                    if kv:
                        self.output(pe, t, kv - 1)
                self.output(pe, t, 3)
            pe.wait_ge(net["l_o_copied"], 8 * (g + 1))
            if n >= 2:
                pe.wait_ge(net["y_ready"], n - 1)
            for c in range(8):
                mm = pe.matmul(bank[g % 2], self.wo[:, c, :], self.o[:, c, :], start=(c == 0), stop=(c == 7))
            mm.then_inc(net["out_ready"], 1)
        net.norm_pe_back(pe, 3 * NG - 1)
        net.norm_pe_forth(pe, 3 * NG - 1)

    def added(self, pe, t):
        net = self.net
        pe.wait_ge(net["l_vd"], t + 1 - t // 8)
        if t:
            pe.wait_ge(net["l_state"], t - t // 8)
        pe.wait_ge(net["normed"], 2 * NG + t // GT)
        for kv in range(NKV):
            pr, half = divmod(kv, 2)
            mm = pe.matmul(net.bank[2][half * HD:half * HD + HD, pr * 256:pr * 256 + 256],
                           self.ktok[:, t % GT, kv * HD:(kv + 1) * HD],
                           self.vd[:, t % 2, kv * 4:kv * 4 + 4, :].rearrange("p a b -> p (a b)"),
                           start=True, stop=True)
        mm.then_inc(net["l_added"], 1)

    def output(self, pe, t, kv):
        net = self.net
        k = t % GT
        pr, half = divmod(kv, 2)
        rows = slice(half * HD, half * HD + HD)
        out = net.bank[6 + pr][rows, :]
        first = t % 8 == 0
        if t and half == 0:
            pe.wait_ge(net["l_o_copied"], 2 * (t - 1) + pr + 1)
        if not first:
            pe.wait_ge(net["l_qd"], t - t // 8)
            pe.wait_ge(net["l_state"], t - t // 8)
            if half == 0:
                for m in range(4):
                    pe.matmul(net.bank[6 + pr][:, m * P:(m + 1) * P], self.state[:, t % 2, pr * 4 + m, :],
                              self.qd[:, t % 2, pr * 4 + m, :], start=(m == 0), stop=False, skip_group_check=True)
        pe.wait_ge(net["l_decayed"], t * NKV + kv + 1)
        mm = pe.matmul(out, self.v[:, k, kv * HD:(kv + 1) * HD], self.s[:, kv % 2, :], start=first, stop=True,
                       skip_group_check=True)
        mm.then_inc(net["l_out"], 1)

    def act(self, act, ch):
        net = self.net
        net.layer_start(act, 2)
        for g in range(NG):
            if g:
                act.wait_ge(net["out_ready"], 2 * NG + g)
                act.wait_ge(net["l_vd"], GT * g - GT * g // 8)
            act.wait_ge(net["l_v"], g + 1)
            act.activation(self.v.rearrange("p a b -> p (a b)"), net.pairs[3][:, :], ACT.Copy) \
               .then_inc(net["l_vk_copied"], 1)
            if g:
                net.norm_act(act, 2 * NG + g - 1)
            act.wait_ge(net["l_kt"], g + 1)
            act.activation(self.ktok.rearrange("p a b -> p (a b)"), net.pairs[2][:, :], ACT.Copy) \
               .then_inc(net["l_vk_copied"], 1)
            for k in range(GT):
                t = g * GT + k
                for pr in range(2):
                    act.wait_ge(net["l_out"], t * NKV + 2 * pr + 2)
                    act.activation(self.o[:, pr * 4:pr * 4 + 4, k * P:(k + 1) * P],
                                   net.bank[6 + pr].rearrange("p (a b) -> p a b", a=4), ACT.Copy) \
                       .then_inc(net["l_o_copied"], 1)
        net.norm_act(act, 3 * NG - 1)

    def dve(self, dve, ch):
        net = self.net
        net.layer_start(dve, 2)
        dve.wait_ge(net["w2_loaded"], 16 * 10)
        dve.wait_ge(net["w3_loaded"], 16 * 2)
        dve.wait_ge(net["l_cleared"], 1)
        for g in range(NG):
            pos = (g % 2) * GW
            if g:
                net.norm_dve_y(dve, 2 * NG + g - 1)
            for p, c in enumerate(self.ORDER):
                if g and p == 1:
                    net.norm_dve_rest(dve, ch, 2 * NG + g - 1)
                i = 10 * g + p
                b = 4 + 2 * (p % 2)
                dve.wait_ge(net["l_qk"], i + 1)
                dst = self.q[:, c, :] if c < 8 else self.k[:, c - 8, :]
                dve.tensor_tensor(out=dst, in0=net.bank[b], in1=self.cos[:, pos:pos + GW], op=ALU.mult)
                if i >= 2:
                    dve.wait_ge(net["l_summed"], i - 1)
                dve.tensor_tensor(out=self.turned[:, p % 2, :], in0=net.bank[b + 1], in1=self.sin[:, pos:pos + GW],
                                  op=ALU.mult).then_inc(net["l_rotated"], 1)
            for k in range(GT):
                t = g * GT + k
                if t % 8 != 7:
                    self.update(dve, ch, t)
                for kv in range(NKV):
                    i = t * NKV + kv
                    dve.wait_ge(net["l_scores"], i + 1)
                    if i >= 2:
                        dve.wait_ge(net["l_out"], i - 1)
                    dve.tensor_tensor(out=self.s[:, kv % 2, :], in0=net.bank[4 + kv % 2],
                                      in1=self.decay[:, kv * 4:kv * 4 + 4, :].rearrange("p a b -> p (a b)"),
                                      op=ALU.mult).then_inc(net["l_decayed"], 1)
        net.norm_dve(dve, ch, 3 * NG - 1)

    def update(self, dve, ch, t):
        net = self.net
        old, new = self.state[:, t % 2, :, :], self.state[:, (t + 1) % 2, :, :]
        if t:
            dve.wait_ge(net["l_out"], t * NKV)
        if t % 8:
            dve.wait_ge(net["l_state"], t - t // 8)
            ch.link(dve.tensor_tensor(out=new, in0=old, in1=bc(self.blk, 2, P), op=ALU.mult))
        dve.wait_ge(net["l_added"], t + 1 - t // 8)
        added = net.bank[2].rearrange("p (c e) -> p c e", c=8)
        for half in range(2):
            r = slice(half * HD, half * HD + HD)
            block = new[r, :, half * HD:half * HD + HD]
            if t % 8:
                ins = dve.tensor_tensor(out=block, in0=block, in1=added[r], op=ALU.add)
            else:
                ins = dve.tensor_copy(block, added[r])
        ins.then_inc(net["l_state"], 1)

    def pool(self, pool, ch):
        net = self.net
        pool.wait_ge(net["w2_loaded"], 16 * 10)
        net.layer_start(pool, 2)
        pool.wait_ge(net["w3_loaded"], 16 * 2)
        pool.memset(self.state, 0.0).then_inc(net["l_cleared"], 1)
        for g in range(NG):
            for p, c in enumerate(self.ORDER):
                if g and p == 1:
                    net.norm_pool(pool, 2 * NG + g - 1)
                dst = self.q[:, c, :] if c < 8 else self.k[:, c - 8, :]
                pool.wait_ge(net["l_rotated"], 10 * g + p + 1)
                pool.tensor_tensor(out=dst, in0=dst, in1=self.turned[:, p % 2, :], op=ALU.add) \
                    .then_inc(net["l_summed"], 1)
                if p == 4:
                    self.decayed_values(pool, g * GT)
            pool.wait_ge(net["l_summed"], 10 * (g + 1))
            for k in range(GT):
                t = g * GT + k
                if t % 8:
                    if t >= 3:
                        pool.wait_ge(net["l_out"], (t - 1) * NKV)
                        pool.wait_ge(net["l_qd"], t - 2 - (t - 2) // 8)
                    pool.tensor_tensor(out=self.qd[:, t % 2, :, :], in0=self.q[:, :, k * P:(k + 1) * P],
                                       in1=self.qdec, op=ALU.mult).then_inc(net["l_qd"], 1)
                if k and t % 8 != 7:
                    self.decayed_values(pool, t)
        net.norm_pool(pool, 3 * NG - 1)

    def decayed_values(self, pool, t):
        net = self.net
        pool.wait_ge(net["l_vk_copied"], 2 * (t // GT) + 1)
        if t >= 2:
            pool.wait_ge(net["l_vd"], t - 1 - (t - 1) // 8)
            pool.wait_ge(net["l_added"], t - 1 - (t - 1) // 8)
        for kv in range(NKV):
            ins = pool.tensor_tensor(out=self.vd[:, t % 2, kv * 4:kv * 4 + 4, :],
                                     in0=bc(self.v[:, t % GT, kv * HD:(kv + 1) * HD], 1, 4),
                                     in1=bc(self.kdec[:, kv * 4:kv * 4 + 4], 2, HD), op=ALU.mult)
        ins.then_inc(net["l_vd"], 1)


class Gates:

    def __init__(self, net, arena, turned, layer, experts, keep, renorm, tag, banks):
        self.net, self.layer, self.experts, self.keep, self.renorm, self.tag = net, layer, experts, keep, renorm, tag
        self.banks = banks
        self.wide = experts + 8 - keep
        a = arena
        self.logit = a.take(NT, 16)
        self.peak, self.total = a.take(NT), a.take(NT)
        self.weights = a.take(NT, 24)
        self.top, self.kept, self.left = a.take(NT, 8), a.take(NT, 8), a.take(NT, 24)
        self.gate = a.take(NT, 16)
        self.parts = a.take(NT * 24).bitcast(BF16).rearrange("p (t s e) -> p t s e", t=NT, s=3)
        self.gateT = turned.take(TOK // 2).bitcast(BF16)
        self.sel = turned.take(experts * P // 2).bitcast(BF16).rearrange("p (e d) -> p e d", e=experts)

    def pe_logits(self, pe, xT, w, b):
        net, E = self.net, self.experts
        for t in range(NT):
            out = net.bank[self.banks[0]][:, t * 16:t * 16 + E]
            mm = pe.matmul(out, xT[:, t * P:(t + 1) * P], w, start=True, stop=(b is None))
            if b is not None:
                mm = pe.matmul(out, net.ones[0:1, :], b, start=False, stop=True)
        mm.then_inc(net[self.tag + "_logits"], 1)

    def pe_turn(self, pe):
        net = self.net
        pe.wait_ge(net["tables_made"], 2)
        pe.wait_ge(net[self.tag + "_gates"], 1)
        for half in range(2):
            bank = net.bank[self.banks[1 - half]].bitcast(BF16)
            for k in range(8):
                mm = pe.transpose(bank[0:48, k * P:(k + 1) * P],
                                  self.parts[:, 8 * half + k, :, :].rearrange("p s e -> p (s e)"), net.identb)
            mm.then_inc(net[self.tag + "_turned"], 1)

    def pe_spread(self, pe, bank, g, e):
        pe.matmul(bank, self.sel[0:48, e, :], self.gateT[0:48, g * GW:(g + 1) * GW], start=True, stop=True) \
          .then_inc(self.net[self.tag + "_wide"], 1)

    def act_exp(self, act):
        net, E = self.net, self.experts
        act.wait_ge(net[self.tag + "_shifted"], 1)
        act.activation(self.weights[:, :, 0:E], self.logit[:, :, 0:E], ACT.Exp).then_inc(net[self.tag + "_exp"], 1)

    def act_turned(self, act):
        net = self.net
        for half in range(2):
            act.wait_ge(net[self.tag + "_turned"], half + 1)
            act.activation(self.gateT[0:48, half * 1024:(half + 1) * 1024],
                           net.bank[self.banks[1 - half]].bitcast(BF16)[0:48, :], ACT.Copy) \
               .then_inc(net[self.tag + "_gateT"], 1)

    def pool_sel(self, pool):
        pool.tensor_tensor(out=self.sel[0:48, :, :], in0=bc(self.net.pick[0:48, 0:self.experts], 2, P),
                           in1=bc(self.net.pick[0:48, 0:self.experts], 2, P), op=ALU.mult) \
            .then_inc(self.net[self.tag + "_sel"], 1)

    def dve_fill(self, dve):
        for i in range(8 - self.keep):
            dve.memset(self.weights[:, :, self.experts + i:self.experts + i + 1], -1.0 - i)
            dve.memset(self.kept[:, :, self.keep + i:self.keep + i + 1], -1.0 - i)
        dve.memset(self.gate[:, :, 0:15], 0.0)
        dve.memset(self.gate[:, :, 15:16], 1.0).then_inc(self.net[self.tag + "_filled"], 1)
        dve.wait_ge(self.net[self.tag + "_filled"], 1)

    def dve(self, dve, ch):
        net, E, keep, wide = self.net, self.experts, self.keep, self.wide
        dve.wait_ge(net[self.tag + "_logits"], 1)
        raw = net.bank[self.banks[0]][:, 0:NT * 16].rearrange("p (k e) -> p k e", k=NT)[:, :, 0:E]
        ch.link(dve.reduce_max(self.peak, raw, AX.X))
        dve.tensor_tensor(out=self.logit[:, :, 0:E], in0=raw, in1=bc(self.peak, 2, E), op=ALU.subtract) \
           .then_inc(net[self.tag + "_shifted"], 1)
        dve.wait_ge(net[self.tag + "_exp"], 1)
        w = self.weights[:, :, 0:E]
        ch.link(dve.reduce_sum(self.total, w, AX.X))
        ch.link(dve.reciprocal(self.total, self.total))
        ch.link(dve.tensor_tensor(out=w, in0=w, in1=bc(self.total, 2, E), op=ALU.mult))
        for k in range(NT):
            ins = dve.max(self.top[:, k, :], self.weights[:, k, 0:E])
        ch.link(ins)
        ch.link(dve.tensor_copy(self.kept[:, :, 0:keep], self.top[:, :, 0:keep]))
        for k in range(NT):
            ins = dve.match_replace(self.left[:, k, 0:wide], self.kept[:, k, :], self.weights[:, k, 0:wide], -99.0)
        ch.link(ins)
        ch.link(dve.tensor_tensor(out=self.left[:, :, 0:E], in0=w, in1=self.left[:, :, 0:E], op=ALU.not_equal))
        ch.link(dve.tensor_tensor(out=self.gate[:, :, 0:E], in0=w, in1=self.left[:, :, 0:E], op=ALU.mult))
        if self.renorm is not None:
            ch.link(dve.reduce_sum(self.total, self.gate[:, :, 0:E], AX.X))
            ch.link(dve.tensor_scalar(self.total, self.total, self.renorm, None, ALU.add))
            ch.link(dve.reciprocal(self.total, self.total))
            ch.link(dve.tensor_tensor(out=self.gate[:, :, 0:E], in0=self.gate[:, :, 0:E],
                                      in1=bc(self.total, 2, E), op=ALU.mult))
        rest = self.logit
        ch.link(dve.tensor_copy(self.parts[:, :, 0, :], self.gate))
        ch.link(dve.tensor_tensor(out=rest, in0=self.gate, in1=self.parts[:, :, 0, :], op=ALU.subtract))
        ch.link(dve.tensor_copy(self.parts[:, :, 1, :], rest))
        ch.link(dve.tensor_tensor(out=rest, in0=rest, in1=self.parts[:, :, 1, :], op=ALU.subtract))
        dve.tensor_copy(self.parts[:, :, 2, :], rest).then_inc(net[self.tag + "_gates"], 1)


class GeluExperts:
    LAYER = 3
    NORM_BACK, NORM_FORTH = 0, 4

    def __init__(self, net):
        self.net = net
        w = net.mid
        w.at = 0
        self.w1, self.w2 = w.take(C1, P), w.take(C1, P)
        self.b1 = w.take(C1)
        self.gw = w.take(16)
        self.gb = w.take(16)
        self.b2 = w.take(P)
        a = Arena(net.work)
        self.gates = Gates(net, a, a, 3, E1, 3, None, "g1", (6, 7))
        self.gateT32 = a.take(TOK)
        self.h, self.hg = a.take(3, GW), a.take(3, GW)

    def pe(self, pe):
        net, bank = self.net, self.net.bank
        xT = net.xT[1]
        net.layer_start(pe, 3)
        pe.wait_ge(net["w3_loaded"], 16 * 8)
        self.gates.pe_logits(pe, xT, self.gw[:, 0:E1], self.gb[0:1, 0:E1])
        for g in range(NG):
            n = 3 * NG + g
            for c in range(C1 + 1):
                i = C1 * g + c
                if c < C1:
                    if i >= 2:
                        pe.wait_ge(net["e1_act"], i - 1)
                    pe.matmul(bank[4 + i % 2], self.w1[:, c, :], xT[:, g * GW:(g + 1) * GW], start=True, stop=True) \
                      .then_inc(net["e1_up"], 1)
                if c:
                    j = i - 1
                    if c == 1 and n >= 2:
                        pe.wait_ge(net["y_ready"], n - 1)
                    if c - 1 < C1S:
                        pe.wait_ge(net["e1_act"], j + 1)
                        src = self.h[:, j % 3, :]
                    else:
                        pe.wait_ge(net["e1_gated"], j + 1 - C1S * (g + 1))
                        src = self.hg[:, j % 3, :]
                    pe.matmul(bank[g % 2], self.w2[:, c - 1, :], src, start=(c == 1), stop=False) \
                      .then_inc(net["e1_down"], 1)
                if g and c == self.NORM_BACK:
                    net.norm_pe_back(pe, n - 1)
                if g and c == self.NORM_FORTH:
                    net.norm_pe_forth(pe, n - 1)
                if g == 0 and c == 3:
                    self.gates.pe_turn(pe)
                    pe.wait_ge(net["g1_gateT"], 2)
                    pe.wait_ge(net["g1_sel"], 1)
                if c == 3 or (c >= 4 and c % 2 == 0 and c < C1S + 2 * (E1 - 1)):
                    e = max(0, (c - 2) // 2)
                    x = E1 * g + e
                    if x >= 2:
                        pe.wait_ge(net["e1_gated"], 2 * (x - 1))
                    self.gates.pe_spread(pe, bank[6 + x % 2], g, e)
            pe.wait_ge(net["g1_gateT32"], 1)
            pe.matmul(bank[g % 2], self.b2[0:48, :], self.gateT32[0:48, g * GW:(g + 1) * GW], start=False, stop=True) \
              .then_inc(net["out_ready"], 1)
        net.norm_pe_back(pe, 4 * NG - 1)
        net.norm_pe_forth(pe, 4 * NG - 1)

    def act(self, act, ch):
        net = self.net
        net.layer_start(act, 3)
        act.wait_ge(net["w3_loaded"], 16 * 8)
        self.gates.act_exp(act)
        for g in range(NG):
            for c in range(C1):
                i = C1 * g + c
                if g == 0 and c == C1S:
                    self.gates.act_turned(act)
                if g and c == self.NORM_FORTH + 1:
                    net.norm_act(act, 3 * NG + g - 1)
                act.wait_ge(net["e1_up"], i + 1)
                if i >= 3:
                    act.wait_ge(net["e1_down"], i - 2)
                act.activation(self.h[:, i % 3, :], net.bank[4 + i % 2], ACT.Gelu, bias=self.b1[:, c:c + 1]) \
                   .then_inc(net["e1_act"], 1)
        net.norm_act(act, 4 * NG - 1)

    def dve(self, dve, ch):
        net = self.net
        net.layer_start(dve, 3)
        dve.wait_ge(net["w3_loaded"], 16 * 8)
        self.gates.dve_fill(dve)
        self.gates.dve(dve, ch)
        for g in range(NG):
            for c in range(C1S, C1):
                i = C1 * g + c
                x = E1 * g + (c - C1S) // 2
                dve.wait_ge(net["e1_act"], i + 1)
                dve.wait_ge(net["g1_wide"], x + 1)
                if i >= 3:
                    dve.wait_ge(net["e1_down"], i - 2)
                dve.tensor_tensor(out=self.hg[:, i % 3, :], in0=self.h[:, i % 3, :], in1=net.bank[6 + x % 2],
                                  op=ALU.mult).then_inc(net["e1_gated"], 1)
            net.norm_dve(dve, ch, 3 * NG + g, twice=True)

    def pool(self, pool, ch):
        net = self.net
        net.layer_start(pool, 3)
        self.gates.pool_sel(pool)
        pool.wait_ge(net["g1_gateT"], 2)
        pool.tensor_copy(self.gateT32[0:48, :], self.gates.gateT[0:48, :]).then_inc(net["g1_gateT32"], 1)
        for g in range(NG):
            net.norm_pool(pool, 3 * NG + g)


class Forgetting:
    LAYER = 4
    TERMS = ((0, 0), (0, 1), (0, 2), (1, 0), (1, 1), (1, 2), (2, 0), (2, 1))
    ROUNDS = 4
    UNITS = 98
    STEPS = 24
    LEAD = 74
    POINTS, AT_OUT = 8, 2
    CASTS = ((0, 0), (1, 0), (0, 1), (1, 1), (2, 0), (0, 2), (1, 2), (2, 1), (2, 2))
    SPLIT_DMAS = 9
    STACK_DMAS = 17

    def __init__(self, net):
        self.net = net
        nc = net.nc
        w = net.const
        self.wq, self.wk = w.take(P), w.take(P)
        self.wv, self.wo, self.wf = w.take(P), w.take(P), w.take(16)
        half = w.take(3 * P // 2).bitcast(BF16)
        self.identb, self.mask_n, self.mask_t = (half[:, i * P:(i + 1) * P] for i in range(3))
        self.mask_n32 = w.take(P)
        a = Arena(net.work)
        both = a.take(4, 4096)
        self.qs = [both[:, i, :].bitcast(BF16).rearrange("p (h t) -> p h t", h=8) for i in (0, 1)]
        self.ks = [both[:, i, :].bitcast(BF16).rearrange("p (h t) -> p h t", h=8) for i in (2, 3)]
        self.rows32 = both
        self.v = a.take(NT * 144 + 32)
        self.e = a.take(2, 4, GW)
        m = net.mid
        m.at = 0
        s, u = Arena(both[:, 1, :]), Arena(both[:, 3, :])
        self.full = [s.take(TOK), s.take(TOK), m.take(TOK)]
        self.parts = [[a.take(TOK // 2).bitcast(BF16) for _ in range(3)] for a in (m, m, u)]
        e2 = self.e.rearrange("p a b c -> p (a b c)")
        self.z, self.zabs = e2[:, 0:TOK], e2[:, TOK:2 * TOK]
        t = net.late
        t.at = 5500
        self.m = t.take(2, 8 * 2, 8)
        self.negm = t.take(GT, 8)
        self.mparts = t.take(GT * 12).bitcast(BF16).rearrange("p (k s h) -> p k s h", k=GT, s=3)
        self.mrows = [t.take(GW // 2).bitcast(BF16) for _ in range(2)]
        self.ot = t.take(2, GW)
        self.rz = t.take(2, GT * 4)
        self.o = t.take(8, P)
        self.oT = t.take(GW)
        self.scratch = [nc.dram_tensor(f"split_{n}", (3, r, TOK), BF16, kind="Internal").ap()
                        for n, r in (("q", P), ("k", P), ("f", 16))]

    def units(self):
        out = [("scores", it, h, 0) for it in range(4) for h in range(8)]
        late = [("scores", it, h, half) for it in range(4, 8) for h in range(8) for half in range(2)]
        out += late[:6] + [("turn", 0, 0, 0)] + late[6:] + [("turn", 1, 0, 0)]
        assert len(out) == self.UNITS
        return out

    def due(self, n):
        at_out = self.POINTS * self.AT_OUT if n >= 2 * self.STEPS else 0
        return min(self.ROUNDS * self.UNITS, self.LEAD + self.UNITS * (n + 1) // self.STEPS + at_out)

    def steps(self):
        return [(g, s, j) for g in range(2) for s in range(2) for j in range(4 * g + 4)]

    def pe(self, pe):
        net, bank = self.net, self.net.bank
        xT = net.xT[0]
        net.layer_start(pe, 4)
        pe.wait_ge(net["w4_loaded"], 16 * 6)
        for g in range(NG):
            pe.matmul(bank[4 + g][0:16, :], self.wf, xT[:, g * GW:(g + 1) * GW], start=True, stop=True) \
              .then_inc(net["f_z"], 1)
        for i in range(8):
            if i < 4:
                pe.wait_ge(net["f_z_copied"], i + 1)
            else:
                pe.wait_ge(net["f_qk_copied"], i - 3)
            pe.matmul(bank[4 + i % 4], (self.wq, self.wk)[i // 4], xT[:, (i % 4) * GW:(i % 4 + 1) * GW],
                      start=True, stop=True).then_inc(net["f_qk"], 1)
        for g in range(NG):
            if g >= 2:
                pe.wait_ge(net["f_v_copied"], g - 1)
            for k in range(GT):
                t = g * GT + k
                mm = pe.matmul(bank[g % 2][:, k * P:(k + 1) * P], xT[:, t * P:(t + 1) * P], self.wv,
                               start=True, stop=True)
            mm.then_inc(net["f_v"], 1)
        pe.wait_ge(net["f_qk_copied"], 8)
        pe.wait_ge(net["f_v_copied"], NG)
        steps = self.steps()
        for u in range(self.LEAD):
            self.unit_pe(pe, u)
        done = self.LEAD
        for r in range(self.ROUNDS):
            for k in range(self.STEPS):
                upto = self.due(r * self.STEPS + k)
                third = (upto - done) // 3
                self.scores_pe(pe, r, k, steps[k], 0)
                for u in range(done, done + third):
                    self.unit_pe(pe, u)
                self.scores_pe(pe, r, k, steps[k], 1)
                for u in range(done + third, done + 2 * third):
                    self.unit_pe(pe, u)
                if k:
                    self.values_pe(pe, r, k - 1, steps[k - 1])
                for u in range(done + 2 * third, upto):
                    self.unit_pe(pe, u)
                done = upto
                if k > 1 and steps[k - 2][2] == 4 * steps[k - 2][0] + 3:
                    self.turn_out_pe(pe, r, steps[k - 2])
            self.values_pe(pe, r, self.STEPS - 1, steps[-1])
            self.turn_out_pe(pe, r, steps[-1])
            if r % 2:
                done = self.out_pe(pe, r // 2, done)

    def unit_pe(self, pe, u):
        net = self.net
        r, i = divmod(u, self.UNITS)
        kind, it, h, half = self.units()[i]
        bank = net.bank[u % 2]
        if i == 0:
            pe.wait_ge(net[f"f_stacked{r % 2}"], 16 * self.STACK_DMAS * (r // 2 + 1))
        if u >= 2:
            pe.wait_ge(net["f_unit_read"], u - 1)
        if kind == "turn":
            pe.wait_ge(net["f_negmax"], 2 * r + it + 1)
            for k in range(GT):
                mm = pe.transpose(bank.bitcast(BF16)[0:24, k * P:(k + 1) * P],
                                  self.mparts[:, k, :, :].rearrange("p s h -> p (s h)"), self.identb)
            mm.then_inc(net["f_unit"], 1)
            return
        q = self.qs[r % 2][0:96, h, it * P:(it + 1) * P]
        k = self.ks[r % 2][0:96, h, :]
        lo, hi = half * GW, min(half * GW + GW, (it + 1) * P)
        own = it // 4 == half
        rest = hi - P if own else hi
        if rest > lo:
            mm = pe.matmul(bank[:, 0:rest - lo], q, k[:, lo:rest], start=True, stop=True)
        if own:
            pe.matmul(bank[:, rest - lo:hi - lo], q, k[:, rest:hi], start=True, stop=False)
            mm = pe.matmul(bank[:, rest - lo:hi - lo], self.identb, self.mask_n, start=False, stop=True)
        mm.then_inc(net["f_unit"], 1)

    def scores_pe(self, pe, r, k, step, pair):
        net = self.net
        g, s, j = step
        n = r * self.STEPS + k
        lo = max(0, j - 4 * g) * P
        if s == 0 and j == 0 and pair == 0:
            pe.wait_ge(net[f"f_mrows{g}"], 48 * (r + 1))
        for q in (2 * pair, 2 * pair + 1):
            if q % 2 == 0 and n:
                pe.wait_ge(net["f_exp"], 2 * n - 1 + q // 2)
            bank, h = net.bank[4 + q], 4 * s + q
            kt = self.ks[r % 2][:, h, j * P:(j + 1) * P]
            at = lo
            if j >= 4 * g:
                pe.matmul(bank[:, lo:lo + P], kt, self.qs[r % 2][:, h, g * GW + lo:g * GW + lo + P],
                          start=True, stop=False)
                mm = pe.matmul(bank[:, lo:lo + P], self.identb, self.mask_t, start=False, stop=True)
                at = lo + P
            if at < GW:
                mm = pe.matmul(bank[:, at:GW], kt, self.qs[r % 2][:, h, g * GW + at:(g + 1) * GW],
                               start=True, stop=True)
            if q % 2:
                mm.then_inc(net["f_shifted"], 1)

    def slot(self, r, step):
        return r * 4 + 2 * step[0] + step[1]

    def values_pe(self, pe, r, k, step):
        net = self.net
        g, s, j = step
        n = r * self.STEPS + k
        lo = max(0, j - 4 * g) * P
        slot = self.slot(r, step)
        pe.wait_ge(net["f_exp"], 2 * n + 2)
        if j == 0 and slot >= 2:
            pe.wait_ge(net["f_normed"], slot - 1)
        for q in range(4):
            h = 8 * (r % 2) + 4 * s + q
            at = ((r // 2) * 8 + j) * 144 + h * 9
            mm = pe.matmul(net.bank[2 + slot % 2][32 * q:32 * q + 32, lo:GW], self.v[:, at:at + 32],
                           self.e[:, n % 2, q, lo:GW], start=(j == 0), stop=(j == 4 * g + 3),
                           skip_group_check=True)
        mm.then_inc(net["f_pv"], 1)

    def turn_out_pe(self, pe, r, step):
        net = self.net
        slot = self.slot(r, step)
        pe.wait_ge(net["f_ot_copied"], slot + 1)
        for k in range(GT):
            mm = pe.transpose(net.bank[2 + slot % 2][:, k * P:(k + 1) * P], self.ot[:, slot % 2, k * P:(k + 1) * P],
                              net.ident)
        mm.then_inc(net["f_turned"], 1)

    def beside(self, unit, b, done):
        upto = done + (0 if b else self.AT_OUT)
        for u in range(done, upto):
            unit(u)
        return upto

    def out_pe(self, pe, b, done):
        net = self.net

        def unit(u):
            self.unit_pe(pe, u)

        pe.wait_ge(net["f_normed"], 8 * (b + 1))
        for g in (2 * b, 2 * b + 1):
            n = 4 * NG + g
            for k in range(GT):
                mm = pe.transpose(net.bank[2][:, k * P:(k + 1) * P], self.o[:, (g % 2) * GT + k, :], net.ident)
            mm.then_inc(net["f_oT"], 1)
            done = self.beside(unit, b, done)
            pe.wait_ge(net["f_oT_copied"], g + 1)
            pe.matmul(net.bank[3], self.wo, self.oT, start=True, stop=True).then_inc(net["out_ready"], 1)
            done = self.beside(unit, b, done)
            net.norm_pe_back(pe, n)
            done = self.beside(unit, b, done)
            net.norm_pe_forth(pe, n)
            done = self.beside(unit, b, done)
            if g % 2 == 0:
                pe.wait_ge(net["xT_done"], n + 1)
        return done

    def act(self, act, ch):
        net = self.net
        net.layer_start(act, 4)
        act.wait_ge(net["f_zabs"], 1)
        ch.link(act.activation(self.zabs[0:16, :], self.zabs[0:16, :], ACT.Exp))
        act.activation(self.zabs[0:16, :], self.zabs[0:16, :], ACT.Ln, bias=1.0).then_inc(net["f_ln"], 1)
        for i in range(8):
            act.wait_ge(net["f_qk"], i + 1)
            act.activation(self.full[i // 4][:, (i % 4) * GW:(i % 4 + 1) * GW], net.bank[4 + i % 4], ACT.Copy,
                           scale=(float(FD) ** -0.5, 1.0)[i // 4]).then_inc(net["f_qk_copied"], 1)
        rests = [c for c in self.CASTS if c[1] < 2]
        for i, part in self.CASTS:
            rows = slice(0, (P, P, 16)[i])
            if part:
                act.wait_ge(net["f_rest"], rests.index((i, part - 1)) + 1)
            elif i < 2:
                act.wait_ge(net["f_qk_copied"], 4 * (i + 1))
            else:
                act.wait_ge(net["f_summed"], 1)
            act.activation(self.parts[i][part][rows, :], self.full[i][rows, :], ACT.Copy).then_inc(net["f_cast"], 1)
        steps = self.steps()
        for r in range(self.ROUNDS):
            for k in range(self.STEPS):
                g, s, j = steps[k]
                n = r * self.STEPS + k
                lo = max(0, j - 4 * g) * P
                for pair in range(2):
                    act.wait_ge(net["f_shifted"], 2 * n + pair + 1)
                    if n >= 2:
                        act.wait_ge(net["f_pv"], n - 1)
                    act.activation(self.e[:, n % 2, 2 * pair:2 * pair + 2, lo:GW],
                                   net.pairs[2 + pair][:, :].rearrange("p (q t) -> p q t", q=2)[:, :, lo:GW],
                                   ACT.Exp).then_inc(net["f_exp"], 1)
                if k and steps[k - 1][2] == 4 * steps[k - 1][0] + 3:
                    self.copy_slot(act, r, k - 1, steps[k - 1])
            self.copy_slot(act, r, self.STEPS - 1, steps[-1])
            if r % 2:
                for g in (r - 1, r):
                    act.wait_ge(net["f_oT"], g + 1)
                    if g:
                        act.wait_ge(net["out_ready"], 4 * NG + g)
                    act.activation(self.oT, net.bank[2], ACT.Copy).then_inc(net["f_oT_copied"], 1)
                    net.norm_act(act, 4 * NG + g)

    def copy_slot(self, act, r, k, step):
        net = self.net
        slot = self.slot(r, step)
        act.wait_ge(net["f_pv"], r * self.STEPS + k + 1)
        if slot >= 2:
            act.wait_ge(net["f_turned"], slot - 1)
        act.activation(self.ot[:, slot % 2, :], net.bank[2 + slot % 2], ACT.Copy).then_inc(net["f_ot_copied"], 1)

    def dve(self, dve, ch):
        net = self.net
        net.layer_start(dve, 4)
        dve.wait_ge(net["w4_loaded"], 16 * 6)
        z, za, fl = self.z[0:16, :], self.zabs[0:16, :], self.full[2][0:16, :]
        dve.tensor_copy(self.identb, net.ident)
        dve.tensor_copy(self.mask_n, self.mask_n32)
        ch.link(dve.tensor_copy(self.mask_t, net.mask))
        for g in range(NG):
            dve.wait_ge(net["f_z"], g + 1)
            dve.tensor_copy(z[:, g * GW:(g + 1) * GW], net.bank[4 + g][0:16, :]).then_inc(net["f_z_copied"], 1)
        dve.wait_ge(net["f_z_copied"], NG)
        dve.scalar_tensor_tensor(out=za, in0=z, scalar=-1.0, in1=z, op0=ALU.mult, op1=ALU.min) \
           .then_inc(net["f_zabs"], 1)
        ch.link(dve.tensor_scalar(fl, z, -1.0, 0.0, ALU.mult, ALU.max))
        dve.wait_ge(net["f_ln"], 1)
        ch.link(dve.tensor_tensor(out=za, in0=fl, in1=za, op=ALU.add))
        ch.link(dve.memset(z, 1.0))
        for b in range(2):
            c = slice(b * 1024, (b + 1) * 1024)
            ins = dve.tensor_tensor_scan(fl[:, c], z[:, c], za[:, c], 0.0, ALU.mult, ALU.add)
        ins.then_inc(net["f_summed"], 1)
        for n, (i, part) in enumerate(self.CASTS):
            if part < 2:
                full = self.full[i][0:(P, P, 16)[i], :]
                dve.wait_ge(net["f_cast"], n + 1)
                dve.tensor_tensor(out=full, in0=full, in1=self.parts[i][part][0:(P, P, 16)[i], :],
                                  op=ALU.subtract).then_inc(net["f_rest"], 1)
        dve.wait_ge(net["f_filled"], 1)
        for g in range(NG):
            dve.wait_ge(net["f_v"], g + 1)
            dve.tensor_copy(self.v[:, g * GT * 144:(g + 1) * GT * 144]
                            .rearrange("p (t h d) -> p t h d", t=GT, h=FH)[:, :, :, 0:FD],
                            net.bank[g % 2].rearrange("p (t h d) -> p t h d", t=GT, h=FH)) \
               .then_inc(net["f_v_copied"], 1)
        steps = self.steps()
        for u in range(self.LEAD):
            self.unit_dve(dve, ch, u)
        done = self.LEAD
        for r in range(self.ROUNDS):
            for k in range(self.STEPS):
                upto = self.due(r * self.STEPS + k)
                for u in range(done, upto):
                    self.unit_dve(dve, ch, u)
                done = upto
                if k > 1 and steps[k - 2][2] == 4 * steps[k - 2][0] + 3:
                    self.norm_slot(dve, ch, r, steps[k - 2])
            self.norm_slot(dve, ch, r, steps[-1])
            if r % 2:
                done = self.out_dve(dve, ch, r // 2, done)

    def out_dve(self, dve, ch, b, done):
        net = self.net

        def unit(u):
            self.unit_dve(dve, ch, u)

        for g in (2 * b, 2 * b + 1):
            n = 4 * NG + g
            done = self.beside(unit, b, done)
            net.norm_dve_y(dve, n, bank=3)
            done = self.beside(unit, b, done)
            net.norm_dve_stats(dve, ch, n)
            done = self.beside(unit, b, done)
            net.norm_dve_apply(dve, n)
            done = self.beside(unit, b, done)
        return done

    def split(self, dve, ch, x, parts):
        for i in range(2):
            ch.link(dve.tensor_copy(parts[i], x))
            ch.link(dve.tensor_tensor(out=x, in0=x, in1=parts[i], op=ALU.subtract))
        return dve.tensor_copy(parts[2], x)

    def unit_dve(self, dve, ch, u):
        net = self.net
        r, i = divmod(u, self.UNITS)
        kind, it, h, half = self.units()[i]
        bank = net.bank[u % 2]
        if kind == "turn":
            dve.wait_ge(net["f_unit"], u + 1)
            n = 2 * r + it
            if n >= 2:
                dve.wait_ge(net[f"f_mrows{n % 2}"], 48 * (n // 2))
            dve.tensor_copy(self.mrows[n % 2][0:24, :], bank.bitcast(BF16)[0:24, 0:GW]).then_inc(net["f_unit_read"], 1)
            return
        dve.wait_ge(net["f_unit"], u + 1)
        width = min(GW, (it + 1) * P - half * GW)
        dve.reduce_max(self.m[:, r % 2, 2 * it + half, h:h + 1], bank[:, 0:width], AX.X) \
           .then_inc(net["f_unit_read"], 1)
        if h == 7 and it % 4 == 3 and half == it // 4:
            dve.wait_ge(net["f_unit_read"], u + 1)
            g = it // 4
            m = self.m[:, r % 2, 8 * g:8 * g + 8, :].rearrange("p (k s) h -> p k s h", s=2)
            if g:
                ch.link(dve.tensor_tensor(out=self.negm, in0=m[:, :, 0, :], in1=m[:, :, 1, :], op=ALU.max))
                ch.link(dve.tensor_scalar(self.negm, self.negm, -1.0, None, ALU.mult))
            else:
                ch.link(dve.tensor_scalar(self.negm, m[:, :, 0, :], -1.0, None, ALU.mult))
            if r or g:
                dve.wait_ge(net["f_unit"], self.turn_unit(2 * r + g - 1) + 1)
            self.split(dve, ch, self.negm, [self.mparts[:, :, s, :] for s in range(3)]) \
                .then_inc(net["f_negmax"], 1)

    def turn_unit(self, n):
        return (n // 2) * self.UNITS + (self.UNITS - 1 if n % 2 else 38)

    def norm_slot(self, dve, ch, r, step):
        net = self.net
        g, s, _ = step
        slot = self.slot(r, step)
        dve.wait_ge(net["f_turned"], slot + 1)
        o = net.bank[2 + slot % 2].rearrange("p (k q e) -> p k q e", k=GT, q=4)
        rz = self.rz[:, slot % 2, :].rearrange("p (k q) -> p k q", k=GT)
        ch.link(dve.reciprocal(rz, o[:, :, :, FD]))
        if r == 2 and g == 0 and s == 0:
            dve.wait_ge(net["f_oT"], 2)
        h = 8 * (r % 2) + 4 * s
        out = self.o[:, 4 * g:4 * g + 4, h * FD:(h + 4) * FD].rearrange("p k (q d) -> p k q d", q=4)
        dve.tensor_tensor(out=out, in0=o[:, :, :, 0:FD], in1=bc(rz, 3, FD), op=ALU.mult) \
           .then_inc(net["f_normed"], 1)

    def pool(self, pool, ch):
        net = self.net
        ones = float(np.array([0x3F803F80], np.uint32).view(np.float32)[0])
        net.layer_start(pool, 4)
        pool.memset(self.v, 1.0).then_inc(net["f_filled"], 1)
        pool.wait_ge(net["f_filled"], 1)
        for i in range(2):
            if i:
                pool.wait_ge(net["f_sent"], 16 * self.SPLIT_DMAS)
            pool.memset(self.rows32[64:96, 2 + i, :], 0.0)
            pool.memset(self.rows32[96:128, 2 + i, :], ones)
            pool.memset(self.rows32[64:96, i, :], ones)
            pool.memset(self.rows32[96:128, i, :], 0.0).then_inc(net["f_filled"], 1)
        for g in range(NG):
            net.norm_pool(pool, 4 * NG + g)

    def send_splits(self, sp):
        net = self.net
        for n, (i, part) in enumerate(self.CASTS):
            sp.wait_ge(net["f_cast"], n + 1)
            sp.dma_start(self.scratch[i][part], self.parts[i][part][0:(P, P, 16)[i], :]).then_inc(net["f_sent"], 16)
        sp.wait_ge(net["f_sent"], 16 * self.SPLIT_DMAS)

    def stack(self, sp, r):
        net = self.net
        b, hh = divmod(r, 2)
        if r >= 2:
            sp.wait_ge(net["f_pv"], self.STEPS * (r - 1))
        toks, heads = slice(b * 1024, b * 1024 + 1024), slice(8 * hh, 8 * hh + 8)
        for n, (i, j) in enumerate(self.TERMS):
            for dst, src in ((self.qs, self.scratch[0][i]), (self.ks, self.scratch[1][j])):
                sp.dma_start(dst[r % 2][8 * n:8 * n + 8, :, :],
                             src.rearrange("(h d) t -> d h t", d=FD)[:, heads, toks]).then_inc(net[f"f_stacked{r % 2}"], 16)
        if r < 2:
            sp.wait_ge(net["f_filled"], r + 2)
        sp.dma_start(self.ks[r % 2][64:67, :, :], self.scratch[2][:, heads, toks]).then_inc(net[f"f_stacked{r % 2}"], 16)

    def send_maxima(self, sp, n):
        net = self.net
        r, g = divmod(n, 2)
        sp.wait_ge(net["f_unit_read"], self.turn_unit(n) + 1)
        for s in range(3):
            sp.dma_start(self.qs[r % 2][96 + s:97 + s, :, g * GW:(g + 1) * GW],
                         self.mrows[n % 2][8 * s:8 * s + 8, :]).then_inc(net[f"f_mrows{g}"], 16)


class SiluExperts:
    LAYER = 5
    SHARED = C2 - 2 * E2
    LAG = 2
    NORM_FORTH = 3

    def __init__(self, net):
        self.net = net
        w = net.mid
        w.at = 0
        self.wg, self.wu, self.wd = w.take(C2, P), w.take(C2, P), w.take(C2, P)
        self.wr = w.take(16)
        a = Arena(net.work)
        self.spread = a.take(E2, TOK)
        self.gates = Gates(net, a, w, 5, E2, 2, 1e-20, "g2", (3, 2))
        self.s, self.h, self.hg = a.take(2, GW), a.take(3, GW), a.take(3, GW)

    def spread_wait(self, eng, i):
        eng.wait_ge(self.net[f"g2_spread{i % 2}"], i // 2 + 1)

    def up_pe(self, pe, g, c):
        net, bank = self.net, self.net.bank
        xg = net.xT[1][:, g * GW:(g + 1) * GW]
        i = C2 * g + c
        if i >= 2:
            pe.wait_ge(net["e2_prod"], i - 1)
        pe.matmul(bank[4 + 2 * (i % 2)], self.wg[:, c, :], xg, start=True, stop=True).then_inc(net["e2_gate"], 1)
        pe.matmul(bank[5 + 2 * (i % 2)], self.wu[:, c, :], xg, start=True, stop=True).then_inc(net["e2_up"], 1)

    def pe(self, pe):
        net, bank = self.net, self.net.bank
        net.layer_start(pe, 5)
        pe.wait_ge(net["w5_loaded"], 16 * 4)
        self.gates.pe_logits(pe, net.xT[1], self.wr[:, 0:E2], None)
        self.up_pe(pe, 0, 0)
        self.up_pe(pe, 0, 1)
        self.gates.pe_turn(pe)
        pe.wait_ge(net["g2_gateT"], 2)
        pe.wait_ge(net["g2_sel"], 1)
        for i in range(NG * E2):
            if i >= 4:
                self.spread_wait(pe, i - 4)
            self.gates.pe_spread(pe, bank[i % 4], i // E2, i % E2)
        for i in range(4 * (NG * E2 // 4) - 4, NG * E2):
            self.spread_wait(pe, i)
        for g in range(NG):
            n = 5 * NG + g
            for c in range(C2 + self.LAG):
                if c < C2 and C2 * g + c >= 2:
                    self.up_pe(pe, g, c)
                if g and c == 0:
                    net.norm_pe_back(pe, n - 1)
                d = c - self.LAG
                j = C2 * g + d
                if d >= 0:
                    if d == 0:
                        pe.wait_ge(net["y_ready"], n - 1)
                    if d < self.SHARED:
                        pe.wait_ge(net["e2_prod"], j + 1)
                        src = self.h[:, j % 3, :]
                    else:
                        pe.wait_ge(net["e2_gated"], j + 1 - self.SHARED * (g + 1))
                        src = self.hg[:, j % 3, :]
                    pe.matmul(bank[g % 2], self.wd[:, d, :], src, start=(d == 0), stop=False) \
                      .then_inc(net["e2_down"], 1)
                if g and c == self.NORM_FORTH:
                    net.norm_pe_forth(pe, n - 1)
            pe.matmul(bank[g % 2], net.zeros[0:1, 0:P], net.zeros[0:1, :], start=False, stop=True) \
              .then_inc(net["out_ready"], 1)
        net.norm_pe_back(pe, 6 * NG - 1)
        net.norm_pe_forth(pe, 6 * NG - 1)

    def act(self, act, ch):
        net = self.net
        net.layer_start(act, 5)
        self.gates.act_exp(act)
        self.gates.act_turned(act)
        for i in range(0, NG * E2, 2):
            act.wait_ge(net["g2_wide"], i + 1)
            act.activation(self.spread[:, i % E2, i // E2 * GW:(i // E2 + 1) * GW], net.bank[i % 4], ACT.Copy) \
               .then_inc(net["g2_spread0"], 1)
        for g in range(NG):
            for c in range(C2):
                i = C2 * g + c
                if g and c == self.NORM_FORTH + 1:
                    net.norm_act(act, 5 * NG + g - 1)
                act.wait_ge(net["e2_gate"], i + 1)
                if i >= 2:
                    act.wait_ge(net["e2_prod"], i - 1)
                act.activation(self.s[:, i % 2, :], net.bank[4 + 2 * (i % 2)], ACT.Silu).then_inc(net["e2_silu"], 1)
        net.norm_act(act, 6 * NG - 1)

    def dve(self, dve, ch):
        net = self.net
        net.layer_start(dve, 5)
        self.gates.dve_fill(dve)
        self.gates.dve(dve, ch)
        for i in range(1, NG * E2, 2):
            dve.wait_ge(net["g2_wide"], i + 1)
            dve.tensor_copy(self.spread[:, i % E2, i // E2 * GW:(i // E2 + 1) * GW], net.bank[i % 4]) \
               .then_inc(net["g2_spread1"], 1)
        for g in range(NG):
            if g:
                net.norm_dve_y(dve, 5 * NG + g - 1)
            for c in range(C2):
                i = C2 * g + c
                dve.wait_ge(net["e2_silu"], i + 1)
                dve.wait_ge(net["e2_up"], i + 1)
                if i >= 3:
                    dve.wait_ge(net["e2_down"], i - 2)
                dve.tensor_tensor(out=self.h[:, i % 3, :], in0=self.s[:, i % 2, :], in1=net.bank[5 + 2 * (i % 2)],
                                  op=ALU.mult).then_inc(net["e2_prod"], 1)
                if g and c == 0:
                    net.norm_dve_rest(dve, ch, 5 * NG + g - 1)
        net.norm_dve(dve, ch, 6 * NG - 1)

    def pool(self, pool, ch):
        net = self.net
        net.layer_start(pool, 5)
        self.gates.pool_sel(pool)
        for g in range(NG):
            self.spread_wait(pool, E2 * (g + 1) - 2)
            self.spread_wait(pool, E2 * (g + 1) - 1)
            for c in range(self.SHARED, C2):
                i = C2 * g + c
                pool.wait_ge(net["e2_prod"], i + 1)
                if i >= 3:
                    pool.wait_ge(net["e2_down"], i - 2)
                pool.tensor_tensor(out=self.hg[:, i % 3, :], in0=self.h[:, i % 3, :],
                                   in1=self.spread[:, (c - self.SHARED) // 2, g * GW:(g + 1) * GW],
                                   op=ALU.mult).then_inc(net["e2_gated"], 1)
            net.norm_pool(pool, 5 * NG + g)


class LinearAttention:
    LAYER = 6

    def __init__(self, net):
        self.net = net
        w = net.const
        self.w = w.take(3 * P)
        self.b = w.take(3 * P)
        self.wp = w.take(P)
        self.bp = w.take(1)
        self.blocks = w.take(P)
        a = Arena(net.work)
        self.qkv = a.take(NT, 3 * P)
        self.sq = a.take(2, GT * 2 * P)
        self.norm = a.take(2, 2, GT * 32)
        self.inverse = a.take(GT * 32)
        self.qT = a.take(TOK)
        self.kv = a.take(2, P)
        self.oT = a.take(2, GW)

    def pe(self, pe):
        net, bank = self.net, self.net.bank
        xT = net.xT[0]
        net.layer_start(pe, 6)
        pe.wait_ge(net["w6_loaded"], 16 * 5)
        for g in range(NG + 2):
            if g < NG:
                for k in range(GT):
                    t = g * GT + k
                    if g:
                        pe.wait_ge(net["u_copied"], t - GT + 1)
                    pe.matmul(bank[4 + k][:, 0:3 * P], xT[:, t * P:(t + 1) * P], self.w, start=True, stop=False)
                    pe.matmul(bank[4 + k][:, 0:3 * P], net.ones[0:1, :], self.b[0:1, :], start=False, stop=True) \
                      .then_inc(net["u_qkv"], 1)
            if g >= 2:
                self.turn_pe(pe, g - 2)
        pe.wait_ge(net["u_masked"], 2)
        pe.wait_ge(net["u_qT_copied"], NG)
        self.heads_pe(pe, 0)
        for g in range(NG):
            n = 6 * NG + g
            pe.wait_ge(net["u_oT_copied"], g + 1)
            pe.wait_ge(net["y_ready"], n - 1)
            pe.matmul(bank[g % 2], self.wp, self.oT[:, g % 2, :], start=True, stop=True).then_inc(net["out_ready"], 1)
            if g + 1 < NG:
                self.heads_pe(pe, g + 1)
            if g:
                net.norm_pe_forth(pe, n - 1)
            net.norm_pe_back(pe, n)
        net.norm_pe_forth(pe, 7 * NG - 1)

    def turn_pe(self, pe, g):
        net, bank = self.net, self.net.bank
        b = g // 2
        pe.wait_ge(net["u_unit"], g + 1)
        if g >= 2:
            pe.wait_ge(net["u_qT_copied"], g - 1)
        for k in range(GT):
            mm = pe.transpose(bank[2 + g % 2][:, k * P:(k + 1) * P], self.qkv[:, g * GT + k, 0:P], net.ident)
        mm.then_inc(net["u_qT"], 1)
        for k in range(GT):
            u = g * GT + k
            mm = pe.matmul(bank[1 - b][:, 0:P], self.qkv[:, u, P:2 * P], self.qkv[:, u, 2 * P:3 * P],
                           start=(u % 8 == 0), stop=(u % 8 == 7))
        if g % 2:
            mm.then_inc(net["u_kv"], 1)

    def heads_pe(self, pe, g):
        net = self.net
        if g >= 2:
            pe.wait_ge(net["u_oT_copied"], g - 1)
        pe.matmul(net.bank[4 + g % 2], self.kv[:, g // 2, :], self.qT[:, g * GW:(g + 1) * GW],
                  start=True, stop=True).then_inc(net["u_o"], 1)

    def act(self, act, ch):
        net = self.net
        net.layer_start(act, 6)
        for g in range(NG + 2):
            if g < NG:
                for k in range(GT):
                    t = g * GT + k
                    act.wait_ge(net["u_qkv"], t + 1)
                    act.activation(self.qkv[:, t, :], net.bank[4 + k][:, 0:3 * P], ACT.Copy) \
                       .then_inc(net["u_copied"], 1)
                act.wait_ge(net["u_copied"], GT * (g + 1))
                if g >= 2:
                    act.wait_ge(net["u_sums"], g - 1)
                act.activation(self.sq[:, g % 2, :].rearrange("p (t c) -> p t c", t=GT),
                               self.qkv[:, g * GT:(g + 1) * GT, 0:2 * P], ACT.Square).then_inc(net["u_sq"], 1)
                act.wait_ge(net["u_sums"], g + 1)
                if g >= 2:
                    act.wait_ge(net["u_unit"], g - 1)
                act.activation(self.norm[:, 1, g % 2, :], self.norm[:, 0, g % 2, :], ACT.Sqrt) \
                   .then_inc(net["u_roots"], 1)
            if g >= 2:
                act.wait_ge(net["u_qT"], g - 1)
                act.activation(self.qT[:, (g - 2) * GW:(g - 1) * GW], net.bank[2 + g % 2], ACT.Copy) \
                   .then_inc(net["u_qT_copied"], 1)
        for g in range(NG):
            act.wait_ge(net["u_o"], g + 1)
            if g >= 2:
                act.wait_ge(net["out_ready"], 6 * NG + g - 1)
            act.activation(self.oT[:, g % 2, :], net.bank[4 + g % 2], ACT.Copy).then_inc(net["u_oT_copied"], 1)
            if g:
                net.norm_act(act, 6 * NG + g - 1)
        net.norm_act(act, 7 * NG - 1)

    def sums_dve(self, dve, g):
        dve.wait_ge(self.net["u_sq"], g + 1)
        dve.reduce_sum(self.norm[:, 0, g % 2, :], self.sq[:, g % 2, :].rearrange("p (h d) -> p h d", d=FD),
                       AX.X).then_inc(self.net["u_sums"], 1)

    def dve(self, dve, ch):
        net = self.net
        net.layer_start(dve, 6)
        dve.wait_ge(net["w6_loaded"], 16 * 5)
        self.sums_dve(dve, 0)
        for g in range(NG):
            if g + 1 < NG:
                self.sums_dve(dve, g + 1)
            r = self.norm[:, 1, g % 2, :]
            dve.wait_ge(net["u_roots"], g + 1)
            inv = self.inverse
            ch.link(dve.tensor_scalar(r, r, 1e-18, None, ALU.max))
            ch.link(dve.reciprocal(inv, r))
            ch.link(dve.tensor_tensor(out=inv, in0=inv, in1=self.norm[:, 0, g % 2, :], op=ALU.mult))
            ch.link(dve.tensor_tensor(out=r, in0=r, in1=inv, op=ALU.add))
            ch.link(dve.tensor_scalar(r, r, 0.5, None, ALU.mult))
            ch.link(dve.tensor_scalar(r, r, 1e-12, None, ALU.max))
            ch.link(dve.reciprocal(r, r))
            for k in range(GT):
                qk = self.qkv[:, g * GT + k, 0:2 * P].rearrange("p (h d) -> p h d", d=FD)
                ins = dve.tensor_tensor(out=qk, in0=qk, in1=bc(r[:, k * 32:(k + 1) * 32], 2, FD), op=ALU.mult)
            ins.then_inc(net["u_unit"], 1)
        for b in range(2):
            dve.wait_ge(net["u_kv"], b + 1)
            dve.tensor_tensor(out=self.kv[:, b, :], in0=net.bank[1 - b][:, 0:P], in1=self.blocks,
                              op=ALU.mult).then_inc(net["u_masked"], 1)
        for g in range(NG):
            net.norm_dve(dve, ch, 6 * NG + g, scalar=self.bp[:, 0:1])

    def pool(self, pool, ch):
        net = self.net
        for g in range(NG):
            net.norm_pool(pool, 6 * NG + g)


class TaskVectors:
    LAYER = 7

    def __init__(self, net):
        self.net = net
        w = net.late
        w.at = 0
        self.tw1 = w.take(E3, GW)
        self.w1 = w.take(GW)
        self.w2 = w.take(GW)
        self.gw1 = w.take(P)
        self.gw2 = w.take(8)
        self.gb1, self.gb2 = w.take(1), w.take(8)
        self.b1, self.tb1 = w.take(C3), w.take(C3, E3)
        self.b2, self.tb2 = w.take(1), w.take(E3)
        w = net.mid
        w.at = 0
        self.tw2 = w.take(E3, GW)
        a = Arena(net.work)
        self.h = a.take(2, GW)
        self.hsum = a.take(NG)
        self.hb = a.take(2)
        self.hrep = a.take(2, P)
        self.g = a.take(2, 8)
        self.tmp = a.take(C3, E3)
        self.tmp2 = a.take(E3)
        self.m1, self.m2 = a.take(2, GW), a.take(2, GW)
        self.mb1, self.mb2 = a.take(2, C3), a.take(2)
        self.u = a.take(3, GW)

    def pe(self, pe):
        net, bank = self.net, self.net.bank
        xT = net.xT[1]
        net.layer_start(pe, 7)
        pe.wait_ge(net["w7_loaded"], 16 * 12)
        for g in range(NG):
            pe.matmul(bank[4 + g], self.gw1, xT[:, g * GW:(g + 1) * GW], start=True, stop=True) \
              .then_inc(net["t_gate_h"], 1)
        for b in range(2):
            pe.wait_ge(net["t_mean"], b + 1)
            if b == 0:
                pe.wait_ge(net["y_ready"], 7 * NG)
            pe.matmul(bank[b][:, 0:8], self.hrep[:, b, :], self.gw2, start=True, stop=True) \
              .then_inc(net["t_gate"], 1)
        for g in range(NG):
            n = 7 * NG + g
            b = g // 2
            pe.wait_ge(net["t_merged"], 2 * b + 1)
            for c in range(C3 + 1):
                i = C3 * g + c
                if c < C3:
                    if i >= 2:
                        pe.wait_ge(net["t_act"], i - 1)
                    pe.matmul(bank[4 + i % 2], self.m1[:, b, c * P:(c + 1) * P], xT[:, g * GW:(g + 1) * GW],
                              start=True, stop=True).then_inc(net["t_up"], 1)
                if g and c == 0:
                    net.norm_pe_back(pe, n - 1)
                if c:
                    j = i - 1
                    pe.wait_ge(net["t_act"], j + 1)
                    if c == 1:
                        pe.wait_ge(net["y_ready"], n - 1)
                        pe.wait_ge(net["t_gated"], 2)
                        pe.wait_ge(net["t_merged"], 2 * b + 2)
                    mm = pe.matmul(bank[g % 2], self.m2[:, b, (c - 1) * P:c * P], self.u[:, j % 3, :],
                                   start=(c == 1), stop=False)
                    mm.then_inc(net["t_down"], 1)
            pe.matmul(bank[g % 2], net.zeros[0:1, 0:P], net.zeros[0:1, :], start=False, stop=True) \
              .then_inc(net["out_ready"], 1)
        net.norm_pe_back(pe, 8 * NG - 1)

    def act(self, act, ch):
        net = self.net
        net.layer_start(act, 7)
        act.wait_ge(net["w7_loaded"], 16 * 12)
        for g in range(NG):
            act.wait_ge(net["t_gate_h"], g + 1)
            if g >= 2:
                act.wait_ge(net["t_relu"], g - 1)
            act.activation(self.h[:, g % 2, :], net.bank[4 + g], ACT.Relu, bias=self.gb1[:, 0:1],
                           accum_out=self.hsum[:, g:g + 1]).then_inc(net["t_relu"], 1)
        for g in range(NG):
            b = g // 2
            act.wait_ge(net["t_merged"], 2 * b + 1)
            for c in range(C3):
                i = C3 * g + c
                act.wait_ge(net["t_up"], i + 1)
                if i >= 3:
                    act.wait_ge(net["t_down"], i - 2)
                act.activation(self.u[:, i % 3, :], net.bank[4 + i % 2], ACT.Gelu_apprx_tanh,
                               bias=self.mb1[:, b, c:c + 1]).then_inc(net["t_act"], 1)

    def dve(self, dve, ch):
        net = self.net
        net.layer_start(dve, 7)
        dve.wait_ge(net["w7_loaded"], 16 * 12)
        for b in range(2):
            dve.wait_ge(net["t_relu"], 2 * b + 2)
            ch.link(dve.tensor_tensor(out=self.hb[:, b:b + 1], in0=self.hsum[:, 2 * b:2 * b + 1],
                                      in1=self.hsum[:, 2 * b + 1:2 * b + 2], op=ALU.add))
            ch.link(dve.memset(self.hrep[:, b, :], 1.0 / 1024))
            dve.tensor_scalar(self.hrep[:, b, :], self.hrep[:, b, :], self.hb[:, b:b + 1], None, ALU.mult) \
               .then_inc(net["t_mean"], 1)
        for b in range(2):
            g = self.g[:, b, :]
            dve.wait_ge(net["t_gate"], b + 1)
            dve.tensor_tensor(out=g, in0=net.bank[b][:, 0:8], in1=self.gb2, op=ALU.add) \
               .then_inc(net["t_gated"], 1)
            dve.wait_ge(net["t_gated"], b + 1)
            ch.link(dve.tensor_tensor(out=self.tmp, in0=self.tb1, in1=bc(g, 1, C3), op=ALU.mult))
            ch.link(dve.tensor_tensor(out=self.tmp2, in0=self.tb2, in1=g, op=ALU.mult))
            ch.link(dve.reduce_sum(self.mb1[:, b, :], self.tmp, AX.X))
            ch.link(dve.tensor_tensor(out=self.mb1[:, b, :], in0=self.mb1[:, b, :], in1=self.b1, op=ALU.add))
            ch.link(dve.reduce_sum(self.mb2[:, b:b + 1], self.tmp2, AX.X))
            ch.link(dve.tensor_tensor(out=self.mb2[:, b:b + 1], in0=self.mb2[:, b:b + 1], in1=self.b2, op=ALU.add))
            m1, m2 = self.m1[:, b, :], self.m2[:, b, :]
            for m, tw, w in ((m1, self.tw1, self.w1), (m2, self.tw2, self.w2)):
                for e in range(E3):
                    ins = dve.scalar_tensor_tensor(out=m, in0=tw[:, e, :], scalar=g[:, e:e + 1],
                                                   in1=(m if e else w), op0=ALU.mult, op1=ALU.add)
                    if e + 1 < E3:
                        ch.link(ins)
                ins.then_inc(net["t_merged"], 1)
        for g in range(NG):
            n = 7 * NG + g
            net.norm_dve(dve, ch, n, scalar=self.mb2[:, g // 2:g // 2 + 1])

    def pool(self, pool, ch):
        for g in range(NG):
            self.net.norm_pool(pool, 7 * NG + g)


LAYERS = (QueryAttention, ProductKeys, Lightning, GeluExperts, Forgetting, SiluExperts, LinearAttention, TaskVectors)
CONST_COLS = 5140
LATE_COLS = 9120
MID_COLS = 8900
WORK_COLS = 22850


def build(nc, io, out):
    with ExitStack() as ctx:
        net = Net(nc, ctx, io)
        layers = [make(net) for make in LAYERS]
        query, keys, light, gelu, forget, silu, linear, tasks = layers
        block = ctx.enter_context(nc.Block())

        def load(eng, name, dst, src):
            eng.dma_start(dst, io[src]).then_inc(net[name], 16)

        @block.sync
        def _(sp):
            loads0 = [(net.xT[0][:], "xT"), (query.w, "a0_w"), (query.b, "a0_b"), (query.bv, "a0_bv"),
                      (query.mask, "a0_mask"), (net.ident, "ident"), (net.ones, "ones"),
                      (net.minus_half, "minus_half"), (net.half, "half"), (net.pick[0:48, :], "pick")]
            loads1 = [(keys.wq, "p_wq"), (keys.wqT, "p_wqT"), (keys.keysT, "p_keysT"), (keys.down, "p_down"),
                      (keys.up, "p_up"), (keys.gamma, "p_gamma"), (keys.beta, "p_beta"), (keys.iota32, "p_iota"),
                      (keys.coef_y, "p_coef"), (keys.invn, "p_invn"),
                      (keys.spread32, "p_spread")]
            loads4 = [(forget.wq, "f_wq"), (forget.wk, "f_wk"), (forget.wv, "f_wv"), (forget.wo, "f_wo"),
                      (forget.wf, "f_wf"), (forget.mask_n32, "f_mask_n")]
            loads6 = [(linear.w, "u_w"), (linear.b[0:1, :], "u_b"), (linear.wp, "u_wp"), (linear.bp, "u_bp"),
                      (linear.blocks, "u_blocks")]
            loads2 = [(light.wq, "l_wq"), (light.wqr, "l_wqr"), (light.wk, "l_wk"), (light.wkr, "l_wkr"),
                      (light.wv, "l_wv"), (light.wo, "l_wo"), (light.cos, "l_cos"), (light.sin, "l_sin"),
                      (light.kdec, "l_kdec"), (light.blk, "l_blk")]
            loads3 = [(gelu.w1, "e1_w1"), (gelu.w2, "e1_w2"), (gelu.b1, "e1_b1"),
                      (gelu.gw[:, 0:E1], "e1_gw"), (gelu.gb[0:1, 0:E1], "e1_gb"), (gelu.b2[0:48, :], "e1_b2")]
            loads5 = [(silu.wg, "e2_wg"), (silu.wu, "e2_wu"), (silu.wd, "e2_wd"), (silu.wr[:, 0:E2], "e2_wr")]
            loads7 = [(tasks.tw1, "t_tw1"), (tasks.w1, "t_w1"), (tasks.w2, "t_w2"), (tasks.gw1, "t_gw1"),
                      (tasks.gw2, "t_gw2"), (tasks.gb1, "t_gb1"), (tasks.gb2, "t_gb2"), (tasks.b1, "t_b1"),
                      (tasks.tb1, "t_tb1"), (tasks.b2, "t_b2"), (tasks.tb2, "t_tb2")]
            for n, loads in ((0, loads0), (1, loads1), (4, loads4), (6, loads6)):
                for dst, src in loads:
                    load(sp, f"w{n}_loaded", dst, src)
            sp.wait_ge(net["p_m"], 1)
            for dst, src in loads2:
                load(sp, "w2_loaded", dst, src)
            sp.wait_ge(net["out_ready"], 2 * NG)
            load(sp, "w3_loaded", light.decay, "l_decay")
            load(sp, "w3_loaded", light.qdec, "l_qdec")
            sp.wait_ge(net["w3_loaded"], 16 * 2)
            for dst, src in loads3:
                load(sp, "w3_loaded", dst, src)
            sp.wait_ge(net["out_ready"], 3 * NG)
            for dst, src in loads7:
                load(sp, "w7_loaded", dst, src)
            forget.send_splits(sp)
            forget.stack(sp, 0)
            forget.stack(sp, 1)
            for dst, src in loads5:
                load(sp, "w5_loaded", dst, src)
            for n in range(2 * forget.ROUNDS):
                forget.send_maxima(sp, n)
                if n in (2, 4):
                    forget.stack(sp, n // 2 + 1)
            sp.wait_ge(net["out_ready"], 6 * NG)
            load(sp, "w7_loaded", tasks.tw2, "t_tw2")
            for g in range(NG):
                sp.wait_ge(net["normed"], 7 * NG + g + 1)
                sp.dma_start(out[:, g * GT:(g + 1) * GT, :], net.x[:, g * GT:(g + 1) * GT, :]) \
                  .then_inc(net["stored"], 16)
            sp.wait_ge(net["stored"], 16 * NG)

        @block.tensor
        def _(pe):
            for layer in layers:
                layer.pe(pe)

        @block.scalar
        def _(act):
            ch = Chain(act, net["act_chain"])
            for layer in layers:
                layer.act(act, ch)

        @block.vector
        def _(dve):
            ch = Chain(dve, net["dve_chain"])
            for layer in layers:
                layer.dve(dve, ch)

        @block.gpsimd
        def _(pool):
            ch = Chain(pool, net["pool_chain"])
            for layer in layers:
                layer.pool(pool, ch)


def constants():
    f = np.float32
    i = np.arange(P)
    above = np.where(i[None, :] < i[:, None], f(NEG), f(0))
    slopes = np.array([2.0 ** (-8.0 / 16 * (h + 1)) for h in range(16)], f)
    t = np.arange(P, dtype=f)
    inv = 1.0 / 10000.0 ** (np.arange(0, HD, 2, dtype=np.float64) / HD)
    angle = np.concatenate([np.outer(np.arange(1024, dtype=np.float64), inv)] * 2, axis=-1).T
    sign = np.where(np.arange(HD) < HD // 2, -1.0, 1.0)[:, None]
    diff = t[None, :] - t[:, None]
    decay = np.where(diff[:, None, :] >= 0, np.exp(-slopes[None, :, None] * np.maximum(diff, 0)[:, None, :]), f(0))
    head = np.array([[4 * (2 * (c // 4) + half) + c % 4 for c in range(8)] for half in range(2)])
    rows = np.repeat(head, HD, axis=0)
    e = np.arange(1024)
    spread = np.zeros((P, 2048), f)
    for q in range(2):
        spread[64 * q + e // 32, 1024 * q + e] = 1
        spread[64 * q + 32 + e % 32, 1024 * q + e] = 1
    return {
        "minus_half": np.full((P, 16), -0.5, f), "half": np.full((P, 32), 0.5, f),
        "ident": np.eye(P, dtype=f), "ones": np.ones((P, P), f), "a0_mask": above.astype(f),
        "f_mask_n": np.ascontiguousarray(above.T).astype(f),
        "p_iota": np.broadcast_to(np.repeat(np.arange(PKEYS, dtype=f), PTOP), (P, PKEYS * PTOP)),
        "p_spread": spread,
        "p_coef": np.broadcast_to(8 - np.arange(8, dtype=f), (P, 8, 8)),
        "p_invn": np.full((P, P), 1.0 / TOK, f),
        "l_cos": np.tile(np.cos(angle), (2, 1)).astype(f), "l_sin": np.tile(np.sin(angle) * sign, (2, 1)).astype(f),
        "l_decay": decay.astype(f),
        "l_qdec": np.exp(-slopes[rows][:, :, None] * (t + 1)[None, None, :]).astype(f),
        "l_kdec": np.exp(-slopes[None, :] * (P - 1 - t)[:, None]).astype(f),
        "l_blk": np.exp(-slopes[rows] * f(P)).astype(f),
        "pick": np.tile(np.eye(16, dtype=f), (3, 1)),
        "u_blocks": np.kron(np.eye(16), np.ones((8, 8))).astype(f),
    }


def kernel(**inputs):
    import concourse.bacc as bacc
    from concourse.bass_utils import run_bass_kernel_spmd as run

    w = {k: np.asarray(v) for k, v in inputs.items()}

    def tiles(a, n):
        return a.reshape(n, P, -1).transpose(1, 0, 2)

    a0, pk, l1, e1 = "L0_attn_", "L0_ffn_", "L1_attn_", "L1_ffn_"
    f2, e2, u3, t3 = "L2_attn_", "L2_ffn_", "L3_attn_", "L3_ffn_"
    arr = dict(constants())
    arr["xT"] = w[a0 + "minibatch"].reshape(TOK, P).T
    arr["a0_w"] = np.stack([w[a0 + "Wq"], w[a0 + "Wk"], w[a0 + "Wv"]], axis=1)
    arr["a0_b"] = np.stack([w[a0 + "bq"], w[a0 + "bk"]], axis=1)
    arr["a0_bv"] = np.broadcast_to(w[a0 + "bv"], (P, P))

    wq = w[pk + "w_q"]
    arr["p_wq"] = wq
    arr["p_wqT"] = wq.reshape(P, PC, P).transpose(2, 1, 0)
    arr["p_keysT"] = w[pk + "keys"].transpose(3, 2, 0, 1).reshape(P, PC, PKEYS)
    arr["p_down"] = w[pk + "down_embed"].T
    arr["p_up"] = tiles(w[pk + "up_embed"], 8)
    arr["p_gamma"] = w[pk + "bn_gamma"].reshape(PC, P).T
    arr["p_beta"] = w[pk + "bn_beta"].reshape(PC, P).T

    swap = np.concatenate([np.arange(32, 64), np.arange(0, 32)])
    lq = w[l1 + "Wq"].reshape(2, 2, 4, HD, P)
    lk = w[l1 + "Wk"].reshape(2, 2, HD, P)

    def qside(a):
        return a.transpose(4, 0, 2, 1, 3).reshape(P, 8, P)

    def kside(a):
        return a.transpose(3, 0, 1, 2).reshape(P, 2, P)

    arr["l_wq"], arr["l_wqr"] = qside(lq), qside(lq[:, :, :, swap])
    arr["l_wk"], arr["l_wkr"] = kside(lk), kside(lk[:, :, swap])
    arr["l_wv"] = w[l1 + "Wv"].T
    arr["l_wo"] = w[l1 + "Wo"].reshape(P, 2, 2, 4, HD).transpose(2, 4, 1, 3, 0).reshape(P, 8, P)

    rw1 = w[e1 + "rW1"].transpose(1, 0, 2).reshape(P, E1 * 2 * P)
    arr["e1_w1"] = np.concatenate([w[e1 + "sW1"][0], rw1], axis=1)
    arr["e1_w2"] = tiles(np.concatenate([w[e1 + "sW2"][0], w[e1 + "rW2"].reshape(-1, P)], axis=0), C1)
    arr["e1_b1"] = np.concatenate([w[e1 + "sb1"].reshape(-1), w[e1 + "rb1"].reshape(-1)]).reshape(C1, P).T
    arr["e1_b2"] = np.concatenate([w[e1 + "rb2"], w[e1 + "sb2"]] * 3, axis=0)
    arr["e1_gw"], arr["e1_gb"] = w[e1 + "gW"], w[e1 + "gb"].reshape(1, E1)

    arr["f_wq"], arr["f_wk"] = w[f2 + "Wq"], w[f2 + "Wk"]
    arr["f_wv"], arr["f_wo"], arr["f_wf"] = w[f2 + "Wv"], w[f2 + "Wo"], w[f2 + "Wf"]

    def experts(routed, shared):
        return np.concatenate([shared, routed.transpose(1, 0, 2).reshape(P, -1)], axis=1)

    arr["e2_wg"] = experts(w[e2 + "Wg"], w[e2 + "Sg"])
    arr["e2_wu"] = experts(w[e2 + "Wu"], w[e2 + "Su"])
    arr["e2_wd"] = tiles(np.concatenate([w[e2 + "Sd"], w[e2 + "Wd"].reshape(-1, P)], axis=0), C2)
    arr["e2_wr"] = w[e2 + "Wr"]

    arr["u_w"], arr["u_b"] = w[u3 + "qkv_w"], w[u3 + "qkv_b"].reshape(1, 3 * P)
    arr["u_wp"], arr["u_bp"] = w[u3 + "proj_w"], w[u3 + "proj_b"].reshape(P, 1)

    arr["t_tw1"] = w[t3 + "TW1"].transpose(2, 0, 1)
    arr["t_w1"] = w[t3 + "W1"].T
    arr["t_w2"] = w[t3 + "W2"].T.reshape(C3, P, P).transpose(1, 0, 2)
    arr["t_tw2"] = w[t3 + "TW2"].transpose(2, 0, 1).reshape(C3, P, E3, P).transpose(1, 2, 0, 3)
    arr["t_gw1"], arr["t_gw2"] = w[t3 + "gate_w1"].T, w[t3 + "gate_w2"].T
    arr["t_gb1"] = w[t3 + "gate_b1"].reshape(P, 1)
    arr["t_gb2"] = np.broadcast_to(w[t3 + "gate_b2"], (P, E3))
    arr["t_b1"] = w[t3 + "b1"].reshape(C3, P).T
    arr["t_tb1"] = w[t3 + "Tb1"].reshape(E3, C3, P).transpose(2, 1, 0)
    arr["t_b2"] = w[t3 + "b2"].reshape(P, 1)
    arr["t_tb2"] = w[t3 + "Tb2"].T

    shaped = {
        "e1_w1": (P, C1, P), "e2_wg": (P, C2, P), "e2_wu": (P, C2, P), "t_w2": (P, GW), "t_tw2": (P, E3, GW)}
    nc = bacc.Bacc("TRN2", target_bir_lowering=False, num_devices=1)
    arrays, io = {}, {}
    for name, a in arr.items():
        a = np.ascontiguousarray(a.reshape(shaped.get(name, a.shape)))
        arrays[f"in_{name}"] = a
        io[name] = nc.dram_tensor(f"in_{name}", a.shape, mybir.dt.from_np(a.dtype), kind="ExternalInput").ap()
    out = nc.dram_tensor("out_x", (P, NT, P), F32, kind="ExternalOutput").ap()
    build(nc, io, out)
    r = run(nc, [arrays], core_ids=[0])
    return r.results[0]["out_x"].transpose(1, 0, 2).reshape(2, 1024, P)
```
